# Optimizing a Trainium2 kernel written in Bass

```python
import numpy as np
import jax
import jax.numpy as jnp

def _softmax(x, axis=-1):
    return jax.nn.softmax(x, axis=axis)

def _gelu(x):
    return jax.nn.gelu(x, approximate=True)

def _silu(x):
    return jax.nn.silu(x)

def _sigmoid(x):
    return jax.nn.sigmoid(x)

def _layernorm(x, axis=-1, eps=1e-05):
    m = jnp.mean(x, axis=axis, keepdims=True)
    v = jnp.var(x, axis=axis, keepdims=True)
    return (x - m) / jnp.sqrt(v + eps)

def _scatter_add(tgt, idx, src, axis=0):
    return tgt.at[idx].add(src)

def _segment_sum(src, seg, n):
    return jax.ops.segment_sum(src, seg, n)
kernel_name = 'mk_hybrid_d2_jaxref_r8_bab156'

def setup_inputs(seed: int=0):
    np.random.seed(seed)
    _w = jnp.asarray

    def _L0_attn_a_setup():
        import jax, jax.numpy as jnp
        import numpy as np
        D_IN = 256
        D_OUT = 256
        N_HEAD = 16
        N_KV = 4
        HEAD_DIM = D_OUT // N_HEAD
        KV_DIM = 64
        LATENT = 128
        SEQ = 256
        BATCH = 2
        GROUP = N_HEAD // N_KV
        key = jax.random.key(seed)
        ks = jax.random.split(key, 12)

        def lin(k, fan_in, shape):
            return jax.random.normal(k, shape, dtype=jnp.float32) / np.sqrt(fan_in)
        return {'x': jax.random.normal(ks[0], (BATCH, SEQ, D_IN), dtype=jnp.float32), 'Wq': lin(ks[1], D_IN, (D_IN, D_OUT)), 'bq': jnp.zeros((D_OUT,), jnp.float32), 'Wl': lin(ks[2], D_IN, (D_IN, LATENT)), 'bl': jnp.zeros((LATENT,), jnp.float32), 'Wk': lin(ks[3], LATENT, (LATENT, N_KV * KV_DIM)), 'bk': jnp.zeros((N_KV * KV_DIM,), jnp.float32), 'Wv': lin(ks[4], LATENT, (LATENT, N_KV * KV_DIM)), 'bv': jnp.zeros((N_KV * KV_DIM,), jnp.float32), 'Wq2kv': lin(ks[5], HEAD_DIM, (HEAD_DIM, KV_DIM)), 'Wkv2h': lin(ks[6], KV_DIM, (KV_DIM, HEAD_DIM)), 'bkv2h': jnp.zeros((HEAD_DIM,), jnp.float32), 'Wo': lin(ks[7], D_OUT, (D_OUT, D_OUT)), 'bo': jnp.zeros((D_OUT,), jnp.float32)}
    _L0_attn_a_in = _L0_attn_a_setup()

    def _L0_attn_b_setup():
        import jax, jax.numpy as jnp
        import numpy as np
        B, S, HIDDEN, H = (4, 512, 256, 16)
        HD = HIDDEN // H

        def apply_rope(x, inv_freq):
            seq_len = x.shape[1]
            t = jnp.arange(seq_len, dtype=jnp.float32)[:, None]
            angle = t * inv_freq[None, :]
            sin = jnp.sin(angle)[None, :, None, :]
            cos = jnp.cos(angle)[None, :, None, :]
            x1, x2 = (x[..., ::2], x[..., 1::2])
            return jnp.concatenate([x1 * cos - x2 * sin, x1 * sin + x2 * cos], axis=-1)
        key = jax.random.key(seed)
        ks = jax.random.split(key, 5)
        x = jax.random.normal(ks[0], (B, S, HIDDEN), dtype=jnp.float32)
        scale = 1.0 / np.sqrt(HIDDEN)
        wq = jax.random.normal(ks[1], (HIDDEN, HIDDEN), dtype=jnp.float32) * scale
        wk = jax.random.normal(ks[2], (HIDDEN, HIDDEN), dtype=jnp.float32) * scale
        wv = jax.random.normal(ks[3], (HIDDEN, HIDDEN), dtype=jnp.float32) * scale
        wo = jax.random.normal(ks[4], (HIDDEN, HIDDEN), dtype=jnp.float32) * scale
        inv_freq = (1.0 / 10000.0 ** (np.arange(0, HD, 2, dtype=np.float32) / HD)).astype(np.float32)
        inv_freq = jnp.asarray(inv_freq)
        return {'x': x, 'wq': wq, 'wk': wk, 'wv': wv, 'wo': wo, 'inv_freq': inv_freq}
    _L0_attn_b_in = _L0_attn_b_setup()

    def _L0_ffn_setup():
        import jax, jax.numpy as jnp
        import numpy as np
        B, S, H, F, E, R, K = (2, 128, 256, 896, 8, 32, 2)

        def _gather_slot(a_all, e):
            return jnp.take_along_axis(a_all, e[:, None, None], axis=1)[:, 0]
        key = jax.random.key(seed)
        ks = jax.random.split(key, 12)
        sc = 0.02
        n = lambda k, shape, s: jax.random.normal(k, shape, dtype=jnp.float32) * s
        return {'hidden_states': n(ks[0], (B, S, H), 1.0), 'Wg': n(ks[1], (E, H), sc), 'W1': n(ks[2], (F, H), sc), 'W2': n(ks[3], (H, F), sc), 'W3': n(ks[4], (F, H), sc), 'A1': n(ks[5], (E, R, H), sc), 'B1': n(ks[6], (E, F, R), sc), 'A2': n(ks[7], (E, R, F), sc), 'B2': n(ks[8], (E, H, R), sc), 'A3': n(ks[9], (E, R, H), sc), 'B3': n(ks[10], (E, F, R), sc)}
    _L0_ffn_in = _L0_ffn_setup()

    def _L1_attn_a_setup():
        import jax, jax.numpy as jnp
        import numpy as np
        H, DK, DV = (6, 32, 64)
        HID = 256
        CONV = 4
        NORM_EPS = 1e-05

        def causal_dwconv_silu(x, w):
            K = w.shape[1]
            xp = jnp.pad(x, ((0, 0), (K - 1, 0), (0, 0)))
            y = jax.lax.conv_general_dilated(jnp.transpose(xp, (0, 2, 1)), w[:, None, :], (1,), 'VALID', feature_group_count=w.shape[0])
            return jax.nn.silu(jnp.transpose(y, (0, 2, 1)))

        def l2norm(x, eps=1e-06):
            return x * jax.lax.rsqrt(jnp.sum(x * x, axis=-1, keepdims=True) + eps)
        key = jax.random.key(seed)
        ks = jax.random.split(key, 16)
        B, T = (2, 512)
        s = HID ** (-0.5)
        return dict(hidden_states=jax.random.normal(ks[0], (B, T, HID), jnp.float32), Wq=jax.random.normal(ks[1], (H * DK, HID), jnp.float32) * s, Wk=jax.random.normal(ks[2], (H * DK, HID), jnp.float32) * s, Wv=jax.random.normal(ks[3], (H * DV, HID), jnp.float32) * s, Wb=jax.random.normal(ks[4], (H, HID), jnp.float32) * s, Wa=jax.random.normal(ks[5], (H, HID), jnp.float32) * s, A_log=jnp.log(jax.random.uniform(ks[6], (H,), jnp.float32, 0.5, 16.0)), dt_bias=jax.random.normal(ks[7], (H,), jnp.float32) * 0.1, conv_wq=jax.random.normal(ks[8], (H * DK, CONV), jnp.float32) * 0.5, conv_wk=jax.random.normal(ks[9], (H * DK, CONV), jnp.float32) * 0.5, conv_wv=jax.random.normal(ks[10], (H * DV, CONV), jnp.float32) * 0.5, Wg=jax.random.normal(ks[11], (H * DV, HID), jnp.float32) * s, norm_w=jnp.ones((DV,), jnp.float32), Wo=jax.random.normal(ks[12], (HID, H * DV), jnp.float32) * (H * DV) ** (-0.5))
    _L1_attn_a_in = _L1_attn_a_setup()

    def _L1_attn_b_setup():
        import jax, jax.numpy as jnp
        import numpy as np
        D_MODEL = 256
        HEADS = 16
        HEAD_DIM = D_MODEL // HEADS
        key = jax.random.key(seed)
        k1, k2, k3 = jax.random.split(key, 3)
        B, S = (1, 256)
        x = jax.random.normal(k1, (B, S, D_MODEL), dtype=jnp.float32)
        Wqkv_w = jax.random.normal(k2, (D_MODEL + 2 * HEAD_DIM, D_MODEL), dtype=jnp.float32) * D_MODEL ** (-0.5)
        Wqkv_b = jnp.zeros((D_MODEL + 2 * HEAD_DIM,), dtype=jnp.float32)
        out_w = jax.random.normal(k3, (D_MODEL, D_MODEL), dtype=jnp.float32) * D_MODEL ** (-0.5)
        out_b = jnp.zeros((D_MODEL,), dtype=jnp.float32)
        return {'x': x, 'Wqkv_w': Wqkv_w, 'Wqkv_b': Wqkv_b, 'out_w': out_w, 'out_b': out_b}
    _L1_attn_b_in = _L1_attn_b_setup()

    def _L1_ffn_setup():
        import jax, jax.numpy as jnp
        import numpy as np
        L, N, E, H, K = (256, 8, 256, 1024, 8)
        key = jax.random.key(seed)
        ks = jax.random.split(key, 6)
        return {'x': jax.random.normal(ks[0], (L, N, E), dtype=jnp.float32), 'proj1': jax.random.normal(ks[1], (H, E), dtype=jnp.float32) * 0.02, 'proj1_bias': jax.random.normal(ks[2], (H,), dtype=jnp.float32) * 0.02, 'proj2': jax.random.normal(ks[3], (E, H), dtype=jnp.float32) * 0.02, 'proj2_bias': jax.random.normal(ks[4], (E,), dtype=jnp.float32) * 0.02, 'gate_w': jax.random.normal(ks[5], (E, K), dtype=jnp.float32)}
    _L1_ffn_in = _L1_ffn_setup()
    _d = {'L0_attn_a_x': _L0_attn_a_in['x'], 'L0_attn_a_Wq': _L0_attn_a_in['Wq'], 'L0_attn_a_bq': _L0_attn_a_in['bq'], 'L0_attn_a_Wl': _L0_attn_a_in['Wl'], 'L0_attn_a_bl': _L0_attn_a_in['bl'], 'L0_attn_a_Wk': _L0_attn_a_in['Wk'], 'L0_attn_a_bk': _L0_attn_a_in['bk'], 'L0_attn_a_Wv': _L0_attn_a_in['Wv'], 'L0_attn_a_bv': _L0_attn_a_in['bv'], 'L0_attn_a_Wq2kv': _L0_attn_a_in['Wq2kv'], 'L0_attn_a_Wkv2h': _L0_attn_a_in['Wkv2h'], 'L0_attn_a_bkv2h': _L0_attn_a_in['bkv2h'], 'L0_attn_a_Wo': _L0_attn_a_in['Wo'], 'L0_attn_a_bo': _L0_attn_a_in['bo'], 'L0_attn_b_wq': _L0_attn_b_in['wq'], 'L0_attn_b_wk': _L0_attn_b_in['wk'], 'L0_attn_b_wv': _L0_attn_b_in['wv'], 'L0_attn_b_wo': _L0_attn_b_in['wo'], 'L0_attn_b_inv_freq': _L0_attn_b_in['inv_freq'], 'L0_ffn_Wg': _L0_ffn_in['Wg'], 'L0_ffn_W1': _L0_ffn_in['W1'], 'L0_ffn_W2': _L0_ffn_in['W2'], 'L0_ffn_W3': _L0_ffn_in['W3'], 'L0_ffn_A1': _L0_ffn_in['A1'], 'L0_ffn_B1': _L0_ffn_in['B1'], 'L0_ffn_A2': _L0_ffn_in['A2'], 'L0_ffn_B2': _L0_ffn_in['B2'], 'L0_ffn_A3': _L0_ffn_in['A3'], 'L0_ffn_B3': _L0_ffn_in['B3'], 'L1_attn_a_Wq': _L1_attn_a_in['Wq'], 'L1_attn_a_Wk': _L1_attn_a_in['Wk'], 'L1_attn_a_Wv': _L1_attn_a_in['Wv'], 'L1_attn_a_Wb': _L1_attn_a_in['Wb'], 'L1_attn_a_Wa': _L1_attn_a_in['Wa'], 'L1_attn_a_A_log': _L1_attn_a_in['A_log'], 'L1_attn_a_dt_bias': _L1_attn_a_in['dt_bias'], 'L1_attn_a_conv_wq': _L1_attn_a_in['conv_wq'], 'L1_attn_a_conv_wk': _L1_attn_a_in['conv_wk'], 'L1_attn_a_conv_wv': _L1_attn_a_in['conv_wv'], 'L1_attn_a_Wg': _L1_attn_a_in['Wg'], 'L1_attn_a_norm_w': _L1_attn_a_in['norm_w'], 'L1_attn_a_Wo': _L1_attn_a_in['Wo'], 'L1_attn_b_Wqkv_w': _L1_attn_b_in['Wqkv_w'], 'L1_attn_b_Wqkv_b': _L1_attn_b_in['Wqkv_b'], 'L1_attn_b_out_w': _L1_attn_b_in['out_w'], 'L1_attn_b_out_b': _L1_attn_b_in['out_b'], 'L1_ffn_proj1': _L1_ffn_in['proj1'], 'L1_ffn_proj1_bias': _L1_ffn_in['proj1_bias'], 'L1_ffn_proj2': _L1_ffn_in['proj2'], 'L1_ffn_proj2_bias': _L1_ffn_in['proj2_bias'], 'L1_ffn_gate_w': _L1_ffn_in['gate_w']}
    _x0 = _d['L0_attn_a_x']
    _d['L0_attn_a_x'] = jax.random.normal(jax.random.fold_in(jax.random.key(seed), 1), (4, 256, 256), dtype=_x0.dtype)
    del _x0
    return _d

def reference(L0_attn_a_x, L0_attn_a_Wq, L0_attn_a_bq, L0_attn_a_Wl, L0_attn_a_bl, L0_attn_a_Wk, L0_attn_a_bk, L0_attn_a_Wv, L0_attn_a_bv, L0_attn_a_Wq2kv, L0_attn_a_Wkv2h, L0_attn_a_bkv2h, L0_attn_a_Wo, L0_attn_a_bo, L0_attn_b_wq, L0_attn_b_wk, L0_attn_b_wv, L0_attn_b_wo, L0_attn_b_inv_freq, L0_ffn_Wg, L0_ffn_W1, L0_ffn_W2, L0_ffn_W3, L0_ffn_A1, L0_ffn_B1, L0_ffn_A2, L0_ffn_B2, L0_ffn_A3, L0_ffn_B3, L1_attn_a_Wq, L1_attn_a_Wk, L1_attn_a_Wv, L1_attn_a_Wb, L1_attn_a_Wa, L1_attn_a_A_log, L1_attn_a_dt_bias, L1_attn_a_conv_wq, L1_attn_a_conv_wk, L1_attn_a_conv_wv, L1_attn_a_Wg, L1_attn_a_norm_w, L1_attn_a_Wo, L1_attn_b_Wqkv_w, L1_attn_b_Wqkv_b, L1_attn_b_out_w, L1_attn_b_out_b, L1_ffn_proj1, L1_ffn_proj1_bias, L1_ffn_proj2, L1_ffn_proj2_bias, L1_ffn_gate_w):

    def _L0_attn_a_ref(x, Wq, bq, Wl, bl, Wk, bk, Wv, bv, Wq2kv, Wkv2h, bkv2h, Wo, bo):
        import jax, jax.numpy as jnp
        import numpy as np
        D_IN = 256
        D_OUT = 256
        N_HEAD = 16
        N_KV = 4
        HEAD_DIM = D_OUT // N_HEAD
        KV_DIM = 64
        LATENT = 128
        SEQ = 256
        BATCH = 2
        GROUP = N_HEAD // N_KV
        b, t, _ = x.shape
        q = (x @ Wq + bq).reshape(b, t, N_HEAD, HEAD_DIM).transpose(0, 2, 1, 3)
        q = jnp.einsum('bhtd,de->bhte', q, Wq2kv)
        lat = jax.nn.silu(x @ Wl + bl)
        k = (lat @ Wk + bk).reshape(b, t, N_KV, KV_DIM).transpose(0, 2, 1, 3)
        v = (lat @ Wv + bv).reshape(b, t, N_KV, KV_DIM).transpose(0, 2, 1, 3)
        k = jnp.repeat(k, GROUP, axis=1)
        v = jnp.repeat(v, GROUP, axis=1)
        scores = jnp.einsum('bhqd,bhkd->bhqk', q, k) / np.sqrt(KV_DIM)
        causal = jnp.tril(jnp.ones((t, t), dtype=bool))
        scores = jnp.where(causal, scores, -jnp.inf)
        attn = jax.nn.softmax(scores, axis=-1)
        ctx = jnp.einsum('bhqk,bhkd->bhqd', attn, v)
        ctx = jnp.einsum('bhtd,de->bhte', ctx, Wkv2h) + bkv2h
        ctx = ctx.transpose(0, 2, 1, 3).reshape(b, t, D_OUT)
        return ctx @ Wo + bo

    def _L0_attn_b_ref(x, wq, wk, wv, wo, inv_freq):
        import jax, jax.numpy as jnp
        import numpy as np
        B, S, HIDDEN, H = (4, 512, 256, 16)
        HD = HIDDEN // H

        def apply_rope(x, inv_freq):
            seq_len = x.shape[1]
            t = jnp.arange(seq_len, dtype=jnp.float32)[:, None]
            angle = t * inv_freq[None, :]
            sin = jnp.sin(angle)[None, :, None, :]
            cos = jnp.cos(angle)[None, :, None, :]
            x1, x2 = (x[..., ::2], x[..., 1::2])
            return jnp.concatenate([x1 * cos - x2 * sin, x1 * sin + x2 * cos], axis=-1)
        b, s, _ = x.shape
        q = (x @ wq.T).reshape(b, s, H, HD)
        k = (x @ wk.T).reshape(b, s, H, HD)
        v = (x @ wv.T).reshape(b, s, H, HD)
        q = apply_rope(q, inv_freq)
        k = apply_rope(k, inv_freq)
        scores = jnp.einsum('bshd,bstd->bsht', q, k) / jnp.sqrt(jnp.float32(HD))
        weights = jax.nn.softmax(scores, axis=-1)
        attn = jnp.einsum('bsht,bstd->bshd', weights, v)
        attn = attn.reshape(b, s, HIDDEN)
        return attn @ wo.T

    def _L0_ffn_ref(hidden_states, Wg, W1, W2, W3, A1, B1, A2, B2, A3, B3):
        import jax, jax.numpy as jnp
        import numpy as np
        B, S, H, F, E, R, K = (2, 128, 256, 896, 8, 32, 2)

        def _gather_slot(a_all, e):
            return jnp.take_along_axis(a_all, e[:, None, None], axis=1)[:, 0]
        b, s, h = hidden_states.shape
        x = hidden_states.reshape(-1, h)
        nE = Wg.shape[0]
        logits = x @ Wg.T
        probs = jax.nn.softmax(logits.astype(jnp.float32), axis=-1)
        rw, sel = jax.lax.top_k(probs, K)
        rw = (rw / rw.sum(axis=-1, keepdims=True)).astype(x.dtype)
        base1 = x @ W1.T
        base3 = x @ W3.T
        a1_all = jnp.einsum('th,erh->ter', x, A1)
        a3_all = jnp.einsum('th,erh->ter', x, A3)
        out = jnp.zeros_like(x)
        for k in range(K):
            e = sel[:, k]
            mask = jax.nn.one_hot(e, nE, dtype=x.dtype)
            a1 = _gather_slot(a1_all, e)
            a3 = _gather_slot(a3_all, e)
            lora1 = jnp.einsum('ter,efr->tf', mask[:, :, None] * a1[:, None, :], B1)
            lora3 = jnp.einsum('ter,efr->tf', mask[:, :, None] * a3[:, None, :], B3)
            x1 = base1 + lora1
            x3 = base3 + lora3
            x2 = jax.nn.silu(x1) * x3
            down = x2 @ W2.T
            a2_all = jnp.einsum('tf,erf->ter', x2, A2)
            a2 = _gather_slot(a2_all, e)
            lora2 = jnp.einsum('ter,ehr->th', mask[:, :, None] * a2[:, None, :], B2)
            out = out + (down + lora2) * rw[:, k:k + 1]
        return out.reshape(b, s, h)

    def _L1_attn_a_ref(hidden_states, Wq, Wk, Wv, Wb, Wa, A_log, dt_bias, conv_wq, conv_wk, conv_wv, Wg, norm_w, Wo):
        import jax, jax.numpy as jnp
        import numpy as np
        H, DK, DV = (6, 32, 64)
        HID = 256
        CONV = 4
        NORM_EPS = 1e-05

        def causal_dwconv_silu(x, w):
            K = w.shape[1]
            xp = jnp.pad(x, ((0, 0), (K - 1, 0), (0, 0)))
            y = jax.lax.conv_general_dilated(jnp.transpose(xp, (0, 2, 1)), w[:, None, :], (1,), 'VALID', feature_group_count=w.shape[0])
            return jax.nn.silu(jnp.transpose(y, (0, 2, 1)))

        def l2norm(x, eps=1e-06):
            return x * jax.lax.rsqrt(jnp.sum(x * x, axis=-1, keepdims=True) + eps)
        x = hidden_states
        B, T, _ = x.shape
        q = causal_dwconv_silu(x @ Wq.T, conv_wq).reshape(B, T, H, DK)
        k = causal_dwconv_silu(x @ Wk.T, conv_wk).reshape(B, T, H, DK)
        v = causal_dwconv_silu(x @ Wv.T, conv_wv).reshape(B, T, H, DV)
        beta = jax.nn.sigmoid(x @ Wb.T)
        g = -jnp.exp(A_log) * jax.nn.softplus(x @ Wa.T + dt_bias)
        q = l2norm(q) * DK ** (-0.5)
        k = l2norm(k)

        def step(S, inp):
            qt, kt, vt, gt, bt = inp
            S = S * jnp.exp(gt)[..., None, None]
            v_new = vt - jnp.einsum('bhk,bhkv->bhv', kt, S)
            S = S + bt[..., None, None] * (kt[..., :, None] * v_new[..., None, :])
            o = jnp.einsum('bhk,bhkv->bhv', qt, S)
            return (S, o)
        S0 = jnp.zeros((B, H, DK, DV), x.dtype)
        tm = lambda a: jnp.moveaxis(a, 1, 0)
        _, o = jax.lax.scan(step, S0, (tm(q), tm(k), tm(v), tm(g), tm(beta)))
        o = jnp.moveaxis(o, 0, 1)
        var = jnp.mean(jnp.square(o.astype(jnp.float32)), axis=-1, keepdims=True)
        o = o * jax.lax.rsqrt(var + NORM_EPS).astype(o.dtype) * norm_w
        gate = (x @ Wg.T).reshape(B, T, H, DV)
        o = o * jax.nn.silu(gate)
        return o.reshape(B, T, H * DV) @ Wo.T

    def _L1_attn_b_ref(x, Wqkv_w, Wqkv_b, out_w, out_b):
        import jax, jax.numpy as jnp
        import numpy as np
        D_MODEL = 256
        HEADS = 16
        HEAD_DIM = D_MODEL // HEADS
        B, S, _ = x.shape
        qkv = jnp.einsum('bsd,ed->bse', x, Wqkv_w) + Wqkv_b
        q = qkv[..., :D_MODEL]
        k = qkv[..., D_MODEL:D_MODEL + HEAD_DIM]
        v = qkv[..., D_MODEL + HEAD_DIM:]
        q = q.reshape(B, S, HEADS, HEAD_DIM)
        scale = 1.0 / np.sqrt(HEAD_DIM)
        scores = jnp.einsum('bqhd,bkd->bhqk', q, k) * scale
        min_val = jnp.finfo(scores.dtype).min
        causal = jnp.tril(jnp.ones((S, S), dtype=bool))
        scores = jnp.where(causal[None, None], scores, min_val)
        attn = jax.nn.softmax(scores, axis=-1)
        ctx = jnp.einsum('bhqk,bkd->bqhd', attn, v)
        ctx = ctx.reshape(B, S, D_MODEL)
        out = jnp.einsum('bsd,ed->bse', ctx, out_w) + out_b
        return out

    def _L1_ffn_ref(x, proj1, proj1_bias, proj2, proj2_bias, gate_w):
        import jax, jax.numpy as jnp
        import numpy as np
        L, N, E, H, K = (256, 8, 256, 1024, 8)
        dst = jnp.argmax(jnp.einsum('lne,ek->lnk', x, gate_w), axis=-1)
        h = jax.nn.gelu(jnp.einsum('lne,he->lnh', x, proj1) + proj1_bias, approximate=False)
        out = jnp.einsum('lnh,eh->lne', h, proj2) + proj2_bias
        del dst
        return out
    x = L0_attn_a_x
    x = x + _L0_attn_a_ref(_layernorm(x, axis=-1), L0_attn_a_Wq, L0_attn_a_bq, L0_attn_a_Wl, L0_attn_a_bl, L0_attn_a_Wk, L0_attn_a_bk, L0_attn_a_Wv, L0_attn_a_bv, L0_attn_a_Wq2kv, L0_attn_a_Wkv2h, L0_attn_a_bkv2h, L0_attn_a_Wo, L0_attn_a_bo)
    x = x + _L0_ffn_ref(_layernorm(x, axis=-1), L0_ffn_Wg, L0_ffn_W1, L0_ffn_W2, L0_ffn_W3, L0_ffn_A1, L0_ffn_B1, L0_ffn_A2, L0_ffn_B2, L0_ffn_A3, L0_ffn_B3)
    x = x + _L0_attn_b_ref(_layernorm(x, axis=-1), L0_attn_b_wq, L0_attn_b_wk, L0_attn_b_wv, L0_attn_b_wo, L0_attn_b_inv_freq)
    x = x + _L0_ffn_ref(_layernorm(x, axis=-1), L0_ffn_Wg, L0_ffn_W1, L0_ffn_W2, L0_ffn_W3, L0_ffn_A1, L0_ffn_B1, L0_ffn_A2, L0_ffn_B2, L0_ffn_A3, L0_ffn_B3)
    x = x + _L1_attn_a_ref(_layernorm(x, axis=-1), L1_attn_a_Wq, L1_attn_a_Wk, L1_attn_a_Wv, L1_attn_a_Wb, L1_attn_a_Wa, L1_attn_a_A_log, L1_attn_a_dt_bias, L1_attn_a_conv_wq, L1_attn_a_conv_wk, L1_attn_a_conv_wv, L1_attn_a_Wg, L1_attn_a_norm_w, L1_attn_a_Wo)
    x = x + _L1_ffn_ref(_layernorm(x, axis=-1), L1_ffn_proj1, L1_ffn_proj1_bias, L1_ffn_proj2, L1_ffn_proj2_bias, L1_ffn_gate_w)
    x = x + _L1_attn_b_ref(_layernorm(x, axis=-1), L1_attn_b_Wqkv_w, L1_attn_b_Wqkv_b, L1_attn_b_out_w, L1_attn_b_out_b)
    x = x + _L1_ffn_ref(_layernorm(x, axis=-1), L1_ffn_proj1, L1_ffn_proj1_bias, L1_ffn_proj2, L1_ffn_proj2_bias, L1_ffn_gate_w)
    return x

_drawn_inputs = setup_inputs


def setup_inputs(seed=0):
    import zlib

    import numpy as np

    out = dict(_drawn_inputs(seed))
    spreads = {'L0_attn_a_bq': (0.0, 0.761),
     'L0_attn_a_bl': (0.0, 0.1),
     'L0_attn_a_bk': (0.0, 2.0),
     'L0_attn_a_bv': (0.0, 0.1),
     'L0_attn_a_bkv2h': (0.0, 0.1),
     'L0_attn_a_bo': (0.0, 0.1),
     'L1_attn_a_norm_w': (1.0, 0.6),
     'L1_attn_b_Wqkv_b': (0.0, 0.8),
     'L1_attn_b_out_b': (0.0, 0.8)}
    factors = {'L0_attn_b_inv_freq': 64.0,
     'L0_ffn_Wg': 5.874,
     'L0_ffn_A1': 8.0,
     'L0_ffn_B1': 8.0,
     'L0_ffn_A2': 8.0,
     'L0_ffn_B2': 8.0,
     'L0_ffn_A3': 8.0,
     'L0_ffn_B3': 8.0,
     'L1_attn_a_dt_bias': 49.464,
     'L1_ffn_proj1_bias': 38.96,
     'L1_attn_a_Wb': 8.0,
     'L1_attn_a_Wa': 8.0,
     'L1_attn_a_A_log': 8.0,
     'L1_attn_b_Wqkv_w': 4.265,
     'L1_attn_b_out_w': 3.98,
     'L1_ffn_proj1': 4.737,
     'L1_ffn_proj2': 4.422,
     'L1_ffn_proj2_bias': 8.0}
    for name, (base, spread) in spreads.items():
        noise = np.random.default_rng([zlib.crc32(name.encode()), seed]).standard_normal(out[name].shape)
        drawn = base * np.exp(spread * noise) if base else spread * noise
        out[name] = jnp.asarray(drawn.astype(out[name].dtype))
    for name, factor in factors.items():
        out[name] = (out[name] * factor).astype(out[name].dtype)
    return out
```

```python
from contextlib import ExitStack

import concourse.bass as bass
from concourse import mybir

F32 = mybir.dt.float32
BF16 = mybir.dt.bfloat16
U32 = mybir.dt.uint32
ALU = mybir.AluOpType
ACT = mybir.ActivationFunctionType
AX = mybir.AxisListType

P = 128
B, T, D = 4, 256, 256
S = 2
NT = T // P
KD = D // P
BANKS, BANK = 8, 512
NEG = -1.0e30

NH, HD = 16, 16
NB = 4
NU = NH // NB
PW = HD + 1

F, E, R, TOPK = 896, 8, 32, 2
FT = F // P
ER = E * R
KER = ER // P

GH, DK, DV, CONV = 6, 32, 64, 4
GQK = 2 * GH * DK
GV = GH * DV
GALL = GQK + GV
GT = GALL // P
VT = GV // P
LEVELS = 7
G_MIN = -200.0
SERIES = 8

H1 = 1024
HT1 = H1 // P

LN_EPS, L2_EPS, RMS_EPS = 1e-5, 1e-6, 1e-5

LN_STAGES = 8


class Ring:

    def __init__(self):
        self.n = 0
        self.fills = [0] * BANKS
        self.uses = [0] * BANKS
        self.at = {}

    def claim(self, key, fills=1):
        b = self.n % BANKS
        self.n += 1
        before = self.uses[b]
        self.uses[b] += 1
        self.at[key] = (b, self.fills[b], before + 1)
        self.fills[b] += fills
        return b, before

    def bank(self, key):
        return self.at[key][0]

    def filled(self, key, fill=1):
        return self.at[key][1] + fill

    def drained(self, key):
        return self.at[key][2]


def hybrid_kernel(nc, x_in, masks, packs, where, out):
    with ExitStack() as ctx:
        def sb(name, shape, dt=F32):
            return ctx.enter_context(nc.sbuf_tensor(name, shape, dt))

        def sem(name):
            return ctx.enter_context(nc.semaphore(name))

        GROUPS = [p.shape[1] for p in packs]
        pk = [sb(f"pack{g}", [P, n]) for g, n in enumerate(GROUPS)]

        def w(name, rows=P):
            g, off, n, _ = where[name]
            return pk[g][0:rows, off:off + n]

        def w3(name, k):
            return w(name).rearrange("p (k n) -> p k n", k=k)

        ident = w("ident")
        levb = sb("levb", [P, LEVELS, P], BF16)
        identb = sb("identb", [P, P], BF16)
        negb = sb("negb", [P, P], BF16)
        neg4b = sb("neg4b", [P, 4, P], BF16)
        BROW = dict(a_bo=(32, 0, D), d_bv=(32, D, HD), d_bo=(64, 0, D), f_b2=(96, 0, D))

        def bias_row(name):
            r0, off, n = BROW[name]
            return w("ones")[r0:r0 + 1, :], w("m_spread")[r0:r0 + 1, off:off + n]

        half = sb("half", [P, 1])
        sin_t = sb("sin_t", [P, NT, 8])
        cos_t = sb("cos_t", [P, NT, 8])
        trig = sb("trig", [P, 4, NT * 8])
        expA = sb("expA", [P, GH])

        X = [sb(f"X{s}", [P, NT, D]) for s in range(S)]
        XnT = [sb(f"XnT{s}", [P, KD, T]) for s in range(S)]
        stat = [sb(f"stat{s}", [P, NT, 6]) for s in range(S)]
        mv = [sb(f"mv{s}", [P, NT, 2]) for s in range(S)]
        veps = [sb(f"veps{s}", [P, NT]) for s in range(S)]
        rstd = [sb(f"rstd{s}", [P, NT]) for s in range(S)]
        Vp = [sb(f"Vp{s}", [P, NT, NB, PW]) for s in range(S)]
        PR = 2
        prob = sb("prob", [P, PR, NB, 3 * P])
        probT = sb("probT", [P, PR, NB, 3 * P])
        negmax = sb("negmax", [P, PR, NB, 2])
        rsum = sb("rsum", [P, PR, NT, NB])
        SCR = 7360
        scr = [sb(f"scr{s}", [P, SCR]) for s in range(S)]

        raw = scr[1][:, 0:masks.shape[1]]

        def part(s, off, shape):
            n = 1
            for d in shape:
                n *= d
            assert off + n <= SCR
            v = scr[s][:, off:off + n]
            if len(shape) == 1:
                return v, off + n
            names = "abcd"[:len(shape)]
            pat = "p (" + " ".join(names) + ") -> p " + " ".join(names)
            return v.rearrange(pat, **{names[i]: shape[i] for i in range(len(shape))}), off + n

        Xn = [part(s, 0, [NT, D])[0] for s in range(S)]
        kT, vT, QT, KpT, latT, ctxn, ctxT = ([] for _ in range(7))
        for s in range(S):
            v, o = part(s, 0, [KD, T]); kT.append(v)
            v, o = part(s, o, [KD, T]); vT.append(v)
            v, o = part(s, o, [NU, T]); QT.append(v)
            v, o = part(s, o, [T]); KpT.append(v)
            v, o = part(s, o, [T]); latT.append(v)
            v, _ = part(s, 6656, [NT, D]); ctxn.append(v)
            v, _ = part(s, 0, [KD, T]); ctxT.append(v)
        aT, amT, silu_x, x2T, am2, am2T, am2b, logit = [], [], [], [], [], [], [], []
        for s in range(S):
            v, o = part(s, 0, [4, T]); aT.append(v)
            v, o = part(s, o, [2, 4, T]); amT.append(v)
            v, o = part(s, o, [2, T]); silu_x.append(v)
            v, o = part(s, o, [2, FT, T]); x2T.append(v)
            v, _ = part(s, 0, [NT, ER]); am2.append(v)
            v, _ = part(s, NT * ER, [NT, ER]); am2b.append(v)
            v, _ = part(s, 4 * T, [KER, T]); am2T.append(v)
        lg = [sb(f"lg{s}", [P, NT, E]) for s in range(S)]
        top = [sb(f"top{s}", [P, NT, 8]) for s in range(S)]
        topi = [sb(f"topi{s}", [P, NT, 8], U32) for s in range(S)]
        topf = [sb(f"topf{s}", [P, NT, 8]) for s in range(S)]
        rw = [sb(f"rw{s}", [P, 4, NT]) for s in range(S)]
        onehot = [sb(f"onehot{s}", [P, NT, 2, E]) for s in range(S)]
        onehotw = [sb(f"onehotw{s}", [P, NT, 2, E]) for s in range(S)]
        onehotT = [sb(f"onehotT{s}", [2 * E, T]) for s in range(S)]
        rot, rtmp, bV, prod, sc, pw = [], [], [], [], [], []
        for s in range(S):
            v, o = part(s, 0, [NT, 2 * NH, HD]); rot.append(v)
            v, o = part(s, o, [NT, NH, HD]); bV.append(v)
            v, o = part(s, o, [NH, NH, HD]); prod.append(v)
            v, _ = part(s, 1536, [2, 2 * NH, HD]); rtmp.append(v)
            v, o = part(s, o, [NT, NH, NH]); sc.append(v)
            v, o = part(s, o, [NT, NH, NH]); pw.append(v)
        bmax = [sb(f"bmax{s}", [P, NT, NH]) for s in range(S)]
        bsum = [sb(f"bsum{s}", [P, NT, NH]) for s in range(S)]
        convT, tokm, gate, kb, bv, KTt, QTt, KbT, QgT, G1, EG, AT, PT = ([] for _ in range(13))
        sqs = []
        kd, kbg, qg, Ukn, U0, U1, S1, osq, on, onT = ([] for _ in range(10))
        MAT = [GH, NT, P]
        for s in range(S):
            v, o = part(s, 0, [GT, T]); convT.append(v)
            v, o = part(s, o, [GT, T]); tokm.append(v.rearrange("p a b -> p (a b)").rearrange("p (a b) -> p a b", a=NT))
            v, o = part(s, o, [NT, GV]); gate.append(v)
            v, o = part(s, o, [NT, GH * DK]); kb.append(v)
            v, o = part(s, o, [NT, GV]); bv.append(v)
            v, o = part(s, o, [2, T]); KTt.append(v)
            v, o = part(s, o, [2, T]); QTt.append(v)
            v, o = part(s, o, [2, T]); KbT.append(v)
            v, o = part(s, o, [2, P]); QgT.append(v)
            v, o = part(s, o, [GH * DK]); kd.append(v)
            v, o = part(s, o, [GH * DK]); kbg.append(v)
            v, o = part(s, o, [GH * DK]); qg.append(v)
            v, _ = part(s, 0, MAT); PT.append(v)
            v, _ = part(s, 0, [NT, GQK]); sqs.append(v)
            v, _ = part(s, 1536, [NT, GV]); osq.append(v)
            v, o2 = part(s, 1536 + 768, [NT, GV]); on.append(v)
            v, _ = part(s, 4992, [VT, T]); onT.append(v)
        def mat(buf, i):
            n = GH * NT * P
            return buf[:, :, :, :].rearrange("p r j n -> p (r j n)")[:, i * n:(i + 1) * n]\
                .rearrange("p (h a i) -> p h a i", h=GH, a=NT)

        G1s, EGs = mat(prob, 0), mat(prob, 1)
        ATs = [part(s, 1536, MAT)[0] for s in range(S)]
        Ams = EGs
        Tms, Wms = mat(probT, 0), mat(probT, 1)
        Yms = G1s
        small = [sb(f"small{s}", [P, 16, NT, GH]) for s in range(S)]
        ss = [sb(f"ss{s}", [P, NT, 2 * GH]) for s in range(S)]
        fac = [sb(f"fac{s}", [P, NT, 2 * GH]) for s in range(S)]
        expin = [sb(f"expin{s}", [P, NT, 2 * GH]) for s in range(S)]
        expo = [sb(f"expo{s}", [P, NT, 2 * GH]) for s in range(S)]
        gdec = [sb(f"gdec{s}", [P, 2, GH]) for s in range(S)]
        U0s = [part(s, 3840, [GV])[0] for s in range(S)]
        U1s = [part(s, 4992, [GV])[0] for s in range(S)]
        Ukns = [part(s, 5504, [2, P])[0] for s in range(S)]
        S1s = [part(s, 5760, [2, DV])[0] for s in range(S)]
        rv = [sb(f"rv{s}", [P, NT, GH]) for s in range(S)]
        rr = [sb(f"rr{s}", [P, NT, GH]) for s in range(S)]
        HT = []
        for s in range(S):
            v, o = part(s, 0, [HT1, T]); HT.append(v)

        bank = [ctx.enter_context(nc.psum_tensor(f"bank{b}", [P, BANK], F32)) for b in range(BANKS)]

        loaded = [sem(f"loaded{g}") for g in range(len(packs))]
        const_ready = sem("const_ready")
        prep = sem("prep")
        prep_pool = sem("prep_pool")
        masks_loaded = sem("masks_loaded")
        trig_in, trig_out = sem("trig_in"), sem("trig_out")
        arrived = sem("arrived")
        settled = sem("settled")
        turn = sem("turn")
        turn_sems = []

        def tsem(name):
            turn_sems.append(sem(name))
            return turn_sems[-1]

        full = [tsem(f"full{b}") for b in range(BANKS)]
        drained = [tsem(f"drained{b}") for b in range(BANKS)]
        x_loaded = [tsem(f"x_loaded{s}") for s in range(S)]
        x_stored = tsem("x_stored")
        act_step, dve_step, pool_step = tsem("act_step"), tsem("dve_step"), tsem("pool_step")
        var_ready = tsem("var_ready")
        rstd_ready = tsem("rstd_ready")
        xn_ready = tsem("xn_ready")
        x_final = tsem("x_final")
        max_ready = tsem("max_ready")
        prob_ready = tsem("prob_ready")
        ctx_ready = tsem("ctx_ready")
        top_diff = tsem("top_diff")
        top_exp = tsem("top_exp")
        onehot_ready = tsem("onehot_ready")
        am_ready = tsem("am_ready")
        silu_ready = tsem("silu_ready")
        x2_first = tsem("x2_first")
        am2_ready = tsem("am2_ready")
        b_in = tsem("b_in")
        b_exp = tsem("b_exp")
        bctx_ready = tsem("bctx_ready")
        conv_ready = tsem("conv_ready")
        convs_ready = tsem("convs_ready")
        gate_in = tsem("gate_in")
        gate_exp = tsem("gate_exp")
        g_ready = tsem("g_ready")
        g1_ready = tsem("g1_ready")
        sq_ready = tsem("sq_ready")
        rn_ready = tsem("rn_ready")
        qk_ready = tsem("qk_ready")
        bv_ready = tsem("bv_ready")
        gdec_ready = tsem("gdec_ready")
        kdec_ready = tsem("kdec_ready")
        at_ready = tsem("at_ready")
        am_mask = tsem("am_mask")
        w_ready = tsem("w_ready")
        osq_ready = tsem("osq_ready")
        orms_in = tsem("orms_in")
        orms = tsem("orms")
        gn_ready = tsem("gn_ready")
        on_ready = tsem("on_ready")
        sem_lo = min(q.num for q in turn_sems)
        sem_hi = max(q.num for q in turn_sems) + 1
        assert sem_hi - sem_lo == len(turn_sems)

        ring = Ring()
        LIB = {}

        def psum(key, *shape):
            v = bank[ring.bank(key)]
            n = 1
            for d in shape:
                n *= d
            v = v[:, 0:n]
            if len(shape) > 1:
                names = "abc"[:len(shape)]
                v = v.rearrange("p (" + " ".join(names) + ") -> p " + " ".join(names),
                                **{names[i]: shape[i] for i in range(len(shape))})
            return v

        def wait_full(eng, key, fill=1):
            eng.wait_ge(full[ring.bank(key)], ring.filled(key, fill))

        def wait_drained(eng, key):
            eng.wait_ge(drained[ring.bank(key)], ring.drained(key))

        def claim(pe, key, fills=1):
            b, before = ring.claim(key, fills)
            if before:
                pe.wait_ge(drained[b], before)
            return bank[b]

        def drain_of(key):
            return drained[ring.bank(key)]

        def bcast(ap, n):
            return ap.unsqueeze(ap.ndim if hasattr(ap, "ndim") else len(ap.shape)).broadcast_to(list(ap.shape) + [n])

        def program(stage):
            for s in range(S):
                stage("norm", 0, s)
                stage("qkv_a", 0, s)
            stage("attend", 0, 0)
            for s in range(S):
                stage("out_a", 0, s)
                stage("norm", 1, s)
            for s in range(S):
                stage("moe", 0, s)
            for s in range(S):
                stage("norm", 2, s)
                stage("heads_in", 0, s)
            for s in range(S):
                stage("heads", 0, s)
            for s in range(S):
                stage("norm", 3, s)
            for s in range(S):
                stage("moe", 1, s)
            for s in range(S):
                stage("norm", 4, s)
                stage("delta_in", 0, s)
            for s in range(S):
                stage("delta_mid", 0, s)
            for s in range(S):
                stage("delta_out", 0, s)
            for s in range(S):
                stage("norm", 5, s)
                stage("ffn", 0, s)
            for s in range(S):
                stage("norm", 6, s)
                stage("qkv_b", 0, s)
            stage("attend", 1, 0)
            for s in range(S):
                stage("out_b", 0, s)
                stage("norm", 7, s)
            for s in range(S):
                stage("ffn", 1, s)

        block = ctx.enter_context(nc.Block())

        @block.sync
        def _(sp):
            for g in range(1, len(packs)):
                sp.dma_start(pk[g][:, :], packs[g]).then_inc(loaded[g], 16)
            with sp.Fori(0, B // S, 1) as it:
                for s in range(S):
                    sp.dma_start(X[s][:, :, :], x_in[it * S + s].rearrange("(a p) d -> p a d", p=P))\
                      .then_inc(x_loaded[s], 16)
                for s in range(S):
                    sp.wait_ge(x_final, s + 1)
                    sp.dma_start(out[it * S + s].rearrange("(a p) d -> p a d", p=P), X[s][:, :, :])\
                      .then_inc(x_stored, 16)
                sp.wait_ge(x_stored, 16 * S)
                sp.wait_ge(arrived, it * 4 + 4)
                sp.sem_inc(settled, 1)
                sp.sem_clear(range(sem_lo, sem_hi))
                sp.sem_inc(turn, 1)

        def next_turn(eng, it):
            eng.sem_inc(arrived, 1)
            eng.wait_ge(turn, it + 1)

        @block.tensor
        def _(pe):
            def mm(o, l, r, start, stop=True):
                return pe.matmul(o, l, r, start=start, stop=stop, skip_group_check=True)

            def transposes(key, src, n, dst_cols=P):
                o = claim(pe, key)
                for t in range(n):
                    for a in range(NT):
                        last = pe.transpose(o[:, t * T + a * P:t * T + a * P + P], src(t, a), ident)
                last.then_inc(full[ring.bank(key)], 1)

            def group(o, pairs, start=True):
                for i, (l, r) in enumerate(pairs):
                    last = mm(o, l, r, start and i == 0, i == len(pairs) - 1)
                return last

            def norm(k, s):
                pe.wait_ge(xn_ready, S * k + s + 1)
                transposes(("xnT", k, s), lambda t, a: Xn[s][:, a, t * P:(t + 1) * P], KD)

            def proj(key, s, weights, tiles, per, k=KD):
                for i in range(0, tiles, per):
                    o = claim(pe, key + (i // per,))
                    for j in range(i, min(i + per, tiles)):
                        last = group(o[:, (j - i) * T:(j - i + 1) * T],
                                     [(weights(c, j), XnT[s][:, c, :]) for c in range(k)])
                    last.then_inc(full[ring.bank(key + (i // per,))], 1)

            def qkv_a(_, s):
                wait_drained(pe, ("xnT", 0, s))
                lat, wk, wv = w3("a_wl", KD), w("a_wk"), w("a_wv")
                proj(("lat", s), s, lambda c, j: lat[:, c, :], 1, 1)
                wq = w3("a_wq", KD)
                proj(("q", 0, s), s, lambda c, j: wq[:, c, j * P:(j + 1) * P], NU, 2)
                wait_drained(pe, ("lat", s, 0))
                for name, wt in (("k", wk), ("v", wv)):
                    o = claim(pe, (name + "T", s))
                    for j in range(KD):
                        last = group(o[:, j * T:(j + 1) * T], [(wt[:, j * P:(j + 1) * P], latT[s][:, :])])
                    last.then_inc(full[ring.bank((name + "T", s))], 1)
                wait_drained(pe, ("kT", s))
                w2 = w3("a_kfold", KD)
                o = claim(pe, ("kp", 0, s))
                group(o[:, 0:T], [(w2[:, c, :], kT[s][:, c, :]) for c in range(KD)])\
                    .then_inc(full[ring.bank(("kp", 0, s))], 1)
                wait_drained(pe, ("vT", s))
                w2 = w3("a_vfold", KD)
                o = claim(pe, ("vp", 0, s))
                for a in range(NT):
                    last = group(o[:, a * 64:a * 64 + 64],
                                 [(vT[s][:, c, a * P:(a + 1) * P], w2[:, c, :]) for c in range(KD)])
                last.then_inc(full[ring.bank(("vp", 0, s))], 1)

            def qkv_b(_, s):
                wait_drained(pe, ("xnT", 6, s))
                pe.wait_ge(loaded[4], 16)
                wq, wk, wv = w3("d_wq", KD), w3("d_wk", KD), w3("d_wv", KD)
                proj(("q", 1, s), s, lambda c, j: wq[:, c, j * P:(j + 1) * P], NU, 2)
                o = claim(pe, ("kp", 1, s))
                group(o[:, 0:T], [(wk[:, c, :], XnT[s][:, c, :]) for c in range(KD)])\
                    .then_inc(full[ring.bank(("kp", 1, s))], 1)
                o = claim(pe, ("vp", 1, s))
                for a in range(NT):
                    last = group(o[:, a * HD:(a + 1) * HD],
                                 [bias_row("d_bv")]
                                 + [(XnT[s][:, c, a * P:(a + 1) * P], wv[:, c, :]) for c in range(KD)])
                last.then_inc(full[ring.bank(("vp", 1, s))], 1)

            def attend(k, _):
                def scores(g):
                    s, u = divmod(g, NU)
                    if u == 0:
                        wait_drained(pe, ("q", k, s, 0))
                        wait_drained(pe, ("q", k, s, 1))
                        wait_drained(pe, ("kp", k, s))
                        wait_drained(pe, ("vp", k, s))
                    for j in range(NB):
                        claim(pe, ("sc", k, g, j))
                    for j in range(NB):
                        o = bank[ring.bank(("sc", k, g, j))]
                        q = QT[s][32 * j:32 * j + HD, u, :]
                        kk = KpT[s][32 * j:32 * j + HD, :]
                        mm(o[:, 0:T], q[:, P:T], kk, True)
                        mm(o[:, T:T + P], q[:, 0:P], kk[:, 0:P], False)
                    for j in range(NB):
                        o = bank[ring.bank(("sc", k, g, j))]
                        mm(o[:, P:T], identb[:, :], negb[:, :], False)
                        mm(o[:, T:T + P], identb[:, :], negb[:, :], False)\
                            .then_inc(full[ring.bank(("sc", k, g, j))], 1)

                def weights_t(g):
                    for j in range(NB):
                        o = claim(pe, ("pT", k, g, j))
                        if j == 0:
                            pe.wait_ge(prob_ready, (k * S * NU + g) * NB + NB)
                        for c in range(3):
                            last = pe.transpose(o[:, c * P:(c + 1) * P],
                                                prob[:, g % PR, j, c * P:(c + 1) * P], ident)
                        last.then_inc(full[ring.bank(("pT", k, g, j))], 1)

                def values(g):
                    s, u = divmod(g, NU)
                    o = claim(pe, ("pv", k, g))
                    for j in range(NB):
                        wait_drained(pe, ("pT", k, g, j))
                        pt = probT[:, g % PR, j, :]
                        mm(o[:, j * PW:(j + 1) * PW], pt[:, 2 * P:3 * P], Vp[s][:, 0, j, :], True)
                        c = (NB + j) * PW
                        last = group(o[:, c:c + PW], [(pt[:, 0:P], Vp[s][:, 0, j, :]),
                                                      (pt[:, P:2 * P], Vp[s][:, 1, j, :])])
                    last.then_inc(full[ring.bank(("pv", k, g))], 1)

                scores(0)
                for g in range(S * NU):
                    if g + 1 < S * NU:
                        scores(g + 1)
                    weights_t(g)
                    values(g)

            def out_proj(k, s, name, bias):
                if k == 0 and s == 0:
                    pe.wait_ge(loaded[1], 16)
                pe.wait_ge(ctx_ready, k * S + s + 1)
                transposes(("ctxT", k, s), lambda t, a: ctxn[s][:, a, t * P:(t + 1) * P], KD)
                wait_drained(pe, ("ctxT", k, s))
                wo = w3(name, KD)
                o = claim(pe, ("y", k, s))
                for a in range(NT):
                    last = group(o[:, a * D:(a + 1) * D],
                                 ([bias_row(bias)] if bias else [])
                                 + [(ctxT[s][:, c, a * P:(a + 1) * P], wo[:, c, :]) for c in range(KD)])
                last.then_inc(full[ring.bank(("y", k, s))], 1)

            def out_a(_, s):
                out_proj(0, s, "a_wo", "a_bo")

            def out_b(_, s):
                out_proj(1, s, "d_wo", "d_bo")

            def moe(k, s):
                r = k * S + s
                ln = 1 if k == 0 else 3
                if r == 0:
                    pe.wait_ge(loaded[1], 16)
                wait_drained(pe, ("xnT", ln, s))
                wa, wg = w3("m_a", KD), w3("m_g", KD)
                o = claim(pe, ("lg", r))
                for a in range(NT):
                    last = group(o[:, a * E:(a + 1) * E],
                                 [(XnT[s][:, c, a * P:(a + 1) * P], wg[:, c, :]) for c in range(KD)])
                last.then_inc(full[ring.bank(("lg", r))], 1)
                proj(("aT", r), s, lambda c, j: wa[:, c, j * P:(j + 1) * P], 4, 2)
                pe.wait_ge(onehot_ready, r + 1)
                o = claim(pe, ("oh", r))
                for a in range(NT):
                    last = pe.transpose(o[0:2 * E, a * P:(a + 1) * P],
                                        onehot[s][:, a].rearrange("p k e -> p (k e)"), ident)
                last.then_inc(full[ring.bank(("oh", r))], 1)
                wait_drained(pe, ("oh", r))
                ex = w("m_spread", 2 * E).rearrange("p (i n) -> p i n", i=2)
                for i in range(2):
                    o = claim(pe, ("ex", r, i))
                    for t in range(KER):
                        last = mm(o[:, t * T:(t + 1) * T], ex[:, i, t * P:(t + 1) * P], onehotT[s][:, :], True)
                    last.then_inc(full[ring.bank(("ex", r, i))], 1)
                w1, w3_, b1, b3 = w3("m_w1", KD), w3("m_w3", KD), w3("m_b1", KER), w3("m_b3", KER)
                pe.wait_ge(am_ready, 4 * r + 2)
                for m in range(FT):
                    o = claim(pe, ("x", r, m), fills=2)
                    c0 = slice(m * P, (m + 1) * P)
                    group(o[:, 0:T], [(w1[:, c, c0], XnT[s][:, c, :]) for c in range(KD)]
                          + [(b1[:, c, c0], amT[s][:, 0, c, :]) for c in range(KER)])
                    group(o[:, T:2 * T], [(w3_[:, c, c0], XnT[s][:, c, :]) for c in range(KD)]
                          + [(b3[:, c, c0], amT[s][:, 0, 2 + c, :]) for c in range(KER)], start=False)\
                        .then_inc(full[ring.bank(("x", r, m))], 1)
                pe.wait_ge(am_ready, 4 * r + 4)
                for m in range(FT):
                    o = bank[ring.bank(("x", r, m))]
                    c0 = slice(m * P, (m + 1) * P)
                    pe.wait_ge(x2_first, r * FT + m + 1)
                    group(o[:, 0:T], [(b1[:, c, c0], amT[s][:, 1, c, :]) for c in range(KER)], start=False)
                    group(o[:, T:2 * T], [(b3[:, c, c0], amT[s][:, 1, 2 + c, :]) for c in range(KER)],
                          start=False).then_inc(full[ring.bank(("x", r, m))], 1)
                wd = w3("m_down", FT)
                for i in range(TOPK):
                    for a in range(NT):
                        o = claim(pe, ("down", r, i, a))
                        if i == 1 and a == 0:
                            for m in range(FT):
                                wait_drained(pe, ("x", r, m))
                        group(o[:, :], [(x2T[s][:, i, m, a * P:(a + 1) * P], wd[:, m, :]) for m in range(FT)])\
                            .then_inc(full[ring.bank(("down", r, i, a))], 1)
                pe.wait_ge(am2_ready, r + 1)
                transposes(("am2T", r), lambda t, a: am2[s][:, a, t * P:(t + 1) * P], KER)
                wait_drained(pe, ("am2T", r))
                b2 = w3("m_b2", KER)
                o = claim(pe, ("lora2", r))
                for a in range(NT):
                    last = group(o[:, a * D:(a + 1) * D],
                                 [(am2T[s][:, c, a * P:(a + 1) * P], b2[:, c, :]) for c in range(KER)])
                last.then_inc(full[ring.bank(("lora2", r))], 1)

            def heads_in(_, s):
                wait_drained(pe, ("xnT", 2, s))
                if s == 0:
                    pe.wait_ge(loaded[2], 16)
                wqkv = w3("b_wqkv", KD)
                for a in range(NT):
                    o = claim(pe, ("bqk", s, a))
                    group(o[:, :], [(XnT[s][:, c, a * P:(a + 1) * P], wqkv[:, c, 0:2 * D]) for c in range(KD)])\
                        .then_inc(full[ring.bank(("bqk", s, a))], 1)
                o = claim(pe, ("bv", s))
                for a in range(NT):
                    last = group(o[:, a * D:(a + 1) * D],
                                 [(XnT[s][:, c, a * P:(a + 1) * P], wqkv[:, c, 2 * D:3 * D]) for c in range(KD)])
                last.then_inc(full[ring.bank(("bv", s))], 1)

            def heads(_, s):
                pe.wait_ge(bctx_ready, s + 1)
                transposes(("bctxT", s), lambda t, a: ctxn[s][:, a, t * P:(t + 1) * P], KD)
                wait_drained(pe, ("bctxT", s))
                wo = w3("b_wo", KD)
                o = claim(pe, ("by", s))
                for a in range(NT):
                    last = group(o[:, a * D:(a + 1) * D],
                                 [(ctxT[s][:, c, a * P:(a + 1) * P], wo[:, c, :]) for c in range(KD)])
                last.then_inc(full[ring.bank(("by", s))], 1)

            def delta_in(_, s):
                wait_drained(pe, ("xnT", 4, s))
                if s == 0:
                    pe.wait_ge(loaded[3], 16)
                wqkv, wba, wg = w3("c_wqkv", KD), w3("c_wba", KD), w3("c_wg", KD)
                o = claim(pe, ("ba", s))
                for a in range(NT):
                    last = group(o[:, a * 2 * GH:(a + 1) * 2 * GH],
                                 [(XnT[s][:, c, a * P:(a + 1) * P], wba[:, c, :]) for c in range(KD)])
                last.then_inc(full[ring.bank(("ba", s))], 1)
                proj(("cv", s), s, lambda c, j: wqkv[:, c, j * P:(j + 1) * P], GT, 2)
                for a in range(NT):
                    o = claim(pe, ("gt", s, a))
                    group(o[:, 0:GV], [(XnT[s][:, c, a * P:(a + 1) * P], wg[:, c, :]) for c in range(KD)])\
                        .then_inc(full[ring.bank(("gt", s, a))], 1)

            def delta_mid(_, s):
                pe.wait_ge(convs_ready, GT // 2 * (s + 1))
                for a in range(NT):
                    for part_, (lo, hi) in enumerate(((0, 4), (4, GT))):
                        o = claim(pe, ("tm", s, a, part_))
                        for t in range(lo, hi):
                            last = pe.transpose(o[:, (t - lo) * P:(t - lo + 1) * P],
                                                convT[s][:, t, a * P:(a + 1) * P], ident)
                        last.then_inc(full[ring.bank(("tm", s, a, part_))], 1)
                pe.wait_ge(g_ready, s + 1)
                o = claim(pe, ("gd", s))
                gl = small[s][:, 9]
                mm(o[:, 0:GH], w("tri_up"), gl[:, 1, :], True)
                mm(o[:, GH:2 * GH], w("low_strict"), gl[:, 0, :], True).then_inc(full[ring.bank(("gd", s))], 1)
                pe.wait_ge(g1_ready, s + 1)
                for q in range(GH // 2):
                    o = claim(pe, ("L", s, q))
                    for hh in range(2):
                        for a in range(NT):
                            c = (hh * NT + a) * P
                            mm(o[:, c:c + P], G1s[:, 2 * q + hh, a, :], w("tri_up"), hh + a == 0)
                    mm(o[:, :], identb[:, :], neg4b[:, :, :].rearrange("p a b -> p (a b)"), False)\
                        .then_inc(full[ring.bank(("L", s, q))], 1)
                pe.wait_ge(qk_ready, s + 1)
                for name, src in (("K", lambda a: tokm[s][:, a, GH * DK:2 * GH * DK]),
                                  ("Kb", lambda a: kb[s][:, a, :]),
                                  ("Q", lambda a: tokm[s][:, a, 0:GH * DK])):
                    o = claim(pe, (name, s))
                    for a in range(NT):
                        pe.transpose(o[:, a * P:(a + 1) * P], src(a)[:, 0:P], ident)
                        last = pe.transpose(o[0:64, T + a * P:T + (a + 1) * P], src(a)[:, P:GH * DK], ident)
                    last.then_inc(full[ring.bank((name, s))], 1)
                for name, right in (("A", KbT), ("PT", QTt)):
                    if name == "A":
                        wait_drained(pe, ("K", s))
                        wait_drained(pe, ("Kb", s))
                    else:
                        wait_drained(pe, ("Q", s))
                    for b in range(4):
                        claim(pe, (name, s, b))
                    for b in range(4):
                        o = bank[ring.bank((name, s, b))]
                        r0 = slice(32 * b, 32 * b + 32)
                        for t in range(2 if b < 2 else 1):
                            for a in range(NT):
                                c = (t * NT + a) * P
                                last = mm(o[:, c:c + P], KTt[s][r0, t, a * P:(a + 1) * P],
                                          right[s][r0, t, a * P:(a + 1) * P], t + a == 0)
                        last.then_inc(full[ring.bank((name, s, b))], 1)
                pe.wait_ge(kdec_ready, s + 1)
                o = claim(pe, ("Qg", s))
                pe.transpose(o[:, 0:P], qg[s][:, 0:P], ident)
                pe.transpose(o[0:64, P:2 * P], qg[s][:, P:GH * DK], ident).then_inc(full[ring.bank(("Qg", s))], 1)
                pe.wait_ge(w_ready, s + 1)
                for q in range(GH // 2):
                    o = claim(pe, ("T0", s, q))
                    for hh in range(2):
                        for a in range(NT):
                            c = (hh * NT + a) * P
                            last = pe.transpose(o[:, c:c + P], Wms[:, 2 * q + hh, a, :], ident)
                    last.then_inc(full[ring.bank(("T0", s, q))], 1)

                def triple(name, l, q, left, right):
                    o = claim(pe, (name, s, l, q))
                    for hh in range(2):
                        for a in range(NT):
                            c = (hh * NT + a) * P
                            last = mm(o[:, c:c + P], left[:, 2 * q + hh, a, :], right[:, 2 * q + hh, a, :],
                                      hh + a == 0)
                    last.then_inc(full[ring.bank((name, s, l, q))], 1)

                for l in range(1, LEVELS):
                    pe.wait_ge(am_mask, s * LEVELS + l + 1)
                    for q in range(GH // 2):
                        wait_drained(pe, ("T0", s, q) if l == 1 else ("dT", s, l - 1, q))
                        triple("Y", l, q, Ams, Tms)
                    for q in range(GH // 2):
                        wait_drained(pe, ("Y", s, l, q))
                        if l > 1:
                            wait_drained(pe, ("dW", s, l - 1, q))
                        if l < LEVELS - 1:
                            triple("dT", l, q, Wms, Yms)
                        triple("dW", l, q, Yms, Wms)
                for q in range(GH // 2):
                    wait_drained(pe, ("dW", s, LEVELS - 1, q))
                pe.wait_ge(bv_ready, s + 1)
                o = claim(pe, ("U0", s))
                for h in range(GH):
                    last = mm(o[:, h * DV:(h + 1) * DV], Wms[:, h, 0, :], bv[s][:, 0, h * DV:(h + 1) * DV], True)
                last.then_inc(full[ring.bank(("U0", s))], 1)
                o = claim(pe, ("Uk", s))
                for h in range(GH):
                    r0 = 32 * (h % 4)
                    t = h // 4
                    last = mm(o[r0:r0 + 32, t * P:(t + 1) * P], kbg[s][:, h * DK:(h + 1) * DK], Wms[:, h, 1, :], True)
                last.then_inc(full[ring.bank(("Uk", s))], 1)
                wait_drained(pe, ("U0", s))
                o = claim(pe, ("S1", s))
                for h in range(GH):
                    r0 = 32 * (h % 4)
                    t = h // 4
                    last = mm(o[r0:r0 + 32, t * DV:(t + 1) * DV], kd[s][:, h * DK:(h + 1) * DK],
                              U0s[s][:, h * DV:(h + 1) * DV], True)
                last.then_inc(full[ring.bank(("S1", s))], 1)
                wait_drained(pe, ("S1", s))
                wait_drained(pe, ("Uk", s))
                for b in range(4):
                    o = claim(pe, ("U1", s, b))
                    r0 = slice(32 * b, 32 * b + 32)
                    for t in range(2 if b < 2 else 1):
                        h = b + 4 * t
                        last = group(o[:, t * DV:(t + 1) * DV],
                                     [(Wms[:, h, 1, :], bv[s][:, 1, h * DV:(h + 1) * DV]),
                                      (Ukns[s][r0, t, :], S1s[s][r0, t, :])])
                    last.then_inc(full[ring.bank(("U1", s, b))], 1)
                for b in range(4):
                    wait_drained(pe, ("PT", s, b))
                o = claim(pe, ("O", s, 0))
                for h in range(GH):
                    last = mm(o[:, h * DV:(h + 1) * DV], PT[s][:, h, 0, :], U0s[s][:, h * DV:(h + 1) * DV], True)
                last.then_inc(full[ring.bank(("O", s, 0))], 1)
                wait_drained(pe, ("Qg", s))
                for b in range(4):
                    wait_drained(pe, ("U1", s, b))
                    o = claim(pe, ("O1", s, b))
                    r0 = slice(32 * b, 32 * b + 32)
                    for t in range(2 if b < 2 else 1):
                        h = b + 4 * t
                        last = group(o[:, t * DV:(t + 1) * DV],
                                     [(PT[s][:, h, 1, :], U1s[s][:, h * DV:(h + 1) * DV]),
                                      (QgT[s][r0, t, :], S1s[s][r0, t, :])])
                    last.then_inc(full[ring.bank(("O1", s, b))], 1)

            def delta_out(_, s):
                pe.wait_ge(on_ready, s + 1)
                for i, (lo, hi) in enumerate(((0, 2), (2, VT))):
                    transposes(("onT", s, i), lambda t, a: on[s][:, a, (lo + t) * P:(lo + t + 1) * P], hi - lo)
                wait_drained(pe, ("onT", s, 0))
                wait_drained(pe, ("onT", s, 1))
                wo = w3("c_wo", VT)
                o = claim(pe, ("cy", s))
                for a in range(NT):
                    last = group(o[:, a * D:(a + 1) * D],
                                 [(onT[s][:, c, a * P:(a + 1) * P], wo[:, c, :]) for c in range(VT)])
                last.then_inc(full[ring.bank(("cy", s))], 1)

            def ffn(k, s):
                r = k * S + s
                if r == 0:
                    pe.wait_ge(loaded[5], 16)
                wait_drained(pe, ("xnT", 5 + 2 * k, s))
                w1, w2 = w3("f_w1", KD), w3("f_w2", HT1)
                proj(("h", r), s, lambda c, j: w1[:, c, j * P:(j + 1) * P], HT1, 2)
                for i in range(HT1 // 2):
                    wait_drained(pe, ("h", r, i))
                o = claim(pe, ("fy", r))
                for a in range(NT):
                    last = group(o[:, a * D:(a + 1) * D],
                                 [bias_row("f_b2")]
                                 + [(HT[s][:, m, a * P:(a + 1) * P], w2[:, m, :]) for m in range(HT1)])
                last.then_inc(full[ring.bank(("fy", r))], 1)

            table = dict(norm=norm, qkv_a=qkv_a, attend=attend, out_a=out_a, moe=moe, heads_in=heads_in,
                         heads=heads, delta_in=delta_in, delta_mid=delta_mid, delta_out=delta_out, ffn=ffn,
                         qkv_b=qkv_b, out_b=out_b)
            pe.wait_ge(loaded[0], 16)
            pe.wait_ge(const_ready, 4)
            with pe.Fori(0, B // S, 1) as it:
                program(lambda name, k, s: table[name](k, s))
                next_turn(pe, it)

        @block.scalar
        def _(act):
            count = [0]

            def step(ins):
                count[0] += 1
                ins.then_inc(act_step, 1)
                return count[0]

            def move(key, dst, src, func=ACT.Copy, **kw):
                act.activation(dst, src, func, **kw).then_inc(drain_of(key), 1)

            def norm(k, s):
                key = ("xnT", k, s)
                wait_full(act, key)
                move(key, XnT[s][:, :, :], psum(key, KD, T))

            def qkv_a(_, s):
                key = ("lat", s, 0)
                wait_full(act, key)
                move(key, latT[s][:, :], psum(key, T), ACT.Silu, bias=w("a_bl"))

            def qkv_b(_, s):
                pass

            def attend(k, _):
                def exps(g):
                    for j in range(NB):
                        key = ("sc", k, g, j)
                        act.wait_ge(max_ready, (k * S * NU + g) * NB + j + 1)
                        if g >= PR and j == 0:
                            wait_full(act, ("pT", k, g - PR, NB - 1))
                        elif k == 1 and j == 0:
                            wait_full(act, ("pT", 0, S * NU - PR + g, NB - 1))
                        src = psum(key, 3 * P)
                        dst = prob[:, g % PR, j, :]
                        act.activation(dst[:, 0:T], src[:, 0:T], ACT.Exp,
                                       bias=negmax[:, g % PR, j, 1:2]).then_inc(prob_ready, 1)
                        act.activation(dst[:, T:T + P], src[:, T:T + P], ACT.Exp,
                                       bias=negmax[:, g % PR, j, 0:1]).then_inc(drain_of(key), 1)

                for g in range(S * NU):
                    exps(g)

            def out_any(k, s, bias):
                key = ("ctxT", k, s)
                wait_full(act, key)
                if bias is None:
                    move(key, ctxT[s][:, :, :], psum(key, KD, T))
                else:
                    move(key, ctxT[s][:, :, :], psum(key, KD, T), ACT.Identity, bias=bias)

            def out_a(_, s):
                out_any(0, s, w("a_b2"))

            def out_b(_, s):
                out_any(1, s, None)

            def moe(k, s):
                r = k * S + s
                for i in range(2):
                    key = ("aT", r, i)
                    wait_full(act, key)
                    move(key, aT[s][:, 2 * i:2 * i + 2, :], psum(key, 2, T))
                act.wait_ge(top_diff, r + 1)
                act.activation(rw[s][:, 2, :], rw[s][:, 3, :], ACT.Exp).then_inc(top_exp, 1)
                key = ("oh", r)
                wait_full(act, key)
                move(key, onehotT[s][:, :], psum(key, T)[0:2 * E])
                for i in range(TOPK):
                    for m in range(FT):
                        key = ("x", r, m)
                        n = (r * TOPK + i) * FT + m
                        wait_full(act, key, i + 1)
                        j = i * FT + m
                        if j >= 2:
                            if j - 2 < FT:
                                act.wait_ge(x2_first, r * FT + j - 1)
                            else:
                                wait_drained(act, ("x", r, j - 2 - FT))
                        act.activation(silu_x[s][:, j % 2, :], psum(key, T), ACT.Silu).then_inc(silu_ready, 1)
                key = ("am2T", r)
                wait_full(act, key)
                move(key, am2T[s][:, :, :], psum(key, KER, T))

            def heads_in(_, s):
                key = ("bv", s)
                wait_full(act, key)
                move(key, bV[s][:, :, :, :].rearrange("p a h d -> p (a h d)"), psum(key, NT * D))

            def heads(_, s):
                for a in range(NT):
                    act.wait_ge(b_in, s * NT + a + 1)
                    act.activation(pw[s][:, a], sc[s][:, a], ACT.Exp, scale=HD ** -0.5).then_inc(b_exp, 1)
                key = ("bctxT", s)
                wait_full(act, key)
                move(key, ctxT[s][:, :, :], psum(key, KD, T))

            def delta_in(_, s):
                for i in range(GT // 2):
                    act.wait_ge(conv_ready, s * (GT // 2) + i + 1)
                    act.activation(convT[s][:, 2 * i:2 * i + 2, :], convT[s][:, 2 * i:2 * i + 2, :], ACT.Silu)\
                       .then_inc(convs_ready, 1)
                for a in range(NT):
                    key = ("gt", s, a)
                    wait_full(act, key)
                    move(key, gate[s][:, a, :], psum(key, GV), ACT.Silu)
                act.wait_ge(gate_in, s + 1)
                act.activation(expo[s][:, :, :], expin[s][:, :, :], ACT.Exp).then_inc(gate_exp, 1)

            def delta_mid(_, s):
                for a in range(NT):
                    for i, (lo, hi) in enumerate(((0, 4), (4, GT))):
                        key = ("tm", s, a, i)
                        wait_full(act, key)
                        move(key, tokm[s][:, a, lo * P:hi * P], psum(key, (hi - lo) * P))
                key = ("gd", s)
                wait_full(act, key)
                move(key, gdec[s][:, :, :], psum(key, 2, GH), ACT.Exp)
                for q in range(GH // 2):
                    key = ("L", s, q)
                    wait_full(act, key)
                    if s and q == 0:
                        for i in range(GH // 2):
                            wait_full(act, ("dW", s - 1, LEVELS - 1, i))
                    move(key, EGs[:, 2 * q:2 * q + 2].rearrange("p h a i -> p (h a i)"), psum(key, BANK), ACT.Exp)
                for name, dst in (("K", KTt), ("Kb", KbT), ("Q", QTt)):
                    key = (name, s)
                    wait_full(act, key)
                    o = psum(key, 2, T)
                    n = step(act.activation(dst[s][:, 0, :], o[:, 0, :], ACT.Copy))
                    act.wait_ge(act_step, n)
                    move(key, dst[s][0:64, 1, :], o[0:64, 1, :])
                key = ("Qg", s)
                wait_full(act, key)
                o = psum(key, 2, P)
                n = step(act.activation(QgT[s][:, 0, :], o[:, 0, :], ACT.Copy))
                act.wait_ge(act_step, n)
                move(key, QgT[s][0:64, 1, :], o[0:64, 1, :])
                for q in range(GH // 2):
                    key = ("T0", s, q)
                    wait_full(act, key)
                    move(key, Tms[:, 2 * q:2 * q + 2].rearrange("p h a i -> p (h a i)"), psum(key, BANK))
                for l in range(1, LEVELS):
                    for q in range(GH // 2):
                        key = ("Y", s, l, q)
                        wait_full(act, key)
                        if l > 1:
                            wait_full(act, ("dW", s, l - 1, q))
                        move(key, Yms[:, 2 * q:2 * q + 2].rearrange("p h a i -> p (h a i)"), psum(key, BANK))
                key = ("U0", s)
                wait_full(act, key)
                move(key, U0s[s][:, :], psum(key, GV))
                key = ("Uk", s)
                wait_full(act, key)
                o = psum(key, 2, P)
                n = step(act.activation(Ukns[s][:, 0, :], o[:, 0, :], ACT.Copy, scale=-1.0))
                act.wait_ge(act_step, n)
                move(key, Ukns[s][0:64, 1, :], o[0:64, 1, :], scale=-1.0)
                key = ("S1", s)
                wait_full(act, key)
                o = psum(key, 2, DV)
                n = step(act.activation(S1s[s][:, 0, :], o[:, 0, :], ACT.Copy))
                act.wait_ge(act_step, n)
                move(key, S1s[s][0:64, 1, :], o[0:64, 1, :])
                for b in range(4):
                    key = ("U1", s, b)
                    wait_full(act, key)
                    n = 2 if b < 2 else 1
                    move(key, U1s[s].rearrange("p (h d) -> p h d", d=DV)[:, b:b + 4 * n - 3:4, :],
                         psum(key, n, DV))
                wait_full(act, ("O", s, 0))
                act.activation(osq[s][:, 0, :], psum(("O", s, 0), GV), ACT.Square).then_inc(osq_ready, 1)
                for b in range(4):
                    key = ("O1", s, b)
                    wait_full(act, key)
                    n = 2 if b < 2 else 1
                    act.activation(osq[s][:, 1, :].rearrange("p (h d) -> p h d", d=DV)[:, b:b + 4 * n - 3:4, :],
                                   psum(key, n, DV), ACT.Square).then_inc(osq_ready, 1)

            def delta_out(_, s):
                for i, n in enumerate((2, VT - 2)):
                    key = ("onT", s, i)
                    wait_full(act, key)
                    move(key, onT[s][:, 2 * i:2 * i + n, :], psum(key, n, T))

            def ffn(k, s):
                r = k * S + s
                for i in range(HT1 // 2):
                    key = ("h", r, i)
                    wait_full(act, key)
                    o = psum(key, 2, T)
                    b1 = w("f_b1")
                    n = step(act.activation(HT[s][:, 2 * i, :], o[:, 0, :], ACT.Gelu, bias=b1[:, 2 * i:2 * i + 1]))
                    act.wait_ge(act_step, n)
                    move(key, HT[s][:, 2 * i + 1, :], o[:, 1, :], ACT.Gelu, bias=b1[:, 2 * i + 1:2 * i + 2])

            table = dict(norm=norm, qkv_a=qkv_a, attend=attend, out_a=out_a, moe=moe, heads_in=heads_in,
                         heads=heads, delta_in=delta_in, delta_mid=delta_mid, delta_out=delta_out, ffn=ffn,
                         qkv_b=qkv_b, out_b=out_b)
            act.dma_start(raw, masks).then_inc(masks_loaded, 16)
            act.dma_start(pk[0][:, :], packs[0]).then_inc(loaded[0], 16)
            act.wait_ge(trig_in, 1)
            act.activation(cos_t[:, :, :].rearrange("p a i -> p (a i)"), trig[:, 1, :], ACT.Sin).then_inc(trig_out, 1)
            act.activation(sin_t[:, :, :].rearrange("p a i -> p (a i)"), trig[:, 0, :], ACT.Sin).then_inc(trig_out, 1)
            act.wait_ge(loaded[3], 16)
            act.activation(expA[:, :], w("c_alog"), ACT.Exp).then_inc(trig_out, 1)
            with act.Fori(0, B // S, 1) as it:
                count[0] = 0
                program(lambda name, k, s: table[name](k, s))
                next_turn(act, it)

        @block.vector
        def _(dve):
            count = [0]

            def step(ins):
                count[0] += 1
                ins.then_inc(dve_step, 1)

            def settle():
                dve.wait_ge(dve_step, count[0])

            def link(ins):
                step(ins)
                settle()

            def residual(key, s, n=NT * D):
                wait_full(dve, key)
                xf = X[s][:, :, :].rearrange("p a d -> p (a d)")
                dve.tensor_tensor(xf, psum(key, n), xf, ALU.add).then_inc(drain_of(key), 1)
                wait_drained(dve, key)

            def norm(k, s):
                if k == 0:
                    dve.wait_ge(x_loaded[s], 16)
                for a in range(NT):
                    step(dve.bn_stats(stat[s][:, a, :], X[s][:, a, :]))
                settle()
                for a in range(NT):
                    step(dve.bn_aggr(mv[s][:, a, :], stat[s][:, a, :]))
                settle()
                dve.tensor_scalar(veps[s][:, :], mv[s][:, :, 1], LN_EPS, None, ALU.add).then_inc(var_ready, 1)
                dve.wait_ge(rstd_ready, S * k + s + 1)
                for a in range(NT):
                    ins = dve.tensor_scalar(Xn[s][:, a, :], X[s][:, a, :], mv[s][:, a, 0:1],
                                            rstd[s][:, a:a + 1], ALU.subtract, ALU.mult)
                    if a < NT - 1:
                        link(ins)
                ins.then_inc(xn_ready, 1)

            def queries(k, s, name, scale):
                bq = w(name)
                for i in range(2):
                    key = ("q", k, s, i)
                    wait_full(dve, key)
                    o = psum(key, 2, T)
                    for j in range(2):
                        u = 2 * i + j
                        ins = dve.tensor_scalar(QT[s][:, u, :], o[:, j, :], bq[:, u:u + 1], scale, ALU.add, ALU.mult)
                        if j == 0:
                            link(ins)
                    ins.then_inc(drain_of(key), 1)

            def qkv_a(_, s):
                queries(0, s, "a_bq", 64 ** -0.5)
                for name, dst, bias in (("kT", kT, w("a_bk")), ("vT", vT, w("a_bv"))):
                    key = (name, s)
                    wait_full(dve, key)
                    o = psum(key, KD, T)
                    for c in range(KD):
                        ins = dve.tensor_scalar(dst[s][:, c, :], o[:, c, :], bias[:, c:c + 1], None, ALU.add)
                        if c == 0:
                            link(ins)
                    ins.then_inc(drain_of(key), 1)
                key = ("kp", 0, s)
                wait_full(dve, key)
                dve.tensor_copy(KpT[s][:, :], psum(key, T)).then_inc(drain_of(key), 1)
                key = ("vp", 0, s)
                wait_full(dve, key)
                dve.tensor_copy(Vp[s][:, :, :, 0:HD], psum(key, NT, NB, HD)).then_inc(drain_of(key), 1)

            def qkv_b(_, s):
                queries(1, s, "d_bq", HD ** -0.5)
                key = ("kp", 1, s)
                wait_full(dve, key)
                dve.tensor_scalar(KpT[s][:, :], psum(key, T), w("d_bk"), None, ALU.add).then_inc(drain_of(key), 1)
                key = ("vp", 1, s)
                wait_full(dve, key)
                o = psum(key, NT, HD)
                for j in range(NB):
                    ins = dve.tensor_copy(Vp[s][:, :, j, 0:HD], o)
                    if j < NB - 1:
                        link(ins)
                ins.then_inc(drain_of(key), 1)

            def attend(k, _):
                def maxes(g):
                    for j in range(NB):
                        key = ("sc", k, g, j)
                        wait_full(dve, key)
                        if g >= PR:
                            wait_drained(dve, ("sc", k, g - PR, j))
                        o = psum(key, 3 * P)
                        link(dve.tensor_reduce(negmax[:, g % PR, j, 1:2], o[:, 0:T], AX.X, ALU.max, negate=True))
                        dve.tensor_reduce(negmax[:, g % PR, j, 0:1], o[:, T:T + P], AX.X, ALU.max, negate=True)\
                           .then_inc(max_ready, 1)

                def finish(g):
                    s, u = divmod(g, NU)
                    for j in range(NB):
                        key = ("pT", k, g, j)
                        wait_full(dve, key)
                        if g >= PR and j == 0:
                            wait_full(dve, ("pv", k, g - PR))
                        dve.tensor_copy(probT[:, g % PR, j, :], psum(key, 3 * P)).then_inc(drain_of(key), 1)

                def contexts(g):
                    s, u = divmod(g, NU)
                    key = ("pv", k, g)
                    wait_full(dve, key)
                    o = psum(key, NT, NB, PW)
                    link(dve.reciprocal(rsum[:, g % PR], o[:, :, :, HD]))
                    c = ctxn[s][:, :, :].rearrange("p a (j u d) -> p a j u d", j=NB, u=NU)
                    dve.tensor_tensor(c[:, :, :, u, :], o[:, :, :, 0:HD], bcast(rsum[:, g % PR], HD), ALU.mult)\
                       .then_inc(drain_of(key), 1)
                    if u == NU - 1:
                        wait_drained(dve, key)
                        for v in range(NU):
                            wait_drained(dve, ("pv", k, s * NU + v))
                        dve.sem_inc(ctx_ready, 1)

                maxes(0)
                for g in range(S * NU):
                    if g + 1 < S * NU:
                        maxes(g + 1)
                    finish(g)
                    contexts(g)

            def out_a(_, s):
                residual(("y", 0, s), s)

            def out_b(_, s):
                residual(("y", 1, s), s)

            def moe(k, s):
                r = k * S + s
                key = ("lg", r)
                wait_full(dve, key)
                dve.tensor_copy(lg[s][:, :, :], psum(key, NT, E)).then_inc(drain_of(key), 1)
                wait_drained(dve, key)
                for a in range(NT):
                    step(dve.max(top[s][:, a, :], lg[s][:, a, :]))
                settle()
                dve.tensor_tensor(rw[s][:, 3, :], top[s][:, :, 1], top[s][:, :, 0], ALU.subtract)\
                   .then_inc(top_diff, 1)
                for a in range(NT):
                    step(dve.max_index(topi[s][:, a, :], top[s][:, a, :], lg[s][:, a, :]))
                settle()
                link(dve.tensor_copy(topf[s][:, :, :], topi[s][:, :, :]))
                iota = w("iota")
                for a in range(NT):
                    for i in range(TOPK):
                        ins = dve.tensor_scalar(onehot[s][:, a, i, :], iota, topf[s][:, a, i:i + 1], None,
                                                ALU.is_equal)
                        if a * TOPK + i < NT * TOPK - 1:
                            link(ins)
                ins.then_inc(onehot_ready, 1)
                dve.wait_ge(top_exp, r + 1)
                link(dve.tensor_scalar(rw[s][:, 3, :], rw[s][:, 2, :], 1.0, None, ALU.add))
                link(dve.reciprocal(rw[s][:, 0, :], rw[s][:, 3, :]))
                link(dve.tensor_tensor(rw[s][:, 1, :], rw[s][:, 2, :], rw[s][:, 0, :], ALU.mult))
                for a in range(NT):
                    for i in range(TOPK):
                        step(dve.tensor_scalar(onehotw[s][:, a, i, :], iota, topf[s][:, a, i:i + 1],
                                               rw[s][:, i, a:a + 1], ALU.is_equal, ALU.mult))
                settle()
                for i in range(2):
                    wait_drained(dve, ("aT", r, i))
                for i in range(2):
                    key = ("ex", r, i)
                    wait_full(dve, key)
                    for j in range(2):
                        dve.tensor_tensor(amT[s][:, i, 2 * j:2 * j + 2, :], aT[s][:, 2 * j:2 * j + 2, :],
                                          psum(key, KER, T), ALU.mult).then_inc(am_ready, 1)
                    dve.wait_ge(am_ready, 4 * r + 2 * i + 2)
                    dve.sem_inc(drain_of(key), 1)
                for i in range(TOPK):
                    for m in range(FT):
                        key = ("x", r, m)
                        n = (r * TOPK + i) * FT + m
                        dve.wait_ge(silu_ready, n + 1)
                        ins = dve.tensor_tensor(x2T[s][:, i, m, :], psum(key, 2, T)[:, 1, :],
                                                silu_x[s][:, (i * FT + m) % 2, :], ALU.mult)
                        ins.then_inc(x2_first if i == 0 else drain_of(key), 1)
                for i in range(TOPK):
                    for a in range(NT):
                        key = ("down", r, i, a)
                        wait_full(dve, key)
                        o = psum(key, 2, D)
                        link(dve.scalar_tensor_tensor(out=X[s][:, a, :], in0=o[:, 0, :],
                                                      scalar=rw[s][:, i, a:a + 1], in1=X[s][:, a, :],
                                                      op0=ALU.mult, op1=ALU.add))
                        dst = am2 if i == 0 else am2b
                        dve.tensor_tensor(dst[s][:, a].rearrange("p (e r) -> p e r", e=E),
                                          o[:, 1, :].rearrange("p (e r) -> p e r", e=E),
                                          bcast(onehotw[s][:, a, i, :], R), ALU.mult).then_inc(drain_of(key), 1)
                        wait_drained(dve, key)
                dve.tensor_tensor(am2[s][:, :, :], am2[s][:, :, :], am2b[s][:, :, :], ALU.add)\
                   .then_inc(am2_ready, 1)
                residual(("lora2", r), s)

            def heads_in(_, s):
                for a in range(NT):
                    key = ("bqk", s, a)
                    wait_full(dve, key)
                    o = psum(key, 2 * NH, 8, 2)
                    for i, tab in enumerate((cos_t, sin_t)):
                        for j in range(2):
                            t = rtmp[s][:, i, :, :].rearrange("p h (j d) -> p h j d", j=2)
                            ins = dve.tensor_tensor(t[:, :, j, :], o[:, :, :, j],
                                                    tab[:, a, :].unsqueeze(1).broadcast_to([P, 2 * NH, 8]), ALU.mult)
                            if i * 2 + j < 3:
                                link(ins)
                    ins.then_inc(drain_of(key), 1)
                    wait_drained(dve, key)
                    c, q = rtmp[s][:, 0], rtmp[s][:, 1]
                    step(dve.tensor_tensor(rot[s][:, a, :, 0:8], c[:, :, 0:8], q[:, :, 8:16], ALU.subtract))
                    step(dve.tensor_tensor(rot[s][:, a, :, 8:16], q[:, :, 0:8], c[:, :, 8:16], ALU.add))
                    settle()

            def heads(_, s):
                wait_drained(dve, ("bv", s))
                for a in range(NT):
                    q = rot[s][:, a, 0:NH, :].unsqueeze(2).broadcast_to([P, NH, NH, HD])
                    kk = rot[s][:, a, NH:2 * NH, :].unsqueeze(1).broadcast_to([P, NH, NH, HD])
                    link(dve.tensor_tensor(prod[s][:, :, :, :], q, kk, ALU.mult))
                    link(dve.tensor_reduce(sc[s][:, a], prod[s][:, :, :, :], AX.X, ALU.add))
                    link(dve.tensor_reduce(bmax[s][:, a], sc[s][:, a], AX.X, ALU.max))
                    dve.tensor_tensor(sc[s][:, a], sc[s][:, a], bcast(bmax[s][:, a], NH), ALU.subtract)\
                       .then_inc(b_in, 1)
                for a in range(NT):
                    dve.wait_ge(b_exp, s * NT + a + 1)
                    link(dve.tensor_reduce(bsum[s][:, a], pw[s][:, a], AX.X, ALU.add))
                    link(dve.reciprocal(bmax[s][:, a], bsum[s][:, a]))
                    pp = pw[s][:, a].unsqueeze(2).broadcast_to([P, NH, HD, NH])
                    vv = bV[s][:, a].rearrange("p t d -> p d t").unsqueeze(1).broadcast_to([P, NH, HD, NH])
                    link(dve.tensor_tensor(prod[s][:, :, :, :], pp, vv, ALU.mult))
                    c = ctxn[s][:, a, :].rearrange("p (h d) -> p h d", h=NH)
                    link(dve.tensor_reduce(c, prod[s][:, :, :, :], AX.X, ALU.add))
                    ins = dve.tensor_tensor(c, c, bcast(bmax[s][:, a], HD), ALU.mult)
                    if a < NT - 1:
                        link(ins)
                ins.then_inc(bctx_ready, 1)
                residual(("by", s), s)

            def delta_in(_, s):
                key = ("ba", s)
                wait_full(dve, key)
                o = psum(key, NT, 2, GH)
                sm = small[s]
                link(dve.tensor_scalar(expin[s][:, :, 0:GH], o[:, :, 0, :], -1.0, None, ALU.mult))
                dve.tensor_tensor(sm[:, 0], o[:, :, 1, :], w("c_dt").unsqueeze(1).broadcast_to([P, NT, GH]),
                                  ALU.add).then_inc(drain_of(key), 1)
                wait_drained(dve, key)
                dve.scalar_tensor_tensor(out=expin[s][:, :, GH:2 * GH], in0=sm[:, 0], scalar=-1.0, in1=sm[:, 0],
                                         op0=ALU.mult, op1=ALU.min).then_inc(gate_in, 1)
                cw = w("c_conv").rearrange("p (t j) -> p t j", t=GT)
                for i in range(GT // 2):
                    key = ("cv", s, i)
                    wait_full(dve, key)
                    o = psum(key, 2, T)
                    for j in range(2):
                        t = 2 * i + j
                        link(dve.tensor_scalar(convT[s][:, t, :], o[:, j, :], cw[:, t, CONV - 1:CONV], None, ALU.mult))
                        for d in range(1, CONV):
                            ins = dve.scalar_tensor_tensor(
                                out=convT[s][:, t, d:T], in0=o[:, j, 0:T - d],
                                scalar=cw[:, t, CONV - 1 - d:CONV - d], in1=convT[s][:, t, d:T],
                                op0=ALU.mult, op1=ALU.add)
                            if d == CONV - 1 and j == 1:
                                ins.then_inc(conv_ready, 1)
                                dve.wait_ge(conv_ready, s * (GT // 2) + i + 1)
                                dve.sem_inc(drain_of(key), 1)
                            else:
                                link(ins)
                dve.wait_ge(gate_exp, s + 1)
                eb, u = expo[s][:, :, 0:GH], expo[s][:, :, GH:2 * GH]
                link(dve.tensor_scalar(sm[:, 1], eb, 1.0, None, ALU.add))
                link(dve.reciprocal(sm[:, 2], sm[:, 1]))
                link(dve.tensor_scalar(sm[:, 3], u, 2.0, None, ALU.add))
                link(dve.reciprocal(sm[:, 4], sm[:, 3]))
                link(dve.tensor_tensor(sm[:, 3], u, sm[:, 4], ALU.mult))
                link(dve.tensor_tensor(sm[:, 4], sm[:, 3], sm[:, 3], ALU.mult))
                link(dve.tensor_scalar(sm[:, 5], sm[:, 4], 1.0 / (2 * SERIES - 1), None, ALU.mult))
                for n in range(SERIES - 2, 0, -1):
                    link(dve.scalar_tensor_tensor(out=sm[:, 5], in0=sm[:, 5], scalar=1.0 / (2 * n + 1),
                                                  in1=sm[:, 4], op0=ALU.add, op1=ALU.mult))
                link(dve.scalar_tensor_tensor(out=sm[:, 6], in0=sm[:, 5], scalar=1.0, in1=sm[:, 3],
                                              op0=ALU.add, op1=ALU.mult))
                link(dve.tensor_scalar(sm[:, 7], sm[:, 0], 0.0, None, ALU.max))
                link(dve.scalar_tensor_tensor(out=sm[:, 8], in0=sm[:, 6], scalar=2.0, in1=sm[:, 7],
                                              op0=ALU.mult, op1=ALU.add))
                link(dve.scalar_tensor_tensor(out=sm[:, 7], in0=sm[:, 8], scalar=-1.0,
                                              in1=expA[:, :].unsqueeze(1).broadcast_to([P, NT, GH]),
                                              op0=ALU.mult, op1=ALU.mult))
                dve.tensor_scalar(sm[:, 9], sm[:, 7], G_MIN, None, ALU.max).then_inc(g_ready, 1)

            def delta_mid(_, s):
                sm = small[s]
                for a in range(NT):
                    for i in range(2):
                        wait_drained(dve, ("tm", s, a, i))
                sq = sqs[s]
                link(dve.tensor_tensor(sq, tokm[s][:, :, 0:GQK], tokm[s][:, :, 0:GQK], ALU.mult))
                link(dve.tensor_reduce(ss[s][:, :, :].rearrange("p a h -> p (a h)"),
                                       sq.rearrange("p a (h d) -> p (a h) d", d=DK), AX.X, ALU.add))
                dve.tensor_scalar(ss[s][:, :, :], ss[s][:, :, :], L2_EPS, None, ALU.add).then_inc(sq_ready, 1)
                dve.wait_ge(rn_ready, s + 1)
                link(dve.tensor_scalar(fac[s][:, :, 0:GH], fac[s][:, :, 0:GH], DK ** -0.5, None, ALU.mult))
                tq = tokm[s][:, :, 0:GQK].rearrange("p a (h d) -> p a h d", d=DK)
                for a in range(NT):
                    step(dve.tensor_tensor(tq[:, a], tq[:, a], bcast(fac[s][:, a, :], DK), ALU.mult))
                settle()
                for a in range(NT):
                    ins = dve.tensor_tensor(kb[s][:, a, :].rearrange("p (h d) -> p h d", d=DK), tq[:, a, GH:2 * GH],
                                            bcast(sm[:, 2, a, :], DK), ALU.mult)
                    if a < NT - 1:
                        link(ins)
                ins.then_inc(qk_ready, 1)
                dve.wait_ge(qk_ready, s + 1)
                wait_drained(dve, ("gd", s))
                g0, gc = gdec[s][:, 0, :], gdec[s][:, 1, :]
                hd = "p (h d) -> p h d"
                link(dve.tensor_tensor(kd[s].rearrange(hd, d=DK), tq[:, 0, GH:2 * GH], bcast(gc, DK), ALU.mult))
                link(dve.tensor_tensor(kbg[s].rearrange(hd, d=DK), kb[s][:, 1, :].rearrange(hd, d=DK),
                                       bcast(g0, DK), ALU.mult))
                dve.tensor_tensor(qg[s].rearrange(hd, d=DK), tq[:, 1, 0:GH], bcast(g0, DK), ALU.mult)\
                   .then_inc(kdec_ready, 1)
                for q in range(GH // 2):
                    wait_drained(dve, ("L", s, q))
                dve.wait_ge(kdec_ready, s + 1)
                dve.wait_ge(bv_ready, s + 1)
                for name, dst in (("A", ATs[s]), ("PT", PT[s])):
                    for b in range(4):
                        key = (name, s, b)
                        wait_full(dve, key)
                        n = 2 if b < 2 else 1
                        o = psum(key, n, NT * P)
                        sl = slice(b, b + 4 * (n - 1) + 1, 4)
                        dve.tensor_tensor(dst[:, sl].rearrange("p h a i -> p h (a i)"), o,
                                          EGs[:, sl].rearrange("p h a i -> p h (a i)"), ALU.mult)\
                           .then_inc(drain_of(key), 1)
                for name in ("A", "PT"):
                    for b in range(4):
                        wait_drained(dve, (name, s, b))
                dve.sem_inc(at_ready, 1)
                dve.wait_ge(am_mask, s * LEVELS + 1)
                if s:
                    for b in range(4):
                        wait_full(dve, ("U1", s - 1, b))
                flat = "p h a i -> p (h a) i"
                dve.tensor_tensor(Wms[:, :, :, :].rearrange(flat),
                                  ident.unsqueeze(1).broadcast_to([P, GH * NT, P]),
                                  Ams[:, :, :, :].rearrange(flat), ALU.subtract).then_inc(w_ready, 1)
                dve.wait_ge(w_ready, s + 1)
                for l in range(1, LEVELS):
                    for q in range(GH // 2):
                        for name, dst in (("dT", Tms), ("dW", Wms)):
                            if name == "dT" and l == LEVELS - 1:
                                continue
                            key = (name, s, l, q)
                            wait_full(dve, key)
                            if name == "dT":
                                wait_drained(dve, ("T0", s, q) if l == 1 else ("dT", s, l - 1, q))
                            if name == "dW" and l > 1:
                                wait_drained(dve, ("dW", s, l - 1, q))
                            v = dst[:, 2 * q:2 * q + 2].rearrange("p h a i -> p (h a i)")
                            dve.tensor_tensor(v, v, psum(key, BANK), ALU.subtract).then_inc(drain_of(key), 1)
                dve.wait_ge(osq_ready, 5 * (s + 1))
                link(dve.tensor_reduce(rv[s][:, :, :].rearrange("p a h -> p (a h)"),
                                       osq[s][:, :, :].rearrange("p a (h d) -> p (a h) d", d=DV), AX.X, ALU.add))
                dve.tensor_scalar(rr[s][:, :, :], rv[s][:, :, :], 1.0 / DV, RMS_EPS, ALU.mult, ALU.add)\
                   .then_inc(orms_in, 1)
                dve.wait_ge(orms, s + 1)
                key = ("O", s, 0)
                dve.tensor_tensor(on[s][:, 0, :].rearrange("p (h d) -> p h d", d=DV), psum(key, GH, DV),
                                  bcast(rv[s][:, 0, :], DV), ALU.mult).then_inc(drain_of(key), 1)
                for b in range(4):
                    key = ("O1", s, b)
                    n = 2 if b < 2 else 1
                    dve.tensor_tensor(on[s][:, 1, :].rearrange("p (h d) -> p h d", d=DV)[:, b:b + 4 * n - 3:4, :],
                                      psum(key, n, DV), bcast(rv[s][:, 1, b:b + 4 * n - 3:4], DV), ALU.mult)\
                       .then_inc(drain_of(key), 1)
                wait_drained(dve, ("O", s, 0))
                for b in range(4):
                    wait_drained(dve, ("O1", s, b))
                dve.wait_ge(gn_ready, s + 1)
                dve.tensor_tensor(on[s][:, :, :], on[s][:, :, :], gate[s][:, :, :], ALU.mult).then_inc(on_ready, 1)

            def delta_out(_, s):
                residual(("cy", s), s)

            def ffn(k, s):
                key = ("fy", k * S + s)
                residual(key, s)
                if k == 1:
                    dve.sem_inc(x_final, 1)

            table = dict(norm=norm, qkv_a=qkv_a, attend=attend, out_a=out_a, moe=moe, heads_in=heads_in,
                         heads=heads, delta_in=delta_in, delta_mid=delta_mid, delta_out=delta_out, ffn=ffn,
                         qkv_b=qkv_b, out_b=out_b)
            dve.memset(Vp[0][:, :, :, HD:PW], 1.0).then_inc(prep, 1)
            dve.memset(Vp[1][:, :, :, HD:PW], 1.0).then_inc(prep, 1)
            dve.wait_ge(loaded[0], 16)
            dve.wait_ge(masks_loaded, 16)
            dve.tensor_copy(identb[:, :], ident).then_inc(const_ready, 1)
            dve.tensor_copy(negb[:, :], raw[:, 0:P]).then_inc(const_ready, 1)
            dve.tensor_copy(levb[:, :, :], raw[:, 2 * P:].rearrange("p (l i) -> p l i", l=LEVELS)).then_inc(const_ready, 1)
            dve.tensor_copy(neg4b[:, :, :], raw[:, P:2 * P].unsqueeze(1).broadcast_to([P, 4, P])).then_inc(const_ready, 1)
            n_prep = [2]

            def plink(ins):
                n_prep[0] += 1
                ins.then_inc(prep, 1)
                dve.wait_ge(prep, n_prep[0])

            PI2 = 6.283185307179586
            C1 = 6.28125
            C2 = 0.0019340515136718750
            C3 = PI2 - C1 - C2
            MAGIC = 12582912.0
            for a in range(NT):
                plink(dve.tensor_scalar(trig[:, 2, a * 8:(a + 1) * 8], w("inv_freq"), w("tok")[:, a:a + 1], None,
                                        ALU.mult))
            for i, (quarter, shift) in enumerate(((0.0, 0.0), (0.25, PI2 / 4))):
                plink(dve.tensor_scalar(trig[:, 3, :], trig[:, 2, :], 1.0 / PI2, quarter, ALU.mult, ALU.add))
                plink(dve.tensor_scalar(trig[:, 3, :], trig[:, 3, :], MAGIC, None, ALU.add))
                plink(dve.tensor_scalar(trig[:, 3, :], trig[:, 3, :], MAGIC, None, ALU.subtract))
                plink(dve.scalar_tensor_tensor(out=trig[:, i, :], in0=trig[:, 3, :], scalar=-C1, in1=trig[:, 2, :],
                                               op0=ALU.mult, op1=ALU.add))
                plink(dve.scalar_tensor_tensor(out=trig[:, i, :], in0=trig[:, 3, :], scalar=-C2, in1=trig[:, i, :],
                                               op0=ALU.mult, op1=ALU.add))
                plink(dve.scalar_tensor_tensor(out=trig[:, i, :], in0=trig[:, 3, :], scalar=-C3, in1=trig[:, i, :],
                                               op0=ALU.mult, op1=ALU.add))
                plink(dve.tensor_scalar(trig[:, i, :], trig[:, i, :], shift, 3.1415925, ALU.add, ALU.min))
                ins = dve.tensor_scalar(trig[:, i, :], trig[:, i, :], -3.1415925, None, ALU.max)
                if i == 0:
                    plink(ins)
            ins.then_inc(trig_in, 1)
            dve.wait_ge(trig_out, 3)
            with dve.Fori(0, B // S, 1) as it:
                count[0] = 0
                program(lambda name, k, s: table[name](k, s))
                next_turn(dve, it)

        @block.gpsimd
        def _(pool):
            def power(dst, src, shape):
                return pool.tensor_tensor(dst, src, half[:, 0:1].broadcast_to(shape) if len(shape) == 2 else
                                          half[:, 0:1].unsqueeze(1).broadcast_to(shape), ALU.pow)

            def nothing(k, s):
                pass

            def norm(k, s):
                pool.wait_ge(var_ready, S * k + s + 1)
                power(rstd[s][:, :], veps[s][:, :], [P, NT]).then_inc(rstd_ready, 1)

            def delta_in(_, s):
                for a in range(NT):
                    wait_drained(pool, ("gt", s, a))
                pool.tensor_tensor(gate[s][:, :, :].rearrange("p a (h d) -> p (a h) d", d=DV),
                                   gate[s][:, :, :].rearrange("p a (h d) -> p (a h) d", d=DV),
                                   w("c_norm").unsqueeze(1).broadcast_to([P, NT * GH, DV]), ALU.mult)\
                    .then_inc(gn_ready, 1)

            def delta_mid(_, s):
                pool.wait_ge(g_ready, s + 1)
                if s:
                    for q in range(GH // 2):
                        wait_full(pool, ("dW", s - 1, LEVELS - 1, q))
                gl = small[s][:, 9].rearrange("p a h -> p h a")
                for a in range(NT):
                    ins = pool.tensor_tensor(G1s[:, :, a, :], w("low_strict").unsqueeze(1).broadcast_to([P, GH, P]),
                                             bcast(small[s][:, 9, a, :], P), ALU.mult)
                    if a < NT - 1:
                        ins.then_inc(pool_step, 1)
                        pool.wait_ge(pool_step, s + 1)
                ins.then_inc(g1_ready, 1)
                pool.wait_ge(sq_ready, s + 1)
                power(fac[s][:, :, :].rearrange("p a h -> p (a h)"), ss[s][:, :, :].rearrange("p a h -> p (a h)"),
                      [P, NT * 2 * GH]).then_inc(rn_ready, 1)
                for a in range(NT):
                    wait_drained(pool, ("tm", s, a, 1))
                for a in range(NT):
                    ins = pool.tensor_tensor(bv[s][:, a, :].rearrange("p (h d) -> p h d", d=DV),
                                             tokm[s][:, a, GQK:GALL].rearrange("p (h d) -> p h d", d=DV),
                                             bcast(small[s][:, 2, a, :], DV), ALU.mult)
                    if a < NT - 1:
                        ins.then_inc(pool_step, 1)
                ins.then_inc(bv_ready, 1)
                pool.wait_ge(at_ready, s + 1)
                lv = levb
                for l in range(LEVELS):
                    if l >= 2:
                        for q in range(GH // 2):
                            wait_full(pool, ("Y", s, l - 1, q))
                    elif l == 1:
                        pool.wait_ge(w_ready, s + 1)
                    pool.tensor_tensor(Ams[:, :, :, :].rearrange("p h a i -> p (h a) i"),
                                       ATs[s][:, :, :, :].rearrange("p h a i -> p (h a) i"),
                                       lv[:, l, :].unsqueeze(1).broadcast_to([P, GH * NT, P]), ALU.mult)\
                        .then_inc(am_mask, 1)
                pool.wait_ge(orms_in, s + 1)
                power(rv[s][:, :, :].rearrange("p a h -> p (a h)"), rr[s][:, :, :].rearrange("p a h -> p (a h)"),
                      [P, NT * GH]).then_inc(orms, 1)

            table = dict(norm=norm, qkv_a=nothing, attend=nothing, out_a=nothing, moe=nothing, heads_in=nothing,
                         heads=nothing, delta_in=delta_in, delta_mid=delta_mid, delta_out=nothing, ffn=nothing,
                         qkv_b=nothing, out_b=nothing)
            pool.memset(half[:, :], -0.5).then_inc(prep_pool, 1)
            pool.wait_ge(prep_pool, 1)
            pool.wait_ge(loaded[0], 16)
            pool.wait_ge(loaded[3], 16)
            pool.wait_ge(const_ready, 4)
            with pool.Fori(0, B // S, 1) as it:
                program(lambda name, k, s: table[name](k, s))
                next_turn(pool, it)


def lay_out(inp):
    import numpy as np

    a = {k: np.asarray(v) for k, v in inp.items()}
    f = np.float32

    def kt(m):
        m = np.asarray(m)
        return m.reshape(m.shape[0] // P, P, m.shape[1]).transpose(1, 0, 2).reshape(P, -1)

    def col(v):
        return np.asarray(v).reshape(-1, P).T

    def rows(v):
        return np.broadcast_to(np.asarray(v).reshape(1, -1), (P, np.asarray(v).size))

    def heads32(m):
        o = np.zeros((m.shape[0], NU, NB, 32), f)
        o[:, :, :, 0:HD] = m.reshape(m.shape[0], NB, NU, HD).transpose(0, 2, 1, 3)
        return o.reshape(m.shape[0], NU * P)

    i, j = np.arange(P)[:, None], np.arange(P)[None, :]
    kfold = np.zeros((NB, 64, NB, 32), f)
    vfold = np.zeros((NB, 64, NB, HD), f)
    for g in range(NB):
        kfold[g, :, g, 0:HD] = a["L0_attn_a_Wq2kv"].T
        vfold[g, :, g, :] = a["L0_attn_a_Wkv2h"]
    spread = np.zeros((2 * E, 2, E, R), f)
    for e in range(E):
        spread[e, 0, e] = 1.0
        spread[E + e, 1, e] = 1.0
        spread[e, 1, e] = -1.0
    spread_rows = np.zeros((P, 2 * ER), f)
    spread_rows[0:2 * E] = spread.reshape(2 * E, 2 * ER)
    spread_rows[32, 0:D] = a["L0_attn_a_bo"]
    spread_rows[32, D:D + HD] = a["L1_attn_b_Wqkv_b"][D + HD:]
    spread_rows[64, 0:D] = a["L1_attn_b_out_b"]
    spread_rows[96, 0:D] = a["L1_ffn_proj2_bias"]
    levels = np.zeros((P, LEVELS, P), f)
    for l in range(LEVELS):
        b = 1 << l
        levels[:, l] = ((i // (2 * b) == j // (2 * b)) & (i // b != j // b) & (i < j))
    qkvw, qkvb = a["L1_attn_b_Wqkv_w"], a["L1_attn_b_Wqkv_b"]
    kw = np.zeros((D, NB, 32), f)
    kw[:, :, 0:HD] = qkvw[D:D + HD].T[:, None, :]
    kbias = np.zeros((1, NB, 32), f)
    kbias[:, :, 0:HD] = qkvb[None, None, D:D + HD]
    conv = np.concatenate([a["L1_attn_a_conv_wq"], a["L1_attn_a_conv_wk"], a["L1_attn_a_conv_wv"]], 0)
    groups = [
        dict(ident=(i == j).astype(f), 
             tri_up=(i <= j).astype(f), low_strict=(i > j).astype(f), ones=np.ones((P, P), f),
             iota=rows(np.arange(E, dtype=f)),
             inv_freq=rows(a["L0_attn_b_inv_freq"]), tok=np.arange(T, dtype=f).reshape(NT, P).T,
             a_wl=kt(a["L0_attn_a_Wl"]), a_bl=col(a["L0_attn_a_bl"]), a_wq=kt(heads32(a["L0_attn_a_Wq"])),
             a_bq=col(heads32(a["L0_attn_a_bq"][None])), a_wk=a["L0_attn_a_Wk"], a_bk=col(a["L0_attn_a_bk"]),
             a_wv=a["L0_attn_a_Wv"], a_bv=col(a["L0_attn_a_bv"]), a_kfold=kt(kfold.reshape(D, P)),
             a_vfold=kt(vfold.reshape(D, 64)), a_b2=np.tile(a["L0_attn_a_bkv2h"], P // HD).reshape(P, 1),
             a_wo=kt(a["L0_attn_a_Wo"])),
        dict(m_g=kt(a["L0_ffn_Wg"].T),
             m_a=kt(np.concatenate([a["L0_ffn_A1"].reshape(ER, D), a["L0_ffn_A3"].reshape(ER, D)], 0).T),
             m_spread=spread_rows, m_w1=kt(a["L0_ffn_W1"].T), m_w3=kt(a["L0_ffn_W3"].T),
             m_b1=kt(a["L0_ffn_B1"].transpose(0, 2, 1).reshape(ER, F)),
             m_b3=kt(a["L0_ffn_B3"].transpose(0, 2, 1).reshape(ER, F)),
             m_down=kt(np.concatenate([a["L0_ffn_W2"].T, a["L0_ffn_A2"].reshape(ER, F).T], 1)),
             m_b2=kt(a["L0_ffn_B2"].transpose(0, 2, 1).reshape(ER, D))),
        dict(b_wqkv=kt(np.concatenate([a["L0_attn_b_wq"], a["L0_attn_b_wk"], a["L0_attn_b_wv"]], 0).T),
             b_wo=kt(a["L0_attn_b_wo"].T)),
        dict(c_alog=rows(a["L1_attn_a_A_log"]), c_dt=rows(a["L1_attn_a_dt_bias"]), c_norm=rows(a["L1_attn_a_norm_w"]),
             c_conv=conv.reshape(GT, P, CONV).transpose(1, 0, 2).reshape(P, -1),
             c_wqkv=kt(np.concatenate([a["L1_attn_a_Wq"], a["L1_attn_a_Wk"], a["L1_attn_a_Wv"]], 0).T),
             c_wba=kt(np.concatenate([a["L1_attn_a_Wb"], a["L1_attn_a_Wa"]], 0).T),
             c_wg=kt(a["L1_attn_a_Wg"].T), c_wo=kt(a["L1_attn_a_Wo"].T)),
        dict(d_wq=kt(heads32(qkvw[0:D].T)), d_bq=col(heads32(qkvb[None, 0:D])), d_wk=kt(kw.reshape(D, P)),
             d_bk=kbias.reshape(P, 1), d_wv=kt(qkvw[D + HD:].T), d_wo=kt(a["L1_attn_b_out_w"].T)),
        dict(f_w1=kt(a["L1_ffn_proj1"].T), f_b1=col(a["L1_ffn_proj1_bias"]), f_w2=kt(a["L1_ffn_proj2"].T)),
    ]
    packs, where = [], {}
    for g, parts in enumerate(groups):
        off, cols = 0, []
        for name, m in parts.items():
            m = np.asarray(m)
            full = np.zeros((P, m.shape[1]), f)
            full[:m.shape[0]] = m
            where[name] = (g, off, m.shape[1], m.shape[0])
            off += m.shape[1]
            cols.append(full)
        packs.append(np.ascontiguousarray(np.concatenate(cols, 1)))
    masks = np.concatenate([np.where(j > i, f(NEG), f(0)), np.where(j < i, f(NEG), f(0)), levels.reshape(P, -1)], 1)
    return np.ascontiguousarray(masks), packs, where


def kernel(**inputs):
    import numpy as _np
    import concourse.bacc as _bacc
    from concourse.bass_utils import run_bass_kernel_spmd as _run

    nc = _bacc.Bacc("TRN2", target_bir_lowering=False, num_devices=1)
    masks, packs, where = lay_out(inputs)
    arrays = {"x": _np.ascontiguousarray(inputs["L0_attn_a_x"]), "masks": masks}
    for g, p in enumerate(packs):
        arrays[f"pack{g}_dram"] = p
    args = {n: nc.dram_tensor(n, v.shape, mybir.dt.from_np(v.dtype), kind="ExternalInput").ap()
            for n, v in arrays.items()}
    out = nc.dram_tensor("out_dram", (B, T, D), F32, kind="ExternalOutput").ap()
    hybrid_kernel(nc, args["x"], args["masks"], [args[f"pack{g}_dram"] for g in range(len(packs))], where, out)
    r = _run(nc, [arrays], core_ids=[0])
    return r.results[0]["out_dram"]
```

```python
from contextlib import ExitStack

import concourse.bass as bass
from concourse import mybir

F32 = mybir.dt.float32
BF16 = mybir.dt.bfloat16
U32 = mybir.dt.uint32
ALU = mybir.AluOpType
ACT = mybir.ActivationFunctionType
AX = mybir.AxisListType

P = 128
B, T, D = 4, 256, 256
S = 2
NT = T // P
KD = D // P
BANKS, BANK = 8, 512
NEG = -1.0e30

NH, HD = 16, 16
NB = 4
NU = NH // NB
QG = P // HD
QTL = NH // QG
SCB = 3
PW = HD + 1

F, E, R, TOPK = 896, 8, 32, 2
FT = F // P
ER = E * R
KER = ER // P

GH, DK, DV, CONV = 6, 32, 64, 4
GQK = 2 * GH * DK
GV = GH * DV
GALL = GQK + GV
GT = GALL // P
VT = GV // P
LEVELS = 7
G_MIN = -200.0
SERIES = 8

H1 = 1024
HT1 = H1 // P

LN_EPS, L2_EPS, RMS_EPS = 1e-5, 1e-6, 1e-5


class Ring:

    def __init__(self):
        self.n = 0
        self.fills = [0] * BANKS
        self.uses = [0] * BANKS
        self.at = {}

    def claim(self, key, fills=1):
        b = self.n % BANKS
        self.n += 1
        before = self.uses[b]
        self.uses[b] += 1
        self.at[key] = (b, self.fills[b], before + 1)
        self.fills[b] += fills
        return b, before

    def bank(self, key):
        return self.at[key][0]

    def filled(self, key, fill=1):
        return self.at[key][1] + fill

    def drained(self, key):
        return self.at[key][2]


def hybrid_kernel(nc, x_in, masks, packs, where, out):
    with ExitStack() as ctx:
        def sb(name, shape, dt=F32):
            return ctx.enter_context(nc.sbuf_tensor(name, shape, dt))

        def sem(name):
            return ctx.enter_context(nc.semaphore(name))

        GROUPS = [p.shape[1] for p in packs]
        pk = [sb(f"pack{g}", [P, n]) for g, n in enumerate(GROUPS)]

        def w(name, rows=P):
            g, off, n, _ = where[name]
            return pk[g][0:rows, off:off + n]

        def w3(name, k):
            return w(name).rearrange("p (k n) -> p k n", k=k)

        ident = w("ident")
        levb = sb("levb", [P, LEVELS, P], BF16)
        identb = sb("identb", [P, P], BF16)
        negb = sb("negb", [P, P], BF16)
        neg4b = sb("neg4b", [P, 4, P], BF16)
        BROW = dict(a_bo=(32, 0, D), d_bv=(32, D, HD), d_bo=(64, 0, D), f_b2=(96, 0, D))

        def bias_row(name):
            r0, off, n = BROW[name]
            return w("ones")[r0:r0 + 1, :], w("m_spread")[r0:r0 + 1, off:off + n]

        half = sb("half", [P, 1])
        sin_t = sb("sin_t", [P, NT, 8])
        cos_t = sb("cos_t", [P, NT, 8])
        trig = sb("trig", [P, 4, NT * 8])
        expA = sb("expA", [P, GH])

        X = [sb(f"X{s}", [P, NT, D]) for s in range(S)]
        XnT = [sb(f"XnT{s}", [P, KD, T]) for s in range(S)]
        stat = [sb(f"stat{s}", [P, NT, 6]) for s in range(S)]
        mv = [sb(f"mv{s}", [P, NT, 2]) for s in range(S)]
        veps = [sb(f"veps{s}", [P, NT]) for s in range(S)]
        rstd = [sb(f"rstd{s}", [P, NT]) for s in range(S)]
        Vp = [sb(f"Vp{s}", [P, NT, NB, PW]) for s in range(S)]
        PR = 2
        prob = sb("prob", [P, PR, SCB * BANK])
        probT = sb("probT", [P, PR, SCB * BANK])
        negmax = sb("negmax", [P, PR, NT, NB])
        rsum = sb("rsum", [P, PR, NT, NB])
        SCR = 7360
        scr = [sb(f"scr{s}", [P, SCR]) for s in range(S)]

        raw = scr[1][:, 0:masks.shape[1]]

        def part(s, off, shape):
            n = 1
            for d in shape:
                n *= d
            assert off + n <= SCR
            v = scr[s][:, off:off + n]
            if len(shape) == 1:
                return v, off + n
            names = "abcd"[:len(shape)]
            pat = "p (" + " ".join(names) + ") -> p " + " ".join(names)
            return v.rearrange(pat, **{names[i]: shape[i] for i in range(len(shape))}), off + n

        Xn = [part(s, 0, [NT, D])[0] for s in range(S)]
        kT, vT, QT, KpT, latT, ctxn, ctxT = ([] for _ in range(7))
        for s in range(S):
            v, o = part(s, 0, [KD, T]); kT.append(v)
            v, o = part(s, o, [KD, T]); vT.append(v)
            v, o = part(s, o, [QTL, T]); QT.append(v)
            v, o = part(s, o, [QG, T]); KpT.append(v)
            v, o = part(s, o, [T]); latT.append(v)
            v, _ = part(s, 6656, [NT, D]); ctxn.append(v)
            v, _ = part(s, 0, [KD, T]); ctxT.append(v)
        SX = 2
        aT, amT, silu_x, x2T, am2, am2T, am2b = ([] for _ in range(7))
        for s in range(S):
            v, o = part(s, 0, [4, T]); aT.append(v)
            v, o = part(s, o, [2, 4, T]); amT.append(v)
            v, o = part(s, o, [SX, T]); silu_x.append(v)
            v, o = part(s, o, [2, FT, T]); x2T.append(v)
            v, _ = part(s, 0, [NT, ER]); am2.append(v)
            v, _ = part(s, NT * ER, [NT, ER]); am2b.append(v)
            v, _ = part(s, 4 * T, [KER, T]); am2T.append(v)
        lg = [sb(f"lg{s}", [P, NT, E]) for s in range(S)]
        top = [sb(f"top{s}", [P, NT, 8]) for s in range(S)]
        topi = [sb(f"topi{s}", [P, NT, 8], U32) for s in range(S)]
        topf = [sb(f"topf{s}", [P, NT, 8]) for s in range(S)]
        rw = [sb(f"rw{s}", [P, 4, NT]) for s in range(S)]
        onehot = [sb(f"onehot{s}", [P, NT, 2, E]) for s in range(S)]
        onehotw = [sb(f"onehotw{s}", [P, NT, 2, E]) for s in range(S)]
        onehotT = [sb(f"onehotT{s}", [2 * E, T]) for s in range(S)]
        rot, rtmp, bV, prod, sc, pw = [], [], [], [], [], []
        for s in range(S):
            v, o = part(s, 0, [NT, 2 * NH, HD]); rot.append(v)
            v, o = part(s, o, [NT, NH, HD]); bV.append(v)
            v, o = part(s, o, [NH, NH, HD]); prod.append(v)
            v, _ = part(s, 1536, [2, 2 * NH, HD]); rtmp.append(v)
            v, o = part(s, o, [NT, NH, NH]); sc.append(v)
            v, o = part(s, o, [NT, NH, NH]); pw.append(v)
        bmax = [sb(f"bmax{s}", [P, NT, NH]) for s in range(S)]
        bsum = [sb(f"bsum{s}", [P, NT, NH]) for s in range(S)]
        convT, tokm, gate, kb, bv, KTt, QTt, KbT, QgT, PT = ([] for _ in range(10))
        sqs = []
        kd, kbg, qg, osq, on, onT = ([] for _ in range(6))
        MAT = [GH, NT, P]
        for s in range(S):
            v, o = part(s, 0, [GT, T]); convT.append(v)
            v, o = part(s, o, [GT, T]); tokm.append(v.rearrange("p a b -> p (a b)").rearrange("p (a b) -> p a b", a=NT))
            v, o = part(s, o, [NT, GV]); gate.append(v)
            v, o = part(s, o, [NT, GH * DK]); kb.append(v)
            v, o = part(s, o, [NT, GV]); bv.append(v)
            v, o = part(s, o, [2, T]); KTt.append(v)
            v, o = part(s, o, [2, T]); QTt.append(v)
            v, o = part(s, o, [2, T]); KbT.append(v)
            v, o = part(s, o, [2, P]); QgT.append(v)
            v, o = part(s, o, [GH * DK]); kd.append(v)
            v, o = part(s, o, [GH * DK]); kbg.append(v)
            v, o = part(s, o, [GH * DK]); qg.append(v)
            v, _ = part(s, 0, MAT); PT.append(v)
            v, _ = part(s, 0, [NT, GQK]); sqs.append(v)
            v, _ = part(s, 1536, [NT, GV]); osq.append(v)
            v, o2 = part(s, 1536 + 768, [NT, GV]); on.append(v)
            v, _ = part(s, 4992, [VT, T]); onT.append(v)
        def mat(buf, i):
            n = GH * NT * P
            return buf[:, :, :].rearrange("p r n -> p (r n)")[:, i * n:(i + 1) * n]\
                .rearrange("p (h a i) -> p h a i", h=GH, a=NT)

        GEs, Yms = mat(prob, 0), mat(prob, 1)
        ATs = [part(s, 1536, MAT)[0] for s in range(S)]
        Tms, Wms = mat(probT, 0), mat(probT, 1)
        small = [sb(f"small{s}", [P, 16, NT, GH]) for s in range(S)]
        ss = [sb(f"ss{s}", [P, NT, 2 * GH]) for s in range(S)]
        fac = [sb(f"fac{s}", [P, NT, 2 * GH]) for s in range(S)]
        expin = [sb(f"expin{s}", [P, NT, 2 * GH]) for s in range(S)]
        expo = [sb(f"expo{s}", [P, NT, 2 * GH]) for s in range(S)]
        gdec = [sb(f"gdec{s}", [P, 2, GH]) for s in range(S)]
        U0s = [part(s, 3840, [GV])[0] for s in range(S)]
        U1s = [part(s, 4992, [GV])[0] for s in range(S)]
        Ukns = [part(s, 5504, [2, P])[0] for s in range(S)]
        S1s = [part(s, 5760, [2, DV])[0] for s in range(S)]
        rv = [sb(f"rv{s}", [P, NT, GH]) for s in range(S)]
        rr = [sb(f"rr{s}", [P, NT, GH]) for s in range(S)]
        HT = []
        for s in range(S):
            v, o = part(s, 0, [HT1, T]); HT.append(v)

        bank = [ctx.enter_context(nc.psum_tensor(f"bank{b}", [P, BANK], F32)) for b in range(BANKS)]

        loaded = [sem(f"loaded{g}") for g in range(len(packs))]
        const_ready = sem("const_ready")
        prep = sem("prep")
        prep_pool = sem("prep_pool")
        masks_loaded = sem("masks_loaded")
        trig_in, trig_out = sem("trig_in"), sem("trig_out")
        arrived = sem("arrived")
        settled = sem("settled")
        turn = sem("turn")
        turn_sems = []

        def tsem(name):
            turn_sems.append(sem(name))
            return turn_sems[-1]

        full = [tsem(f"full{b}") for b in range(BANKS)]
        drained = [tsem(f"drained{b}") for b in range(BANKS)]
        x_loaded = [tsem(f"x_loaded{s}") for s in range(S)]
        x_stored = tsem("x_stored")
        act_step, dve_step, pool_step = tsem("act_step"), tsem("dve_step"), tsem("pool_step")
        var_ready = [tsem(f"var_ready{s}") for s in range(S)]
        rstd_ready = [tsem(f"rstd_ready{s}") for s in range(S)]
        xn_ready = [tsem(f"xn_ready{s}") for s in range(S)]
        x_final = tsem("x_final")
        max_ready = tsem("max_ready")
        ctx_ready = tsem("ctx_ready")
        top_diff = tsem("top_diff")
        top_exp = tsem("top_exp")
        onehot_ready = tsem("onehot_ready")
        am_ready = tsem("am_ready")
        silu_ready = tsem("silu_ready")
        x2_first = tsem("x2_first")
        am2_ready = tsem("am2_ready")
        rot_ready = tsem("rot_ready")
        prod_ready = tsem("prod_ready")
        prod_used = tsem("prod_used")
        b_in = tsem("b_in")
        b_exp = tsem("b_exp")
        bctx_ready = tsem("bctx_ready")
        tap_ready = tsem("tap_ready")
        conv_ready = tsem("conv_ready")
        convs_ready = tsem("convs_ready")
        gate_in = tsem("gate_in")
        gate_exp = tsem("gate_exp")
        g_ready = tsem("g_ready")
        g1_ready = tsem("g1_ready")
        sq_ready = tsem("sq_ready")
        rn_ready = tsem("rn_ready")
        qk_ready = tsem("qk_ready")
        bv_ready = tsem("bv_ready")
        gdec_ready = tsem("gdec_ready")
        kdec_ready = tsem("kdec_ready")
        w_ready = tsem("w_ready")
        osq_ready = tsem("osq_ready")
        orms_in = tsem("orms_in")
        orms = tsem("orms")
        gn_ready = tsem("gn_ready")
        on_ready = tsem("on_ready")
        sem_lo = min(q.num for q in turn_sems)
        sem_hi = max(q.num for q in turn_sems) + 1
        assert sem_hi - sem_lo == len(turn_sems)

        ring = Ring()

        def psum(key, *shape):
            v = bank[ring.bank(key)]
            n = 1
            for d in shape:
                n *= d
            v = v[:, 0:n]
            if len(shape) > 1:
                names = "abc"[:len(shape)]
                v = v.rearrange("p (" + " ".join(names) + ") -> p " + " ".join(names),
                                **{names[i]: shape[i] for i in range(len(shape))})
            return v

        def wait_full(eng, key, fill=1):
            eng.wait_ge(full[ring.bank(key)], ring.filled(key, fill))

        def wait_drained(eng, key):
            eng.wait_ge(drained[ring.bank(key)], ring.drained(key))

        def claim(pe, key, fills=1):
            b, before = ring.claim(key, fills)
            if before:
                pe.wait_ge(drained[b], before)
            return bank[b]

        def drain_of(key):
            return drained[ring.bank(key)]

        def weights_out(eng, k, g, b):
            key = ("pT", k, g, b)
            wait_full(eng, key)
            if g >= PR:
                wait_full(eng, ("pv", k, g - PR))
            dst = probT[:, g % PR, b * BANK:(b + 1) * BANK]
            if eng is nc.scalar:
                ins = eng.activation(dst, psum(key, BANK), ACT.Copy)
            else:
                ins = eng.tensor_copy(dst, psum(key, BANK))
            ins.then_inc(drain_of(key), 1)

        SILUS = [im for m in range(FT + 2) for im in ((0, m), (1, m - 2)) if 0 <= im[1] < FT]

        def silu_at(i, m):
            return SILUS.index((i, m))

        def bcast(ap, n):
            return ap.unsqueeze(ap.ndim if hasattr(ap, "ndim") else len(ap.shape)).broadcast_to(list(ap.shape) + [n])

        def half_blocks(v, l, odd):
            return v.rearrange("p m (n two w) -> p m n two w", two=2, w=1 << l)[:, :, :, odd, :]

        def qk_pairs(s, a, hh):
            n = hh.stop - hh.start
            return (rot[s][:, a, hh, :].unsqueeze(2).broadcast_to([P, n, NH, HD]),
                    rot[s][:, a, NH:2 * NH, :].unsqueeze(1).broadcast_to([P, n, NH, HD]))

        def pv_pairs(s, a, hh):
            n = hh.stop - hh.start
            return (pw[s][:, a, hh].unsqueeze(2).broadcast_to([P, n, HD, NH]),
                    bV[s][:, a].rearrange("p t d -> p d t").unsqueeze(1).broadcast_to([P, n, HD, NH]))

        def program(stage):
            both = range(S)
            for s in both:
                stage("norm_x", 0, s)
            for s in both:
                stage("norm_t", 0, s)
                stage("latent", 0, s)
            for name in ("kv", "kv_fold"):
                for s in both:
                    stage(name, 0, s)
            attention(stage, 0, 1, (("router", 0, 0), ("spread_t", 0, 0), ("spread", 0, 0)))
            experts(stage, 0, 0, {1: [("norm_t", 1, 1)], 3: [("router", 0, 1)], 5: [("spread_t", 0, 1)],
                                  6: [("spread", 0, 1)]})
            stage("x_first", 0, (1, 0))
            stage("lora", 0, 0)
            stage("norm_x", 2, 0)
            experts(stage, 0, 1, token_heads(0))
            stage("spread_t", 1, 0)
            stage("lora", 0, 1)
            stage("spread", 1, 0)
            stage("norm_x", 2, 1)
            stage("x_first", 1, (0, 0))
            experts(stage, 1, 0, token_heads(1))
            stage("spread_t", 1, 1)
            stage("lora", 1, 0)
            stage("spread", 1, 1)
            stage("norm_x", 4, 0)
            stage("x_first", 1, (1, 0))
            def conv_(s, *pairs):
                return [(n, 0, (s, i)) for i in pairs for n in ("delta_conv", "conv_silu")]

            experts(stage, 1, 1, {1: [("norm_t", 4, 0)], 2: [("delta_gate", 0, 0)],
                                  3: conv_(0, 0) + [("delta_log", 0, 0)], 4: conv_(0, 1), 5: conv_(0, 2),
                                  6: [("delta_g1", 0, 0)], 8: [("delta_tok", 0, 0)],
                                  "down00": [("delta_decay", 0, 0), ("delta_qk", 0, 0)],
                                  "down01": [("delta_rows", 0, 0)],
                                  "down10": [("delta_mats", 0, 0)], "down11": [("delta_start", 0, 0)]})
            chain(stage, 0, {1: [("lora", 1, 1), ("norm_x", 4, 1)],
                             2: [("norm_t", 4, 1), ("delta_gate", 0, 1)] + conv_(1, 0),
                             3: conv_(1, 1) + [("delta_log", 0, 1)],
                             4: conv_(1, 2) + [("delta_g1", 0, 1)],
                             5: [("delta_tok", 0, 1)], 6: [("delta_decay", 0, 1)]})
            stage("delta_u", 0, 0)
            stage("delta_qk", 0, 1)
            stage("delta_rows", 0, 1)
            stage("delta_s", 0, 0)
            stage("delta_mats", 0, 1)
            stage("delta_v", 0, 0)
            stage("delta_start", 0, 1)
            chain(stage, 1, {1: [("delta_o", 0, 0)], 2: [("delta_on", 0, 0), ("delta_out_t", 0, 0)],
                             3: [("delta_out", 0, 0), ("norm_x", 5, 0)], 4: [("norm_t", 5, 0)],
                             5: [("ffn_in", 0, 0)], 6: [("ffn_out", 0, 0), ("norm_x", 6, 0)]})
            stage("delta_u", 0, 1)
            stage("norm_t", 6, 0)
            stage("delta_s", 0, 1)
            stage("qkv_b", 0, 0)
            stage("delta_v", 0, 1)
            stage("delta_o", 0, 1)
            attention(stage, 1, 7, (), {-1: [("delta_on", 0, 1), ("delta_out_t", 0, 1)],
                                        0: [("delta_out", 0, 1), ("norm_x", 5, 1)],
                                        1: [("norm_t", 5, 1), ("ffn_in", 0, 1), ("ffn_out", 0, 1),
                                            ("norm_x", 6, 1)],
                                        2: [("norm_t", 6, 1), ("qkv_b", 0, 1)]})
            stage("ffn_in", 1, 0)
            stage("norm_t", 7, 1)
            stage("ffn_out", 1, 0)
            stage("ffn_in", 1, 1)
            stage("ffn_out", 1, 1)

        def chain(stage, s, beside):
            for l in range(1, LEVELS):
                stage("delta_level", 0, (s, l))
                for b in beside.get(l, ()):
                    stage(*b)

        def token_heads(s):
            pieces = [("head_scores", 0, (s, a, h)) for a in range(NT) for h in range(2)] \
                + [("head_mix", 0, (s, a, h)) for a in range(NT) for h in range(2)]
            beside = {1: [("norm_t", 2, s)], 2: [("heads_in", 0, s)] + pieces[0:1]}
            for i in range(1, 7):
                beside[2 + i] = pieces[i:i + 1]
            beside["down00"] = pieces[7:8]
            beside["down01"] = [("head_out_t", 0, s), ("head_out", 0, s), ("norm_x", 3, s)]
            beside["down10"] = [("norm_t", 3, s), ("router", 1, s)]
            return beside

        def experts(stage, k, s, beside):
            for m in range(FT + 2):
                if m < FT and (m or (k, s) == (0, 0)):
                    stage("x_first", k, (s, m))
                if m >= 2:
                    stage("x_second", k, (s, m - 2))
                for b in beside.get(m, ()):
                    stage(*b)
            for i in range(TOPK):
                for a in range(NT):
                    stage("down", k, (s, i, a))
                    for b in beside.get(f"down{i}{a}", ()):
                        stage(*b)
            stage("lora_t", k, s)

        def attention(stage, k, ln, then, beside={}):
            units = S * NU
            for b in range(SCB):
                stage("scores", k, (0, b))
            for other in beside.get(-1, ()):
                stage(*other)
            for g in range(units + 1):
                for b in range(SCB):
                    if g + 1 < units:
                        stage("scores", k, (g + 1, b))
                    if g and b < 2:
                        stage("values", k, (g - 1, b))
                if g < units:
                    stage("weights", k, g)
                for other in beside.get(g, ()):
                    stage(*other)
                if g == NU + 1:
                    stage("out_in", k, 0)
                if g == NU + 2:
                    stage("out_proj", k, 0)
                    stage("norm_x", ln, 0)
                if g == NU + 3:
                    stage("norm_t", ln, 0)
            for b in then[0:1]:
                stage(*b)
            stage("out_in", k, 1)
            for b in then[1:2]:
                stage(*b)
            stage("out_proj", k, 1)
            for b in then[2:]:
                stage(*b)
            stage("norm_x", ln, 1)

        def nothing(k, s):
            pass

        block = ctx.enter_context(nc.Block())

        @block.sync
        def _(sp):
            with sp.Fori(0, B // S, 1) as it:
                for s in range(S):
                    sp.dma_start(X[s][:, :, :], x_in[it * S + s].rearrange("(a p) d -> p a d", p=P))\
                      .then_inc(x_loaded[s], 16)
                for s in range(S):
                    sp.wait_ge(x_final, s + 1)
                    sp.dma_start(out[it * S + s].rearrange("(a p) d -> p a d", p=P), X[s][:, :, :])\
                      .then_inc(x_stored, 16)
                sp.wait_ge(x_stored, 16 * S)
                sp.wait_ge(arrived, it * 4 + 4)
                sp.sem_inc(settled, 1)
                sp.sem_clear(range(sem_lo, sem_hi))
                sp.sem_inc(turn, 1)

        def next_turn(eng, it):
            eng.sem_inc(arrived, 1)
            eng.wait_ge(turn, it + 1)

        @block.tensor
        def _(pe):
            def mm(o, l, r, start, stop=True):
                return pe.matmul(o, l, r, start=start, stop=stop, skip_group_check=True)

            def transposes(key, src, n, dst_cols=P):
                o = claim(pe, key)
                for t in range(n):
                    for a in range(NT):
                        last = pe.transpose(o[:, t * T + a * P:t * T + a * P + P], src(t, a), ident)
                last.then_inc(full[ring.bank(key)], 1)

            def group(o, pairs, start=True):
                for i, (l, r) in enumerate(pairs):
                    last = mm(o, l, r, start and i == 0, i == len(pairs) - 1)
                return last

            def norm_t(k, s):
                pe.wait_ge(xn_ready[s], k + 1)
                transposes(("xnT", k, s), lambda t, a: Xn[s][:, a, t * P:(t + 1) * P], KD)

            def proj(key, s, weights, tiles, per, k=KD):
                for i in range(0, tiles, per):
                    o = claim(pe, key + (i // per,))
                    for j in range(i, min(i + per, tiles)):
                        last = group(o[:, (j - i) * T:(j - i + 1) * T],
                                     [(weights(c, j), XnT[s][:, c, :]) for c in range(k)])
                    last.then_inc(full[ring.bank(key + (i // per,))], 1)

            def latent(_, s):
                wait_drained(pe, ("xnT", 0, s))
                lat = w3("a_wl", KD)
                proj(("lat", s), s, lambda c, j: lat[:, c, :], 1, 1)
                wq = w3("a_wq", KD)
                proj(("q", 0, s), s, lambda c, j: wq[:, c, j * P:(j + 1) * P], QTL, 2)

            def kv(_, s):
                wk, wv = w("a_wk"), w("a_wv")
                wait_drained(pe, ("lat", s, 0))
                for name, wt in (("k", wk), ("v", wv)):
                    o = claim(pe, (name + "T", s))
                    for j in range(KD):
                        last = group(o[:, j * T:(j + 1) * T], [(wt[:, j * P:(j + 1) * P], latT[s][:, :])])
                    last.then_inc(full[ring.bank((name + "T", s))], 1)

            def kv_fold(_, s):
                wait_drained(pe, ("kT", s))
                w2 = w3("a_kfold", KD)
                o = claim(pe, ("kp", 0, s))
                group(o[:, 0:T], [(w2[:, c, :], kT[s][:, c, :]) for c in range(KD)])\
                    .then_inc(full[ring.bank(("kp", 0, s))], 1)
                wait_drained(pe, ("vT", s))
                w2 = w3("a_vfold", KD)
                o = claim(pe, ("vp", 0, s))
                for a in range(NT):
                    last = group(o[:, a * 64:a * 64 + 64],
                                 [(vT[s][:, c, a * P:(a + 1) * P], w2[:, c, :]) for c in range(KD)])
                last.then_inc(full[ring.bank(("vp", 0, s))], 1)

            def qkv_b(_, s):
                wait_drained(pe, ("xnT", 6, s))
                pe.wait_ge(loaded[4], 16)
                wq, wk, wv = w3("d_wq", KD), w3("d_wk", KD), w3("d_wv", KD)
                proj(("q", 1, s), s, lambda c, j: wq[:, c, j * P:(j + 1) * P], QTL, 2)
                o = claim(pe, ("kp", 1, s))
                group(o[:, 0:T], [(wk[:, c, :], XnT[s][:, c, :]) for c in range(KD)])\
                    .then_inc(full[ring.bank(("kp", 1, s))], 1)
                o = claim(pe, ("vp", 1, s))
                for a in range(NT):
                    last = group(o[:, a * HD:(a + 1) * HD],
                                 [bias_row("d_bv")]
                                 + [(XnT[s][:, c, a * P:(a + 1) * P], wv[:, c, :]) for c in range(KD)])
                last.then_inc(full[ring.bank(("vp", 1, s))], 1)

            def scores(k, gb):
                g, b = gb
                s, u = divmod(g, NU)
                if u == 0 and b == 0:
                    wait_drained(pe, ("q", k, s, 0))
                    wait_drained(pe, ("kp", k, s))
                    wait_drained(pe, ("vp", k, s))
                key = ("sc", k, g, b)
                o = claim(pe, key)
                q = QT[s][:, u // 2, :]
                h0 = NB * (u % 2)
                if b < 2:
                    mm(o[:, :], q[:, P:T],
                       KpT[s][:, h0 + 2 * b:h0 + 2 * b + 2, :].rearrange("p h t -> p (h t)"), True)
                    mm(o[:, :].rearrange("p (h t) -> p h t", h=2)[:, :, P:T], identb[:, :],
                       negb[:, :].unsqueeze(1).broadcast_to([P, 2, P]), False).then_inc(full[ring.bank(key)], 1)
                else:
                    mm(o[:, :], q[:, 0:P], KpT[s][:, h0:h0 + NB, 0:P], True)
                    mm(o[:, :], identb[:, :], negb[:, :].unsqueeze(1).broadcast_to([P, NB, P]), False)\
                        .then_inc(full[ring.bank(key)], 1)

            def weights(k, g):
                for b in range(SCB):
                    o = claim(pe, ("pT", k, g, b))
                    wait_drained(pe, ("sc", k, g, b))
                    for c in range(4 * b, 4 * b + 4):
                        last = pe.transpose(o[:, (c - 4 * b) * P:(c - 4 * b + 1) * P],
                                            prob[:, g % PR, c * P:(c + 1) * P], ident)
                    last.then_inc(full[ring.bank(("pT", k, g, b))], 1)

            def values(k, gb):
                g, b = gb
                s, u = divmod(g, NU)
                if b == 0:
                    claim(pe, ("pv", k, g))
                o = bank[ring.bank(("pv", k, g))]
                wait_drained(pe, ("pT", k, g, b))
                if b == 0:
                    wait_drained(pe, ("pT", k, g, 2))
                for j in (2 * b, 2 * b + 1):
                    pt = probT[:, g % PR, :]
                    mm(o[:, j * PW:(j + 1) * PW], pt[:, (8 + j) * P:(9 + j) * P], Vp[s][:, 0, j, :], True)
                    c = (NB + j) * PW
                    last = group(o[:, c:c + PW], [(pt[:, 2 * j * P:(2 * j + 1) * P], Vp[s][:, 0, j, :]),
                                                  (pt[:, (2 * j + 1) * P:(2 * j + 2) * P], Vp[s][:, 1, j, :])])
                if b == 1:
                    last.then_inc(full[ring.bank(("pv", k, g))], 1)

            def out_in(k, s):
                pe.wait_ge(ctx_ready, k * S + s + 1)
                transposes(("ctxT", k, s), lambda t, a: ctxn[s][:, a, t * P:(t + 1) * P], KD)

            def out_proj(k, s):
                name, bias = (("a_wo", "a_bo"), ("d_wo", "d_bo"))[k]
                if k == 0 and s == 0:
                    pe.wait_ge(loaded[1], 16)
                wait_drained(pe, ("ctxT", k, s))
                wo = w3(name, KD)
                o = claim(pe, ("y", k, s))
                for a in range(NT):
                    last = group(o[:, a * D:(a + 1) * D],
                                 [bias_row(bias)]
                                 + [(ctxT[s][:, c, a * P:(a + 1) * P], wo[:, c, :]) for c in range(KD)])
                last.then_inc(full[ring.bank(("y", k, s))], 1)

            def router(k, s):
                r = k * S + s
                ln = 1 if k == 0 else 3
                if r == 0:
                    pe.wait_ge(loaded[1], 16)
                wait_drained(pe, ("xnT", ln, s))
                wa, wg = w3("m_a", KD), w3("m_g", KD)
                o = claim(pe, ("lg", r))
                for a in range(NT):
                    last = group(o[:, a * E:(a + 1) * E],
                                 [(XnT[s][:, c, a * P:(a + 1) * P], wg[:, c, :]) for c in range(KD)])
                last.then_inc(full[ring.bank(("lg", r))], 1)
                proj(("aT", r), s, lambda c, j: wa[:, c, j * P:(j + 1) * P], 4, 2)

            def spread_t(k, s):
                r = k * S + s
                pe.wait_ge(onehot_ready, r + 1)
                o = claim(pe, ("oh", r))
                for a in range(NT):
                    last = pe.transpose(o[0:2 * E, a * P:(a + 1) * P],
                                        onehot[s][:, a].rearrange("p k e -> p (k e)"), ident)
                last.then_inc(full[ring.bank(("oh", r))], 1)

            def spread(k, s):
                r = k * S + s
                wait_drained(pe, ("oh", r))
                ex = w("m_spread", 2 * E).rearrange("p (i n) -> p i n", i=2)
                for i in range(2):
                    o = claim(pe, ("ex", r, i))
                    for t in range(KER):
                        last = mm(o[:, t * T:(t + 1) * T], ex[:, i, t * P:(t + 1) * P], onehotT[s][:, :], True)
                    last.then_inc(full[ring.bank(("ex", r, i))], 1)

            def x_first(k, sm):
                s, m = sm
                r = k * S + s
                w1, w3_, b1, b3 = w3("m_w1", KD), w3("m_w3", KD), w3("m_b1", KER), w3("m_b3", KER)
                o = claim(pe, ("x", r, m), fills=2)
                c0 = slice(m * P, (m + 1) * P)
                for n, (wt, bt) in enumerate(((w1, b1), (w3_, b3))):
                    group_ = [(wt[:, c, c0], XnT[s][:, c, :]) for c in range(KD)]
                    for c, (l, q) in enumerate(group_):
                        mm(o[:, n * T:(n + 1) * T], l, q, n + c == 0, False)
                    if m == 0 and n == 0:
                        pe.wait_ge(am_ready, 4 * (r + 1))
                    last = group(o[:, n * T:(n + 1) * T],
                                 [(bt[:, c, c0], amT[s][:, 0, 2 * n + c, :]) for c in range(KER)], start=False)
                last.then_inc(full[ring.bank(("x", r, m))], 1)

            def x_second(k, sm):
                s, m = sm
                r = k * S + s
                b1, b3 = w3("m_b1", KER), w3("m_b3", KER)
                o = bank[ring.bank(("x", r, m))]
                c0 = slice(m * P, (m + 1) * P)
                pe.wait_ge(x2_first, r * FT + m + 1)
                group(o[:, 0:T], [(b1[:, c, c0], amT[s][:, 1, c, :]) for c in range(KER)], start=False)
                group(o[:, T:2 * T], [(b3[:, c, c0], amT[s][:, 1, 2 + c, :]) for c in range(KER)],
                      start=False).then_inc(full[ring.bank(("x", r, m))], 1)

            def down(k, sia):
                s, i, a = sia
                r = k * S + s
                wd = w3("m_down", FT)
                o = claim(pe, ("down", r, i, a))
                if i == 1 and a == 0:
                    for m in range(FT):
                        wait_drained(pe, ("x", r, m))
                group(o[:, :], [(x2T[s][:, i, m, a * P:(a + 1) * P], wd[:, m, :]) for m in range(FT)])\
                    .then_inc(full[ring.bank(("down", r, i, a))], 1)

            def lora_t(k, s):
                r = k * S + s
                pe.wait_ge(am2_ready, r + 1)
                transposes(("am2T", r), lambda t, a: am2[s][:, a, t * P:(t + 1) * P], KER)

            def lora(k, s):
                r = k * S + s
                wait_drained(pe, ("am2T", r))
                b2 = w3("m_b2", KER)
                o = claim(pe, ("lora2", r))
                for a in range(NT):
                    last = group(o[:, a * D:(a + 1) * D],
                                 [(am2T[s][:, c, a * P:(a + 1) * P], b2[:, c, :]) for c in range(KER)])
                last.then_inc(full[ring.bank(("lora2", r))], 1)

            def heads_in(_, s):
                wait_drained(pe, ("xnT", 2, s))
                if s == 0:
                    pe.wait_ge(loaded[2], 16)
                wqkv = w3("b_wqkv", KD)
                for a in range(NT):
                    o = claim(pe, ("bqk", s, a))
                    group(o[:, :], [(XnT[s][:, c, a * P:(a + 1) * P], wqkv[:, c, 0:2 * D]) for c in range(KD)])\
                        .then_inc(full[ring.bank(("bqk", s, a))], 1)
                o = claim(pe, ("bv", s))
                for a in range(NT):
                    last = group(o[:, a * D:(a + 1) * D],
                                 [(XnT[s][:, c, a * P:(a + 1) * P], wqkv[:, c, 2 * D:3 * D]) for c in range(KD)])
                last.then_inc(full[ring.bank(("bv", s))], 1)

            def head_out_t(_, s):
                pe.wait_ge(bctx_ready, s + 1)
                transposes(("bctxT", s), lambda t, a: ctxn[s][:, a, t * P:(t + 1) * P], KD)

            def head_out(_, s):
                wait_drained(pe, ("bctxT", s))
                wo = w3("b_wo", KD)
                o = claim(pe, ("by", s))
                for a in range(NT):
                    last = group(o[:, a * D:(a + 1) * D],
                                 [(ctxT[s][:, c, a * P:(a + 1) * P], wo[:, c, :]) for c in range(KD)])
                last.then_inc(full[ring.bank(("by", s))], 1)

            def delta_gate(_, s):
                wait_drained(pe, ("xnT", 4, s))
                if s == 0:
                    pe.wait_ge(loaded[3], 16)
                wba, wg = w3("c_wba", KD), w3("c_wg", KD)
                o = claim(pe, ("ba", s))
                for a in range(NT):
                    last = group(o[:, a * 2 * GH:(a + 1) * 2 * GH],
                                 [(XnT[s][:, c, a * P:(a + 1) * P], wba[:, c, :]) for c in range(KD)])
                last.then_inc(full[ring.bank(("ba", s))], 1)
                for a in range(NT):
                    o = claim(pe, ("gt", s, a))
                    group(o[:, 0:GV], [(XnT[s][:, c, a * P:(a + 1) * P], wg[:, c, :]) for c in range(KD)])\
                        .then_inc(full[ring.bank(("gt", s, a))], 1)

            def delta_conv(_, si):
                s, i = si
                wqkv = w3("c_wqkv", KD)
                o = claim(pe, ("cv", s, i))
                for j in range(2):
                    c0 = slice((2 * i + j) * P, (2 * i + j + 1) * P)
                    last = group(o[:, j * T:(j + 1) * T], [(wqkv[:, c, c0], XnT[s][:, c, :]) for c in range(KD)])
                last.then_inc(full[ring.bank(("cv", s, i))], 1)

            def delta_tok(_, s):
                pe.wait_ge(convs_ready, GT // 2 * (s + 1))
                for a in range(NT):
                    for part_, (lo, hi) in enumerate(((0, 4), (4, GT))):
                        o = claim(pe, ("tm", s, a, part_))
                        for t in range(lo, hi):
                            last = pe.transpose(o[:, (t - lo) * P:(t - lo + 1) * P],
                                                convT[s][:, t, a * P:(a + 1) * P], ident)
                        last.then_inc(full[ring.bank(("tm", s, a, part_))], 1)

            def delta_decay(_, s):
                pe.wait_ge(g_ready, s + 1)
                o = claim(pe, ("gd", s))
                gl = small[s][:, 9]
                mm(o[:, 0:GH], w("tri_up"), gl[:, 1, :], True)
                mm(o[:, GH:2 * GH], w("low_strict"), gl[:, 0, :], True).then_inc(full[ring.bank(("gd", s))], 1)
                pe.wait_ge(g1_ready, s + 1)
                for q in range(GH // 2):
                    o = claim(pe, ("L", s, q))
                    for hh in range(2):
                        for a in range(NT):
                            c = (hh * NT + a) * P
                            mm(o[:, c:c + P], GEs[:, 2 * q + hh, a, :], w("tri_up"), hh + a == 0)
                    mm(o[:, :], identb[:, :], neg4b[:, :, :].rearrange("p a b -> p (a b)"), False)\
                        .then_inc(full[ring.bank(("L", s, q))], 1)

            def delta_rows(_, s):
                pe.wait_ge(qk_ready, s + 1)
                for name, src in (("K", lambda a: tokm[s][:, a, GH * DK:2 * GH * DK]),
                                  ("Kb", lambda a: kb[s][:, a, :]),
                                  ("Q", lambda a: tokm[s][:, a, 0:GH * DK])):
                    o = claim(pe, (name, s))
                    for a in range(NT):
                        pe.transpose(o[:, a * P:(a + 1) * P], src(a)[:, 0:P], ident)
                        last = pe.transpose(o[0:64, T + a * P:T + (a + 1) * P], src(a)[:, P:GH * DK], ident)
                    last.then_inc(full[ring.bank((name, s))], 1)

            def delta_mats(_, s):
                for name, right in (("A", KbT), ("PT", QTt)):
                    if name == "A":
                        wait_drained(pe, ("K", s))
                        wait_drained(pe, ("Kb", s))
                    else:
                        wait_drained(pe, ("Q", s))
                    for b in range(4):
                        claim(pe, (name, s, b))
                    for b in range(4):
                        o = bank[ring.bank((name, s, b))]
                        r0 = slice(32 * b, 32 * b + 32)
                        for t in range(2 if b < 2 else 1):
                            for a in range(NT):
                                c = (t * NT + a) * P
                                last = mm(o[:, c:c + P], KTt[s][r0, t, a * P:(a + 1) * P],
                                          right[s][r0, t, a * P:(a + 1) * P], t + a == 0)
                        last.then_inc(full[ring.bank((name, s, b))], 1)
                pe.wait_ge(kdec_ready, s + 1)
                o = claim(pe, ("Qg", s))
                pe.transpose(o[:, 0:P], qg[s][:, 0:P], ident)
                pe.transpose(o[0:64, P:2 * P], qg[s][:, P:GH * DK], ident).then_inc(full[ring.bank(("Qg", s))], 1)

            def delta_start(_, s):
                for q in range(GH // 2):
                    pe.wait_ge(w_ready, s * GH // 2 + q + 1)
                    o = claim(pe, ("T0", s, q))
                    for hh in range(2):
                        for a in range(NT):
                            c = (hh * NT + a) * P
                            last = pe.transpose(o[:, c:c + P], Wms[:, 2 * q + hh, a, :], ident)
                    last.then_inc(full[ring.bank(("T0", s, q))], 1)

            def delta_level(_, sl):
                s, l = sl

                def quad(name, q, left, right):
                    o = claim(pe, (name, s, l, q))
                    for hh in range(2):
                        for a in range(NT):
                            c = (hh * NT + a) * P
                            last = mm(o[:, c:c + P], left[:, 2 * q + hh, a, :], right[:, 2 * q + hh, a, :],
                                      hh + a == 0)
                    last.then_inc(full[ring.bank((name, s, l, q))], 1)

                for q in range(GH // 2):
                    wait_drained(pe, ("T0", s, q) if l == 1 else ("dT", s, l - 1, q))
                    quad("Y", q, ATs[s], Tms)
                for q in range(GH // 2):
                    wait_drained(pe, ("Y", s, l, q))
                    if l > 1:
                        wait_drained(pe, ("dW", s, l - 1, q))
                    if l < LEVELS - 1:
                        quad("dT", q, Wms, Yms)
                    quad("dW", q, Yms, Wms)

            def delta_u(_, s):
                for q in range(GH // 2):
                    wait_drained(pe, ("dW", s, LEVELS - 1, q))
                pe.wait_ge(bv_ready, s + 1)
                o = claim(pe, ("U0", s))
                for h in range(GH):
                    last = mm(o[:, h * DV:(h + 1) * DV], Wms[:, h, 0, :], bv[s][:, 0, h * DV:(h + 1) * DV], True)
                last.then_inc(full[ring.bank(("U0", s))], 1)
                o = claim(pe, ("Uk", s))
                for h in range(GH):
                    r0 = 32 * (h % 4)
                    t = h // 4
                    last = mm(o[r0:r0 + 32, t * P:(t + 1) * P], kbg[s][:, h * DK:(h + 1) * DK], Wms[:, h, 1, :], True)
                last.then_inc(full[ring.bank(("Uk", s))], 1)

            def delta_s(_, s):
                wait_drained(pe, ("U0", s))
                o = claim(pe, ("S1", s))
                for h in range(GH):
                    r0 = 32 * (h % 4)
                    t = h // 4
                    last = mm(o[r0:r0 + 32, t * DV:(t + 1) * DV], kd[s][:, h * DK:(h + 1) * DK],
                              U0s[s][:, h * DV:(h + 1) * DV], True)
                last.then_inc(full[ring.bank(("S1", s))], 1)

            def delta_v(_, s):
                wait_drained(pe, ("S1", s))
                wait_drained(pe, ("Uk", s))
                for b in range(4):
                    o = claim(pe, ("U1", s, b))
                    r0 = slice(32 * b, 32 * b + 32)
                    for t in range(2 if b < 2 else 1):
                        h = b + 4 * t
                        last = group(o[:, t * DV:(t + 1) * DV],
                                     [(Wms[:, h, 1, :], bv[s][:, 1, h * DV:(h + 1) * DV]),
                                      (Ukns[s][r0, t, :], S1s[s][r0, t, :])])
                    last.then_inc(full[ring.bank(("U1", s, b))], 1)

            def delta_o(_, s):
                for b in range(4):
                    wait_drained(pe, ("PT", s, b))
                o = claim(pe, ("O", s, 0))
                for h in range(GH):
                    last = mm(o[:, h * DV:(h + 1) * DV], PT[s][:, h, 0, :], U0s[s][:, h * DV:(h + 1) * DV], True)
                last.then_inc(full[ring.bank(("O", s, 0))], 1)
                wait_drained(pe, ("Qg", s))
                for b in range(4):
                    wait_drained(pe, ("U1", s, b))
                    o = claim(pe, ("O1", s, b))
                    r0 = slice(32 * b, 32 * b + 32)
                    for t in range(2 if b < 2 else 1):
                        h = b + 4 * t
                        last = group(o[:, t * DV:(t + 1) * DV],
                                     [(PT[s][:, h, 1, :], U1s[s][:, h * DV:(h + 1) * DV]),
                                      (QgT[s][r0, t, :], S1s[s][r0, t, :])])
                    last.then_inc(full[ring.bank(("O1", s, b))], 1)

            def delta_out_t(_, s):
                pe.wait_ge(on_ready, s + 1)
                for i, (lo, hi) in enumerate(((0, 2), (2, VT))):
                    transposes(("onT", s, i), lambda t, a: on[s][:, a, (lo + t) * P:(lo + t + 1) * P], hi - lo)

            def delta_out(_, s):
                wait_drained(pe, ("onT", s, 0))
                wait_drained(pe, ("onT", s, 1))
                wo = w3("c_wo", VT)
                o = claim(pe, ("cy", s))
                for a in range(NT):
                    last = group(o[:, a * D:(a + 1) * D],
                                 [(onT[s][:, c, a * P:(a + 1) * P], wo[:, c, :]) for c in range(VT)])
                last.then_inc(full[ring.bank(("cy", s))], 1)

            def ffn_in(k, s):
                r = k * S + s
                if r == 0:
                    pe.wait_ge(loaded[5], 16)
                wait_drained(pe, ("xnT", 5 + 2 * k, s))
                w1 = w3("f_w1", KD)
                proj(("h", r), s, lambda c, j: w1[:, c, j * P:(j + 1) * P], HT1, 2)

            def ffn_out(k, s):
                r = k * S + s
                w2 = w3("f_w2", HT1)
                for i in range(HT1 // 2):
                    wait_drained(pe, ("h", r, i))
                o = claim(pe, ("fy", r))
                for a in range(NT):
                    last = group(o[:, a * D:(a + 1) * D],
                                 [bias_row("f_b2")]
                                 + [(HT[s][:, m, a * P:(a + 1) * P], w2[:, m, :]) for m in range(HT1)])
                last.then_inc(full[ring.bank(("fy", r))], 1)

            table = dict(norm_x=nothing, norm_t=norm_t, latent=latent, kv=kv, kv_fold=kv_fold,
                         scores=scores, weights=weights, values=values, out_in=out_in, out_proj=out_proj, router=router, spread_t=spread_t, spread=spread, x_first=x_first,
                         x_second=x_second, down=down, lora_t=lora_t, lora=lora,
                         heads_in=heads_in, head_scores=nothing, head_mix=nothing, head_out_t=head_out_t,
                         head_out=head_out, delta_gate=delta_gate, delta_conv=delta_conv, delta_log=nothing, delta_g1=nothing, conv_silu=nothing,
                         delta_qk=nothing, delta_on=nothing,
                         delta_tok=delta_tok, delta_decay=delta_decay, delta_rows=delta_rows, delta_mats=delta_mats,
                         delta_start=delta_start, delta_level=delta_level, delta_u=delta_u, delta_s=delta_s,
                         delta_v=delta_v, delta_o=delta_o, delta_out_t=delta_out_t, delta_out=delta_out, ffn_in=ffn_in, ffn_out=ffn_out, qkv_b=qkv_b)
            pe.wait_ge(loaded[0], 16)
            pe.wait_ge(const_ready, 4)
            with pe.Fori(0, B // S, 1) as it:
                program(lambda name, k, s: table[name](k, s))
                next_turn(pe, it)

        @block.scalar
        def _(act):
            count = [0]

            def step(ins):
                count[0] += 1
                ins.then_inc(act_step, 1)
                return count[0]

            def move(key, dst, src, func=ACT.Copy, **kw):
                act.activation(dst, src, func, **kw).then_inc(drain_of(key), 1)

            def norm_t(k, s):
                key = ("xnT", k, s)
                wait_full(act, key)
                move(key, XnT[s][:, :, :], psum(key, KD, T))

            def latent(_, s):
                key = ("lat", s, 0)
                wait_full(act, key)
                move(key, latT[s][:, :], psum(key, T), ACT.Silu, bias=w("a_bl"))

            def scores(k, gb):
                g, b = gb
                key = ("sc", k, g, b)
                act.wait_ge(max_ready, (k * S * NU + g) * SCB + b + 1)
                if k * S * NU + g >= PR:
                    wait_full(act, ("pT", k, g - PR, b) if g >= PR else ("pT", 0, S * NU - PR + g, b))
                tile = 0 if b == 2 else 1
                n = NB if b == 2 else 2
                width = BANK // n
                for i in range(n):
                    j = i if b == 2 else 2 * b + i
                    ins = act.activation(prob[:, g % PR, b * BANK + i * width:b * BANK + (i + 1) * width],
                                         psum(key, BANK)[:, i * width:(i + 1) * width], ACT.Exp,
                                         bias=negmax[:, g % PR, tile, j:j + 1])
                ins.then_inc(drain_of(key), 1)

            def weights(k, g):
                weights_out(act, k, g, SCB - 1)

            def out_in(k, s):
                key = ("ctxT", k, s)
                wait_full(act, key)
                if k == 0:
                    move(key, ctxT[s][:, :, :], psum(key, KD, T), ACT.Identity, bias=w("a_b2"))
                else:
                    move(key, ctxT[s][:, :, :], psum(key, KD, T))

            def router(k, s):
                r = k * S + s
                for i in range(2):
                    key = ("aT", r, i)
                    wait_full(act, key)
                    move(key, aT[s][:, 2 * i:2 * i + 2, :], psum(key, 2, T))
                act.wait_ge(top_diff, r + 1)
                act.activation(rw[s][:, 2, :], rw[s][:, 3, :], ACT.Exp).then_inc(top_exp, 1)

            def spread_t(k, s):
                key = ("oh", k * S + s)
                wait_full(act, key)
                move(key, onehotT[s][:, :], psum(key, T)[0:2 * E])

            def silu(k, s, i, m):
                r = k * S + s
                key = ("x", r, m)
                wait_full(act, key, i + 1)
                n = silu_at(i, m)
                if n >= SX:
                    i0, m0 = SILUS[n - SX]
                    if i0 == 0:
                        act.wait_ge(x2_first, r * FT + m0 + 1)
                    else:
                        wait_drained(act, ("x", r, m0))
                act.activation(silu_x[s][:, n % SX, :], psum(key, T), ACT.Silu).then_inc(silu_ready, 1)

            def x_first(k, sm):
                silu(k, sm[0], 0, sm[1])

            def x_second(k, sm):
                silu(k, sm[0], 1, sm[1])

            def lora_t(k, s):
                key = ("am2T", k * S + s)
                wait_full(act, key)
                move(key, am2T[s][:, :, :], psum(key, KER, T))

            def heads_in(_, s):
                key = ("bv", s)
                wait_full(act, key)
                move(key, bV[s][:, :, :, :].rearrange("p a h d -> p (a h d)"), psum(key, NT * D))

            def head_scores(_, sah):
                s, a, h = sah
                if h == 1:
                    act.wait_ge(b_in, s * NT + a + 1)
                    act.activation(pw[s][:, a], sc[s][:, a], ACT.Exp, scale=HD ** -0.5).then_inc(b_exp, 1)

            def head_out_t(_, s):
                key = ("bctxT", s)
                wait_full(act, key)
                move(key, ctxT[s][:, :, :], psum(key, KD, T))

            def delta_gate(_, s):
                act.wait_ge(gate_in, s + 1)
                act.activation(expo[s][:, :, :], expin[s][:, :, :], ACT.Exp).then_inc(gate_exp, 1)
                for a in range(NT):
                    key = ("gt", s, a)
                    wait_full(act, key)
                    move(key, gate[s][:, a, :], psum(key, GV), ACT.Silu)

            def delta_conv(_, si):
                s, i = si
                cw = w("c_conv").rearrange("p (t j) -> p t j", t=GT)
                key = ("cv", s, i)
                wait_full(act, key)
                o = psum(key, 2, T)
                for j in range(2):
                    t = 2 * i + j
                    ins = act.activation(convT[s][:, t, :], o[:, j, :], ACT.Copy, scale=cw[:, t, CONV - 1:CONV])
                ins.then_inc(tap_ready, 1)

            def conv_silu(_, si):
                s, i = si
                act.wait_ge(conv_ready, s * (GT // 2) + i + 1)
                act.activation(convT[s][:, 2 * i:2 * i + 2, :], convT[s][:, 2 * i:2 * i + 2, :], ACT.Silu)\
                   .then_inc(convs_ready, 1)

            def delta_tok(_, s):
                for a in range(NT):
                    for i, (lo, hi) in enumerate(((0, 4), (4, GT))):
                        key = ("tm", s, a, i)
                        wait_full(act, key)
                        move(key, tokm[s][:, a, lo * P:hi * P], psum(key, (hi - lo) * P))

            def delta_decay(_, s):
                key = ("gd", s)
                wait_full(act, key)
                move(key, gdec[s][:, :, :], psum(key, 2, GH), ACT.Exp)
                for q in range(GH // 2):
                    key = ("L", s, q)
                    wait_full(act, key)
                    move(key, GEs[:, 2 * q:2 * q + 2].rearrange("p h a i -> p (h a i)"), psum(key, BANK), ACT.Exp)

            def delta_rows(_, s):
                for name, dst in (("K", KTt), ("Kb", KbT), ("Q", QTt)):
                    key = (name, s)
                    wait_full(act, key)
                    o = psum(key, 2, T)
                    n = step(act.activation(dst[s][:, 0, :], o[:, 0, :], ACT.Copy))
                    act.wait_ge(act_step, n)
                    move(key, dst[s][0:64, 1, :], o[0:64, 1, :])

            def delta_mats(_, s):
                key = ("Qg", s)
                wait_full(act, key)
                o = psum(key, 2, P)
                n = step(act.activation(QgT[s][:, 0, :], o[:, 0, :], ACT.Copy))
                act.wait_ge(act_step, n)
                move(key, QgT[s][0:64, 1, :], o[0:64, 1, :])

            def delta_start(_, s):
                for q in range(GH // 2):
                    key = ("T0", s, q)
                    wait_full(act, key)
                    move(key, Tms[:, 2 * q:2 * q + 2].rearrange("p h a i -> p (h a i)"), psum(key, BANK))

            def delta_u(_, s):
                key = ("U0", s)
                wait_full(act, key)
                move(key, U0s[s][:, :], psum(key, GV))
                key = ("Uk", s)
                wait_full(act, key)
                o = psum(key, 2, P)
                n = step(act.activation(Ukns[s][:, 0, :], o[:, 0, :], ACT.Copy, scale=-1.0))
                act.wait_ge(act_step, n)
                move(key, Ukns[s][0:64, 1, :], o[0:64, 1, :], scale=-1.0)

            def delta_s(_, s):
                key = ("S1", s)
                wait_full(act, key)
                o = psum(key, 2, DV)
                n = step(act.activation(S1s[s][:, 0, :], o[:, 0, :], ACT.Copy))
                act.wait_ge(act_step, n)
                move(key, S1s[s][0:64, 1, :], o[0:64, 1, :])

            def delta_v(_, s):
                for b in range(4):
                    key = ("U1", s, b)
                    wait_full(act, key)
                    n = 2 if b < 2 else 1
                    move(key, U1s[s].rearrange("p (h d) -> p h d", d=DV)[:, b:b + 4 * n - 3:4, :],
                         psum(key, n, DV))

            def delta_o(_, s):
                wait_full(act, ("O", s, 0))
                act.activation(osq[s][:, 0, :], psum(("O", s, 0), GV), ACT.Square).then_inc(osq_ready, 1)
                for b in range(4):
                    key = ("O1", s, b)
                    wait_full(act, key)
                    n = 2 if b < 2 else 1
                    act.activation(osq[s][:, 1, :].rearrange("p (h d) -> p h d", d=DV)[:, b:b + 4 * n - 3:4, :],
                                   psum(key, n, DV), ACT.Square).then_inc(osq_ready, 1)

            def delta_out_t(_, s):
                for i, n in enumerate((2, VT - 2)):
                    key = ("onT", s, i)
                    wait_full(act, key)
                    move(key, onT[s][:, 2 * i:2 * i + n, :], psum(key, n, T))

            def ffn_in(k, s):
                r = k * S + s
                for i in range(HT1 // 2):
                    key = ("h", r, i)
                    wait_full(act, key)
                    o = psum(key, 2, T)
                    b1 = w("f_b1")
                    n = step(act.activation(HT[s][:, 2 * i, :], o[:, 0, :], ACT.Gelu, bias=b1[:, 2 * i:2 * i + 1]))
                    act.wait_ge(act_step, n)
                    move(key, HT[s][:, 2 * i + 1, :], o[:, 1, :], ACT.Gelu, bias=b1[:, 2 * i + 1:2 * i + 2])

            table = dict(norm_x=nothing, norm_t=norm_t, latent=latent, kv=nothing, kv_fold=nothing,
                         scores=scores, weights=weights, values=nothing, out_in=out_in, out_proj=nothing, router=router, spread_t=spread_t, spread=nothing, x_first=x_first,
                         x_second=x_second, down=nothing, lora_t=lora_t, lora=nothing,
                         heads_in=heads_in, head_scores=head_scores, head_mix=nothing, head_out_t=head_out_t,
                         head_out=nothing, delta_gate=delta_gate, delta_conv=delta_conv, delta_log=nothing, delta_g1=nothing, conv_silu=conv_silu,
                         delta_qk=nothing, delta_on=nothing,
                         delta_tok=delta_tok, delta_decay=delta_decay, delta_rows=delta_rows, delta_mats=delta_mats,
                         delta_start=delta_start, delta_level=nothing, delta_u=delta_u, delta_s=delta_s,
                         delta_v=delta_v, delta_o=delta_o, delta_out_t=delta_out_t, delta_out=nothing, ffn_in=ffn_in, ffn_out=nothing, qkv_b=nothing)
            act.dma_start(raw, masks).then_inc(masks_loaded, 16)
            for g in range(len(packs)):
                act.dma_start(pk[g][:, :], packs[g]).then_inc(loaded[g], 16)
            act.wait_ge(trig_in, 1)
            act.activation(cos_t[:, :, :].rearrange("p a i -> p (a i)"), trig[:, 1, :], ACT.Sin).then_inc(trig_out, 1)
            act.activation(sin_t[:, :, :].rearrange("p a i -> p (a i)"), trig[:, 0, :], ACT.Sin).then_inc(trig_out, 1)
            act.wait_ge(loaded[0], 16)
            act.activation(expA[:, :], w("c_alog"), ACT.Exp).then_inc(trig_out, 1)
            with act.Fori(0, B // S, 1) as it:
                count[0] = 0
                program(lambda name, k, s: table[name](k, s))
                next_turn(act, it)

        @block.vector
        def _(dve):
            count = [0]

            def step(ins):
                count[0] += 1
                ins.then_inc(dve_step, 1)

            def settle():
                dve.wait_ge(dve_step, count[0])

            def link(ins):
                step(ins)
                settle()

            def residual(key, s, n=NT * D):
                wait_full(dve, key)
                xf = X[s][:, :, :].rearrange("p a d -> p (a d)")
                dve.tensor_tensor(xf, psum(key, n), xf, ALU.add).then_inc(drain_of(key), 1)
                wait_drained(dve, key)

            def norm_x(k, s):
                if k == 0:
                    dve.wait_ge(x_loaded[s], 16)
                for a in range(NT):
                    step(dve.bn_stats(stat[s][:, a, :], X[s][:, a, :]))
                settle()
                for a in range(NT):
                    step(dve.bn_aggr(mv[s][:, a, :], stat[s][:, a, :]))
                settle()
                dve.tensor_scalar(veps[s][:, :], mv[s][:, :, 1], LN_EPS, None, ALU.add).then_inc(var_ready[s], 1)
                dve.wait_ge(rstd_ready[s], k + 1)
                for a in range(NT):
                    ins = dve.tensor_scalar(Xn[s][:, a, :], X[s][:, a, :], mv[s][:, a, 0:1],
                                            rstd[s][:, a:a + 1], ALU.subtract, ALU.mult)
                    if a < NT - 1:
                        link(ins)
                ins.then_inc(xn_ready[s], 1)

            def queries(k, s, name, scale):
                bq = w(name)
                key = ("q", k, s, 0)
                wait_full(dve, key)
                o = psum(key, QTL, T)
                for t in range(QTL):
                    ins = dve.tensor_scalar(QT[s][:, t, :], o[:, t, :], bq[:, t:t + 1], scale, ALU.add, ALU.mult)
                    if t == 0:
                        link(ins)
                ins.then_inc(drain_of(key), 1)

            def latent(_, s):
                queries(0, s, "a_bq", 64 ** -0.5)

            def kv(_, s):
                for name, dst, bias in (("kT", kT, w("a_bk")), ("vT", vT, w("a_bv"))):
                    key = (name, s)
                    wait_full(dve, key)
                    o = psum(key, KD, T)
                    for c in range(KD):
                        ins = dve.tensor_scalar(dst[s][:, c, :], o[:, c, :], bias[:, c:c + 1], None, ALU.add)
                        if c == 0:
                            link(ins)
                    ins.then_inc(drain_of(key), 1)

            def kv_fold(_, s):
                key = ("kp", 0, s)
                wait_full(dve, key)
                own = w("own_rows")
                for i in range(QG):
                    ins = dve.tensor_scalar(KpT[s][:, i, :], psum(key, T), own[:, i:i + 1], None, ALU.mult)
                    if i < QG - 1:
                        step(ins)
                ins.then_inc(drain_of(key), 1)
                key = ("vp", 0, s)
                wait_full(dve, key)
                dve.tensor_copy(Vp[s][:, :, :, 0:HD], psum(key, NT, NB, HD)).then_inc(drain_of(key), 1)

            def qkv_b(_, s):
                queries(1, s, "d_bq", HD ** -0.5)
                key = ("kp", 1, s)
                wait_full(dve, key)
                own = w("own_rows")
                for i in range(QG):
                    ins = dve.tensor_scalar(KpT[s][:, i, :], psum(key, T), w("d_bk"), own[:, i:i + 1],
                                            ALU.add, ALU.mult)
                    if i < QG - 1:
                        step(ins)
                ins.then_inc(drain_of(key), 1)
                key = ("vp", 1, s)
                wait_full(dve, key)
                o = psum(key, NT, HD)
                for j in range(NB):
                    ins = dve.tensor_copy(Vp[s][:, :, j, 0:HD], o)
                    if j < NB - 1:
                        link(ins)
                ins.then_inc(drain_of(key), 1)

            def scores(k, gb):
                g, b = gb
                key = ("sc", k, g, b)
                wait_full(dve, key)
                if g >= PR:
                    wait_drained(dve, ("sc", k, g - PR, b))
                n = NB if b == 2 else 2
                dst = negmax[:, g % PR, 0, :] if b == 2 else negmax[:, g % PR, 1, 2 * b:2 * b + 2]
                dve.tensor_reduce(dst, psum(key, n, BANK // n), AX.X, ALU.max, negate=True).then_inc(max_ready, 1)

            def weights(k, g):
                for b in range(SCB - 1):
                    weights_out(dve, k, g, b)

            def values(k, gb):
                g, b = gb
                if b == 0:
                    return
                s, u = divmod(g, NU)
                key = ("pv", k, g)
                wait_full(dve, key)
                o = psum(key, NT, NB, PW)
                link(dve.reciprocal(rsum[:, g % PR], o[:, :, :, HD]))
                c = ctxn[s][:, :, :].rearrange("p a (j u d) -> p a j u d", j=NB, u=NU)
                dve.tensor_tensor(c[:, :, :, u, :], o[:, :, :, 0:HD], bcast(rsum[:, g % PR], HD), ALU.mult)\
                   .then_inc(drain_of(key), 1)
                if u == NU - 1:
                    for v in range(NU):
                        wait_drained(dve, ("pv", k, s * NU + v))
                    dve.sem_inc(ctx_ready, 1)

            def out_proj(k, s):
                residual(("y", k, s), s)

            def router(k, s):
                r = k * S + s
                key = ("lg", r)
                wait_full(dve, key)
                dve.tensor_copy(lg[s][:, :, :], psum(key, NT, E)).then_inc(drain_of(key), 1)
                wait_drained(dve, key)
                for a in range(NT):
                    step(dve.max(top[s][:, a, :], lg[s][:, a, :]))
                settle()
                dve.tensor_tensor(rw[s][:, 3, :], top[s][:, :, 1], top[s][:, :, 0], ALU.subtract)\
                   .then_inc(top_diff, 1)
                for a in range(NT):
                    step(dve.max_index(topi[s][:, a, :], top[s][:, a, :], lg[s][:, a, :]))
                settle()
                link(dve.tensor_copy(topf[s][:, :, :], topi[s][:, :, :]))
                iota = w("iota")
                for a in range(NT):
                    for i in range(TOPK):
                        ins = dve.tensor_scalar(onehot[s][:, a, i, :], iota, topf[s][:, a, i:i + 1], None,
                                                ALU.is_equal)
                        if a * TOPK + i < NT * TOPK - 1:
                            link(ins)
                ins.then_inc(onehot_ready, 1)
                dve.wait_ge(top_exp, r + 1)
                link(dve.tensor_scalar(rw[s][:, 3, :], rw[s][:, 2, :], 1.0, None, ALU.add))
                link(dve.reciprocal(rw[s][:, 0, :], rw[s][:, 3, :]))
                link(dve.tensor_tensor(rw[s][:, 1, :], rw[s][:, 2, :], rw[s][:, 0, :], ALU.mult))
                for a in range(NT):
                    for i in range(TOPK):
                        step(dve.tensor_scalar(onehotw[s][:, a, i, :], iota, topf[s][:, a, i:i + 1],
                                               rw[s][:, i, a:a + 1], ALU.is_equal, ALU.mult))
                settle()

            def spread(k, s):
                r = k * S + s
                for i in range(2):
                    wait_drained(dve, ("aT", r, i))
                for i in range(2):
                    key = ("ex", r, i)
                    wait_full(dve, key)
                    for j in range(2):
                        dve.tensor_tensor(amT[s][:, i, 2 * j:2 * j + 2, :], aT[s][:, 2 * j:2 * j + 2, :],
                                          psum(key, KER, T), ALU.mult).then_inc(am_ready, 1)
                    dve.wait_ge(am_ready, 4 * r + 2 * i + 2)
                    dve.sem_inc(drain_of(key), 1)

            def product(k, s, i, m):
                r = k * S + s
                key = ("x", r, m)
                n = silu_at(i, m)
                dve.wait_ge(silu_ready, r * len(SILUS) + n + 1)
                dve.tensor_tensor(x2T[s][:, i, m, :], psum(key, 2, T)[:, 1, :], silu_x[s][:, n % SX, :], ALU.mult)\
                   .then_inc(x2_first if i == 0 else drain_of(key), 1)

            def x_first(k, sm):
                product(k, sm[0], 0, sm[1])

            def x_second(k, sm):
                product(k, sm[0], 1, sm[1])

            def down(k, sia):
                s, i, a = sia
                r = k * S + s
                key = ("down", r, i, a)
                wait_full(dve, key)
                o = psum(key, 2, D)
                link(dve.scalar_tensor_tensor(out=X[s][:, a, :], in0=o[:, 0, :],
                                              scalar=rw[s][:, i, a:a + 1], in1=X[s][:, a, :],
                                              op0=ALU.mult, op1=ALU.add))
                dst = am2 if i == 0 else am2b
                dve.tensor_tensor(dst[s][:, a].rearrange("p (e r) -> p e r", e=E),
                                  o[:, 1, :].rearrange("p (e r) -> p e r", e=E),
                                  bcast(onehotw[s][:, a, i, :], R), ALU.mult).then_inc(drain_of(key), 1)
                wait_drained(dve, key)

            def lora_t(k, s):
                r = k * S + s
                dve.tensor_tensor(am2[s][:, :, :], am2[s][:, :, :], am2b[s][:, :, :], ALU.add)\
                   .then_inc(am2_ready, 1)

            def lora(k, s):
                residual(("lora2", k * S + s), s)

            def heads_in(_, s):
                for a in range(NT):
                    key = ("bqk", s, a)
                    wait_full(dve, key)
                    o = psum(key, 2 * NH, 8, 2)
                    for i, tab in enumerate((cos_t, sin_t)):
                        for j in range(2):
                            t = rtmp[s][:, i, :, :].rearrange("p h (j d) -> p h j d", j=2)
                            ins = dve.tensor_tensor(t[:, :, j, :], o[:, :, :, j],
                                                    tab[:, a, :].unsqueeze(1).broadcast_to([P, 2 * NH, 8]), ALU.mult)
                            if i * 2 + j < 3:
                                link(ins)
                    ins.then_inc(drain_of(key), 1)
                    wait_drained(dve, key)
                    c, q = rtmp[s][:, 0], rtmp[s][:, 1]
                    step(dve.tensor_tensor(rot[s][:, a, :, 0:8], c[:, :, 0:8], q[:, :, 8:16], ALU.subtract))
                    step(dve.tensor_tensor(rot[s][:, a, :, 8:16], q[:, :, 0:8], c[:, :, 8:16], ALU.add))
                    settle()
                dve.sem_inc(rot_ready, 1)

            def head_scores(_, sah):
                s, a, h = sah
                hh = slice(h * NH // 2, (h + 1) * NH // 2)
                if h == 0:
                    link(dve.tensor_tensor(prod[s][:, hh], *qk_pairs(s, a, hh), ALU.mult))
                else:
                    dve.wait_ge(prod_ready, 2 * NT * s + a + 1)
                ins = dve.tensor_reduce(sc[s][:, a, hh], prod[s][:, hh], AX.X, ALU.add)
                if h == 0:
                    link(ins)
                    return
                ins.then_inc(prod_used, 1)
                dve.wait_ge(prod_used, 2 * NT * s + a + 1)
                link(dve.tensor_reduce(bmax[s][:, a], sc[s][:, a], AX.X, ALU.max))
                dve.tensor_tensor(sc[s][:, a], sc[s][:, a], bcast(bmax[s][:, a], NH), ALU.subtract)\
                   .then_inc(b_in, 1)

            def head_mix(_, sah):
                s, a, h = sah
                hh = slice(h * NH // 2, (h + 1) * NH // 2)
                c = ctxn[s][:, a, :].rearrange("p (h d) -> p h d", h=NH)
                if h == 0:
                    dve.wait_ge(b_exp, s * NT + a + 1)
                    wait_drained(dve, ("bv", s))
                    link(dve.tensor_reduce(bsum[s][:, a], pw[s][:, a], AX.X, ALU.add))
                    link(dve.reciprocal(bmax[s][:, a], bsum[s][:, a]))
                    link(dve.tensor_tensor(prod[s][:, hh], *pv_pairs(s, a, hh), ALU.mult))
                    link(dve.tensor_reduce(c[:, hh], prod[s][:, hh], AX.X, ALU.add))
                    return
                dve.wait_ge(prod_ready, 2 * NT * s + NT + a + 1)
                dve.tensor_reduce(c[:, hh], prod[s][:, hh], AX.X, ALU.add).then_inc(prod_used, 1)
                dve.wait_ge(prod_used, 2 * NT * s + NT + a + 1)
                ins = dve.tensor_tensor(c, c, bcast(bmax[s][:, a], HD), ALU.mult)
                if a < NT - 1:
                    link(ins)
                else:
                    ins.then_inc(bctx_ready, 1)

            def head_out(_, s):
                residual(("by", s), s)

            def delta_gate(_, s):
                key = ("ba", s)
                wait_full(dve, key)
                o = psum(key, NT, 2, GH)
                sm = small[s]
                link(dve.tensor_scalar(expin[s][:, :, 0:GH], o[:, :, 0, :], -1.0, None, ALU.mult))
                dve.tensor_tensor(sm[:, 0], o[:, :, 1, :], w("c_dt").unsqueeze(1).broadcast_to([P, NT, GH]),
                                  ALU.add).then_inc(drain_of(key), 1)
                wait_drained(dve, key)
                dve.scalar_tensor_tensor(out=expin[s][:, :, GH:2 * GH], in0=sm[:, 0], scalar=-1.0, in1=sm[:, 0],
                                         op0=ALU.mult, op1=ALU.min).then_inc(gate_in, 1)

            def delta_conv(_, si):
                s, i = si
                cw = w("c_conv").rearrange("p (t j) -> p t j", t=GT)
                key = ("cv", s, i)
                wait_full(dve, key)
                o = psum(key, 2, T)
                dve.wait_ge(tap_ready, s * (GT // 2) + i + 1)
                for d in range(1, CONV):
                    for j in range(2):
                        t = 2 * i + j
                        if d > 1:
                            dve.wait_ge(dve_step, count[0] - 1)
                        ins = dve.scalar_tensor_tensor(
                            out=convT[s][:, t, d:T], in0=o[:, j, 0:T - d],
                            scalar=cw[:, t, CONV - 1 - d:CONV - d], in1=convT[s][:, t, d:T],
                            op0=ALU.mult, op1=ALU.add)
                        if d == CONV - 1 and j == 1:
                            ins.then_inc(conv_ready, 1)
                        else:
                            step(ins)
                settle()
                dve.wait_ge(conv_ready, s * (GT // 2) + i + 1)
                dve.sem_inc(drain_of(key), 1)

            def delta_log(_, s):
                sm = small[s]
                dve.wait_ge(gate_exp, s + 1)
                eb, u = expo[s][:, :, 0:GH], expo[s][:, :, GH:2 * GH]
                link(dve.tensor_scalar(sm[:, 1], eb, 1.0, None, ALU.add))
                link(dve.reciprocal(sm[:, 2], sm[:, 1]))
                link(dve.tensor_scalar(sm[:, 3], u, 2.0, None, ALU.add))
                link(dve.reciprocal(sm[:, 4], sm[:, 3]))
                link(dve.tensor_tensor(sm[:, 3], u, sm[:, 4], ALU.mult))
                link(dve.tensor_tensor(sm[:, 4], sm[:, 3], sm[:, 3], ALU.mult))
                link(dve.tensor_scalar(sm[:, 5], sm[:, 4], 1.0 / (2 * SERIES - 1), None, ALU.mult))
                for n in range(SERIES - 2, 0, -1):
                    link(dve.scalar_tensor_tensor(out=sm[:, 5], in0=sm[:, 5], scalar=1.0 / (2 * n + 1),
                                                  in1=sm[:, 4], op0=ALU.add, op1=ALU.mult))
                link(dve.scalar_tensor_tensor(out=sm[:, 6], in0=sm[:, 5], scalar=1.0, in1=sm[:, 3],
                                              op0=ALU.add, op1=ALU.mult))
                link(dve.tensor_scalar(sm[:, 7], sm[:, 0], 0.0, None, ALU.max))
                link(dve.scalar_tensor_tensor(out=sm[:, 8], in0=sm[:, 6], scalar=2.0, in1=sm[:, 7],
                                              op0=ALU.mult, op1=ALU.add))
                link(dve.scalar_tensor_tensor(out=sm[:, 7], in0=sm[:, 8], scalar=-1.0,
                                              in1=expA[:, :].unsqueeze(1).broadcast_to([P, NT, GH]),
                                              op0=ALU.mult, op1=ALU.mult))
                dve.tensor_scalar(sm[:, 9], sm[:, 7], G_MIN, None, ALU.max).then_inc(g_ready, 1)

            def delta_tok(_, s):
                sm = small[s]
                for a in range(NT):
                    for i in range(2):
                        wait_drained(dve, ("tm", s, a, i))
                sq = sqs[s]
                link(dve.tensor_tensor(sq, tokm[s][:, :, 0:GQK], tokm[s][:, :, 0:GQK], ALU.mult))
                link(dve.tensor_reduce(ss[s][:, :, :].rearrange("p a h -> p (a h)"),
                                       sq.rearrange("p a (h d) -> p (a h) d", d=DK), AX.X, ALU.add))
                dve.tensor_scalar(ss[s][:, :, :], ss[s][:, :, :], L2_EPS, None, ALU.add).then_inc(sq_ready, 1)

            def delta_qk(_, s):
                sm = small[s]
                dve.wait_ge(rn_ready, s + 1)
                link(dve.tensor_scalar(fac[s][:, :, 0:GH], fac[s][:, :, 0:GH], DK ** -0.5, None, ALU.mult))
                tq = tokm[s][:, :, 0:GQK].rearrange("p a (h d) -> p a h d", d=DK)
                for a in range(NT):
                    step(dve.tensor_tensor(tq[:, a], tq[:, a], bcast(fac[s][:, a, :], DK), ALU.mult))
                settle()
                for a in range(NT):
                    ins = dve.tensor_tensor(kb[s][:, a, :].rearrange("p (h d) -> p h d", d=DK), tq[:, a, GH:2 * GH],
                                            bcast(sm[:, 2, a, :], DK), ALU.mult)
                    if a < NT - 1:
                        link(ins)
                ins.then_inc(qk_ready, 1)
                dve.wait_ge(qk_ready, s + 1)
                wait_drained(dve, ("gd", s))
                g0, gc = gdec[s][:, 0, :], gdec[s][:, 1, :]
                hd = "p (h d) -> p h d"
                link(dve.tensor_tensor(kd[s].rearrange(hd, d=DK), tq[:, 0, GH:2 * GH], bcast(gc, DK), ALU.mult))
                link(dve.tensor_tensor(kbg[s].rearrange(hd, d=DK), kb[s][:, 1, :].rearrange(hd, d=DK),
                                       bcast(g0, DK), ALU.mult))
                dve.tensor_tensor(qg[s].rearrange(hd, d=DK), tq[:, 1, 0:GH], bcast(g0, DK), ALU.mult)\
                   .then_inc(kdec_ready, 1)

            def delta_mats(_, s):
                for q in range(GH // 2):
                    wait_drained(dve, ("L", s, q))
                dve.wait_ge(kdec_ready, s + 1)
                dve.wait_ge(bv_ready, s + 1)

                def under_decays(name, dst):
                    for b in range(4):
                        key = (name, s, b)
                        wait_full(dve, key)
                        n = 2 if b < 2 else 1
                        o = psum(key, n, NT * P)
                        sl = slice(b, b + 4 * (n - 1) + 1, 4)
                        dve.tensor_tensor(dst[:, sl].rearrange("p h a i -> p h (a i)"), o,
                                          GEs[:, sl].rearrange("p h a i -> p h (a i)"), ALU.mult)\
                           .then_inc(drain_of(key), 1)

                under_decays("A", ATs[s])
                under_decays("PT", PT[s])

            def delta_start(_, s):
                for b in range(4):
                    wait_drained(dve, ("A", s, b))
                if s:
                    for b in range(4):
                        wait_full(dve, ("U1", s - 1, b))
                flat = "p h a i -> p (h a) i"
                for q in range(GH // 2):
                    v = Wms[:, 2 * q:2 * q + 2].rearrange(flat)
                    link(dve.tensor_tensor(v, ATs[s][:, 2 * q:2 * q + 2].rearrange(flat),
                                           levb[:, 0, :].unsqueeze(1).broadcast_to([P, 2 * NT, P]), ALU.mult))
                    dve.tensor_tensor(v, ident.unsqueeze(1).broadcast_to([P, 2 * NT, P]), v, ALU.subtract)\
                       .then_inc(w_ready, 1)

            def delta_level(_, sl):
                s, l = sl
                for q in range(GH // 2):
                    key = ("Y", s, l, q)
                    wait_full(dve, key)
                    if l > 1:
                        wait_full(dve, ("dW", s, l - 1, q))
                    dve.tensor_tensor(Yms[:, 2 * q:2 * q + 2].rearrange("p h a i -> p (h a) i"),
                                      psum(key, 2 * NT, P),
                                      levb[:, l, :].unsqueeze(1).broadcast_to([P, 2 * NT, P]), ALU.mult)\
                       .then_inc(drain_of(key), 1)
                for q in range(GH // 2):
                    for name, dst in (("dT", Tms), ("dW", Wms)):
                        if name == "dT" and l == LEVELS - 1:
                            continue
                        key = (name, s, l, q)
                        wait_full(dve, key)
                        if name == "dT":
                            wait_drained(dve, ("T0", s, q) if l == 1 else ("dT", s, l - 1, q))
                            wait_full(dve, ("dW", s, l, q))
                        elif l > 1:
                            wait_drained(dve, ("dW", s, l - 1, q))
                        else:
                            dve.wait_ge(w_ready, s * GH // 2 + q + 1)
                        odd = int(name == "dW")
                        v = half_blocks(dst[:, 2 * q:2 * q + 2].rearrange("p h a i -> p (h a) i"), l, odd)
                        dve.tensor_tensor(v, v, half_blocks(psum(key, 2 * NT, P), l, odd), ALU.subtract)\
                           .then_inc(drain_of(key), 1)

            def delta_o(_, s):
                dve.wait_ge(osq_ready, 5 * (s + 1))
                link(dve.tensor_reduce(rv[s][:, :, :].rearrange("p a h -> p (a h)"),
                                       osq[s][:, :, :].rearrange("p a (h d) -> p (a h) d", d=DV), AX.X, ALU.add))
                dve.tensor_scalar(rr[s][:, :, :], rv[s][:, :, :], 1.0 / DV, RMS_EPS, ALU.mult, ALU.add)\
                   .then_inc(orms_in, 1)
                dve.wait_ge(gn_ready, s + 1)
                hd = "p (h d) -> p h d"
                key = ("O", s, 0)
                dve.tensor_tensor(on[s][:, 0, :], psum(key, GV), gate[s][:, 0, :], ALU.mult)\
                   .then_inc(drain_of(key), 1)
                for b in range(4):
                    key = ("O1", s, b)
                    n = 2 if b < 2 else 1
                    h = slice(b, b + 4 * n - 3, 4)
                    dve.tensor_tensor(on[s][:, 1, :].rearrange(hd, d=DV)[:, h, :], psum(key, n, DV),
                                      gate[s][:, 1, :].rearrange(hd, d=DV)[:, h, :], ALU.mult)\
                       .then_inc(drain_of(key), 1)

            def delta_on(_, s):
                dve.wait_ge(orms, s + 1)
                wait_drained(dve, ("O", s, 0))
                for b in range(4):
                    wait_drained(dve, ("O1", s, b))
                v = on[s][:, :, :].rearrange("p a (h d) -> p a h d", d=DV)
                dve.tensor_tensor(v, v, bcast(rv[s][:, :, :], DV), ALU.mult).then_inc(on_ready, 1)

            def delta_out(_, s):
                residual(("cy", s), s)

            def ffn_out(k, s):
                key = ("fy", k * S + s)
                residual(key, s)
                if k == 1:
                    dve.sem_inc(x_final, 1)

            table = dict(norm_x=norm_x, norm_t=nothing, latent=latent, kv=kv, kv_fold=kv_fold,
                         scores=scores, weights=weights, values=values, out_in=nothing, out_proj=out_proj, router=router, spread_t=nothing, spread=spread, x_first=x_first,
                         x_second=x_second, down=down, lora_t=lora_t, lora=lora,
                         heads_in=heads_in, head_scores=head_scores, head_mix=head_mix, head_out_t=nothing,
                         head_out=head_out, delta_gate=delta_gate, delta_conv=delta_conv, delta_log=delta_log, delta_g1=nothing, conv_silu=nothing,
                         delta_qk=delta_qk, delta_on=delta_on,
                         delta_tok=delta_tok, delta_decay=nothing, delta_rows=nothing, delta_mats=delta_mats,
                         delta_start=delta_start, delta_level=delta_level, delta_u=nothing, delta_s=nothing,
                         delta_v=nothing, delta_o=delta_o, delta_out_t=nothing, delta_out=delta_out, ffn_in=nothing, ffn_out=ffn_out, qkv_b=qkv_b)
            dve.memset(Vp[0][:, :, :, HD:PW], 1.0).then_inc(prep, 1)
            dve.memset(Vp[1][:, :, :, HD:PW], 1.0).then_inc(prep, 1)
            dve.wait_ge(loaded[0], 16)
            dve.wait_ge(masks_loaded, 16)
            dve.tensor_copy(identb[:, :], ident).then_inc(const_ready, 1)
            dve.tensor_copy(negb[:, :], raw[:, 0:P]).then_inc(const_ready, 1)
            dve.tensor_copy(levb[:, :, :], raw[:, 2 * P:].rearrange("p (l i) -> p l i", l=LEVELS)).then_inc(const_ready, 1)
            dve.tensor_copy(neg4b[:, :, :], raw[:, P:2 * P].unsqueeze(1).broadcast_to([P, 4, P])).then_inc(const_ready, 1)
            n_prep = [2]

            def plink(ins):
                n_prep[0] += 1
                ins.then_inc(prep, 1)
                dve.wait_ge(prep, n_prep[0])

            PI2 = 6.283185307179586
            C1 = 6.28125
            C2 = 0.0019340515136718750
            C3 = PI2 - C1 - C2
            MAGIC = 12582912.0
            for a in range(NT):
                plink(dve.tensor_scalar(trig[:, 2, a * 8:(a + 1) * 8], w("inv_freq"), w("tok")[:, a:a + 1], None,
                                        ALU.mult))
            for i, (quarter, shift) in enumerate(((0.0, 0.0), (0.25, PI2 / 4))):
                plink(dve.tensor_scalar(trig[:, 3, :], trig[:, 2, :], 1.0 / PI2, quarter, ALU.mult, ALU.add))
                plink(dve.tensor_scalar(trig[:, 3, :], trig[:, 3, :], MAGIC, None, ALU.add))
                plink(dve.tensor_scalar(trig[:, 3, :], trig[:, 3, :], MAGIC, None, ALU.subtract))
                plink(dve.scalar_tensor_tensor(out=trig[:, i, :], in0=trig[:, 3, :], scalar=-C1, in1=trig[:, 2, :],
                                               op0=ALU.mult, op1=ALU.add))
                plink(dve.scalar_tensor_tensor(out=trig[:, i, :], in0=trig[:, 3, :], scalar=-C2, in1=trig[:, i, :],
                                               op0=ALU.mult, op1=ALU.add))
                plink(dve.scalar_tensor_tensor(out=trig[:, i, :], in0=trig[:, 3, :], scalar=-C3, in1=trig[:, i, :],
                                               op0=ALU.mult, op1=ALU.add))
                plink(dve.tensor_scalar(trig[:, i, :], trig[:, i, :], shift, 3.1415925, ALU.add, ALU.min))
                ins = dve.tensor_scalar(trig[:, i, :], trig[:, i, :], -3.1415925, None, ALU.max)
                if i == 0:
                    plink(ins)
            ins.then_inc(trig_in, 1)
            dve.wait_ge(trig_out, 3)
            with dve.Fori(0, B // S, 1) as it:
                count[0] = 0
                program(lambda name, k, s: table[name](k, s))
                next_turn(dve, it)

        @block.gpsimd
        def _(pool):
            def step(ins):
                ins.then_inc(pool_step, 1)

            def power(dst, src, shape):
                return pool.tensor_tensor(dst, src, half[:, 0:1].broadcast_to(shape) if len(shape) == 2 else
                                          half[:, 0:1].unsqueeze(1).broadcast_to(shape), ALU.pow)

            def norm_x(k, s):
                pool.wait_ge(var_ready[s], k + 1)
                power(rstd[s][:, :], veps[s][:, :], [P, NT]).then_inc(rstd_ready[s], 1)

            HALF = slice(NH // 2, NH)

            def head_scores(_, sah):
                s, a, h = sah
                if h == 0:
                    return
                n = 2 * NT * s + a
                pool.wait_ge(rot_ready, s + 1)
                if n:
                    pool.wait_ge(prod_used, n)
                pool.tensor_tensor(prod[s][:, HALF], *qk_pairs(s, a, HALF), ALU.mult).then_inc(prod_ready, 1)

            def head_mix(_, sah):
                s, a, h = sah
                if h == 0:
                    return
                n = 2 * NT * s + NT + a
                pool.wait_ge(b_exp, s * NT + a + 1)
                wait_drained(pool, ("bv", s))
                pool.wait_ge(prod_used, n)
                pool.tensor_tensor(prod[s][:, HALF], *pv_pairs(s, a, HALF), ALU.mult).then_inc(prod_ready, 1)

            def delta_gate(_, s):
                for a in range(NT):
                    wait_drained(pool, ("gt", s, a))
                pool.tensor_tensor(gate[s][:, :, :].rearrange("p a (h d) -> p (a h) d", d=DV),
                                   gate[s][:, :, :].rearrange("p a (h d) -> p (a h) d", d=DV),
                                   w("c_norm").unsqueeze(1).broadcast_to([P, NT * GH, DV]), ALU.mult)\
                    .then_inc(gn_ready, 1)

            def delta_g1(_, s):
                pool.wait_ge(g_ready, s + 1)
                if s:
                    for b in range(4):
                        wait_drained(pool, ("A", s - 1, b))
                        wait_drained(pool, ("PT", s - 1, b))
                for a in range(NT):
                    ins = pool.tensor_tensor(GEs[:, :, a, :], w("low_strict").unsqueeze(1).broadcast_to([P, GH, P]),
                                             bcast(small[s][:, 9, a, :], P), ALU.mult)
                    if a < NT - 1:
                        step(ins)
                ins.then_inc(g1_ready, 1)

            def delta_tok(_, s):
                pool.wait_ge(sq_ready, s + 1)
                power(fac[s][:, :, :].rearrange("p a h -> p (a h)"), ss[s][:, :, :].rearrange("p a h -> p (a h)"),
                      [P, NT * 2 * GH]).then_inc(rn_ready, 1)
                for a in range(NT):
                    wait_drained(pool, ("tm", s, a, 1))
                for a in range(NT):
                    ins = pool.tensor_tensor(bv[s][:, a, :].rearrange("p (h d) -> p h d", d=DV),
                                             tokm[s][:, a, GQK:GALL].rearrange("p (h d) -> p h d", d=DV),
                                             bcast(small[s][:, 2, a, :], DV), ALU.mult)
                    if a < NT - 1:
                        step(ins)
                ins.then_inc(bv_ready, 1)

            def delta_o(_, s):
                pool.wait_ge(orms_in, s + 1)
                power(rv[s][:, :, :].rearrange("p a h -> p (a h)"), rr[s][:, :, :].rearrange("p a h -> p (a h)"),
                      [P, NT * GH]).then_inc(orms, 1)

            table = dict(norm_x=norm_x, norm_t=nothing, latent=nothing, kv=nothing, kv_fold=nothing,
                         scores=nothing, weights=nothing, values=nothing, out_in=nothing, out_proj=nothing, router=nothing, spread_t=nothing, spread=nothing, x_first=nothing,
                         x_second=nothing, down=nothing, lora_t=nothing, lora=nothing,
                         heads_in=nothing, head_scores=head_scores, head_mix=head_mix, head_out_t=nothing,
                         head_out=nothing, delta_gate=delta_gate, delta_conv=nothing, delta_log=nothing, delta_g1=delta_g1, conv_silu=nothing,
                         delta_qk=nothing, delta_on=nothing,
                         delta_tok=delta_tok, delta_decay=nothing, delta_rows=nothing, delta_mats=nothing,
                         delta_start=nothing, delta_level=nothing, delta_u=nothing, delta_s=nothing,
                         delta_v=nothing, delta_o=delta_o, delta_out_t=nothing, delta_out=nothing, ffn_in=nothing, ffn_out=nothing, qkv_b=nothing)
            pool.memset(half[:, :], -0.5).then_inc(prep_pool, 1)
            pool.wait_ge(prep_pool, 1)
            pool.wait_ge(loaded[0], 16)
            pool.wait_ge(const_ready, 4)
            with pool.Fori(0, B // S, 1) as it:
                program(lambda name, k, s: table[name](k, s))
                next_turn(pool, it)


def lay_out(inp):
    import numpy as np

    a = {k: np.asarray(v) for k, v in inp.items()}
    f = np.float32

    def kt(m):
        m = np.asarray(m)
        return m.reshape(m.shape[0] // P, P, m.shape[1]).transpose(1, 0, 2).reshape(P, -1)

    def col(v):
        return np.asarray(v).reshape(-1, P).T

    def rows(v):
        return np.broadcast_to(np.asarray(v).reshape(1, -1), (P, np.asarray(v).size))

    def units(m):
        return m.reshape(m.shape[0], NB, NU, HD).transpose(0, 2, 1, 3).reshape(m.shape[0], NH * HD)

    i, j = np.arange(P)[:, None], np.arange(P)[None, :]
    kfold = np.zeros((NB, 64, 2, NB, HD), f)
    vfold = np.zeros((NB, 64, NB, HD), f)
    for g in range(NB):
        kfold[g, :, :, g, :] = a["L0_attn_a_Wq2kv"].T[:, None, :]
        vfold[g, :, g, :] = a["L0_attn_a_Wkv2h"]
    spread = np.zeros((2 * E, 2, E, R), f)
    for e in range(E):
        spread[e, 0, e] = 1.0
        spread[E + e, 1, e] = 1.0
        spread[e, 1, e] = -1.0
    spread_rows = np.zeros((P, 2 * ER), f)
    spread_rows[0:2 * E] = spread.reshape(2 * E, 2 * ER)
    spread_rows[32, 0:D] = a["L0_attn_a_bo"]
    spread_rows[32, D:D + HD] = a["L1_attn_b_Wqkv_b"][D + HD:]
    spread_rows[64, 0:D] = a["L1_attn_b_out_b"]
    spread_rows[96, 0:D] = a["L1_ffn_proj2_bias"]
    levels = np.zeros((P, LEVELS, P), f)
    for l in range(LEVELS):
        b = 1 << l
        pair = (i // (2 * b) == j // (2 * b)) & (i // b != j // b)
        levels[:, l] = pair & ((i < j) if l == 0 else (i > j))
    qkvw, qkvb = a["L1_attn_b_Wqkv_w"], a["L1_attn_b_Wqkv_b"]
    kw = np.tile(qkvw[D:D + HD].T, (1, QG))
    kbias = np.tile(qkvb[D:D + HD], QG)
    conv = np.concatenate([a["L1_attn_a_conv_wq"], a["L1_attn_a_conv_wk"], a["L1_attn_a_conv_wv"]], 0)
    groups = [
        dict(ident=(i == j).astype(f),              own_rows=(i // HD == j[:, 0:QG]).astype(f),
             tri_up=(i <= j).astype(f), low_strict=(i > j).astype(f), ones=np.ones((P, P), f),
             c_alog=rows(a["L1_attn_a_A_log"]), iota=rows(np.arange(E, dtype=f)),
             inv_freq=rows(a["L0_attn_b_inv_freq"]), tok=np.arange(T, dtype=f).reshape(NT, P).T,
             a_wl=kt(a["L0_attn_a_Wl"]), a_bl=col(a["L0_attn_a_bl"]), a_wq=kt(units(a["L0_attn_a_Wq"])),
             a_bq=col(units(a["L0_attn_a_bq"][None])), a_wk=a["L0_attn_a_Wk"], a_bk=col(a["L0_attn_a_bk"]),
             a_wv=a["L0_attn_a_Wv"], a_bv=col(a["L0_attn_a_bv"]), a_kfold=kt(kfold.reshape(D, P)),
             a_vfold=kt(vfold.reshape(D, 64)), a_b2=np.tile(a["L0_attn_a_bkv2h"], P // HD).reshape(P, 1),
             a_wo=kt(a["L0_attn_a_Wo"])),
        dict(m_g=kt(a["L0_ffn_Wg"].T),
             m_a=kt(np.concatenate([a["L0_ffn_A1"].reshape(ER, D), a["L0_ffn_A3"].reshape(ER, D)], 0).T),
             m_spread=spread_rows, m_w1=kt(a["L0_ffn_W1"].T), m_w3=kt(a["L0_ffn_W3"].T),
             m_b1=kt(a["L0_ffn_B1"].transpose(0, 2, 1).reshape(ER, F)),
             m_b3=kt(a["L0_ffn_B3"].transpose(0, 2, 1).reshape(ER, F)),
             m_down=kt(np.concatenate([a["L0_ffn_W2"].T, a["L0_ffn_A2"].reshape(ER, F).T], 1)),
             m_b2=kt(a["L0_ffn_B2"].transpose(0, 2, 1).reshape(ER, D))),
        dict(b_wqkv=kt(np.concatenate([a["L0_attn_b_wq"], a["L0_attn_b_wk"], a["L0_attn_b_wv"]], 0).T),
             b_wo=kt(a["L0_attn_b_wo"].T)),
        dict(c_dt=rows(a["L1_attn_a_dt_bias"]), c_norm=rows(a["L1_attn_a_norm_w"]),
             c_conv=conv.reshape(GT, P, CONV).transpose(1, 0, 2).reshape(P, -1),
             c_wqkv=kt(np.concatenate([a["L1_attn_a_Wq"], a["L1_attn_a_Wk"], a["L1_attn_a_Wv"]], 0).T),
             c_wba=kt(np.concatenate([a["L1_attn_a_Wb"], a["L1_attn_a_Wa"]], 0).T),
             c_wg=kt(a["L1_attn_a_Wg"].T), c_wo=kt(a["L1_attn_a_Wo"].T)),
        dict(d_wq=kt(units(qkvw[0:D].T)), d_bq=col(units(qkvb[None, 0:D])), d_wk=kt(kw),
             d_bk=kbias.reshape(P, 1), d_wv=kt(qkvw[D + HD:].T), d_wo=kt(a["L1_attn_b_out_w"].T)),
        dict(f_w1=kt(a["L1_ffn_proj1"].T), f_b1=col(a["L1_ffn_proj1_bias"]), f_w2=kt(a["L1_ffn_proj2"].T)),
    ]
    packs, where = [], {}
    for g, parts in enumerate(groups):
        off, cols = 0, []
        for name, m in parts.items():
            m = np.asarray(m)
            full = np.zeros((P, m.shape[1]), f)
            full[:m.shape[0]] = m
            where[name] = (g, off, m.shape[1], m.shape[0])
            off += m.shape[1]
            cols.append(full)
        packs.append(np.ascontiguousarray(np.concatenate(cols, 1)))
    masks = np.concatenate([np.where(j > i, f(NEG), f(0)), np.where(j < i, f(NEG), f(0)), levels.reshape(P, -1)], 1)
    return np.ascontiguousarray(masks), packs, where


def kernel(**inputs):
    import numpy as _np
    import concourse.bacc as _bacc
    from concourse.bass_utils import run_bass_kernel_spmd as _run

    nc = _bacc.Bacc("TRN2", target_bir_lowering=False, num_devices=1)
    masks, packs, where = lay_out(inputs)
    arrays = {"x": _np.ascontiguousarray(inputs["L0_attn_a_x"]), "masks": masks}
    for g, p in enumerate(packs):
        arrays[f"pack{g}_dram"] = p
    args = {n: nc.dram_tensor(n, v.shape, mybir.dt.from_np(v.dtype), kind="ExternalInput").ap()
            for n, v in arrays.items()}
    out = nc.dram_tensor("out_dram", (B, T, D), F32, kind="ExternalOutput").ap()
    hybrid_kernel(nc, args["x"], args["masks"], [args[f"pack{g}_dram"] for g in range(len(packs))], where, out)
    r = _run(nc, [arrays], core_ids=[0])
    return r.results[0]["out_dram"]
```
